# Optimizing a Trainium2 kernel written in Bass

```python
import numpy as np
import jax
import jax.numpy as jnp

def _softmax(x, axis=-1):
    return jax.nn.softmax(x, axis=axis)

def _gelu(x):
    return jax.nn.gelu(x, approximate=True)

def _silu(x):
    return jax.nn.silu(x)

def _sigmoid(x):
    return jax.nn.sigmoid(x)

def _layernorm(x, axis=-1, eps=1e-05):
    m = jnp.mean(x, axis=axis, keepdims=True)
    v = jnp.var(x, axis=axis, keepdims=True)
    return (x - m) / jnp.sqrt(v + eps)

def _scatter_add(tgt, idx, src, axis=0):
    return tgt.at[idx].add(src)

def _segment_sum(src, seg, n):
    return jax.ops.segment_sum(src, seg, n)
kernel_name = 'mk_flamingo_gated_d2_seqx_r4_0a4cf0'

def setup_inputs(seed: int=0):
    np.random.seed(seed)
    _w = jnp.asarray

    def _rec_inputs():
        import jax
        import jax.numpy as jnp
        _rk = jax.random.key(seed)
        x = 7.22e-05 + 1 * jax.random.normal(jax.random.fold_in(_rk, 1), (2, 1024, 256), jnp.float32)
        _lenS = 1024 - jax.random.randint(jax.random.fold_in(_rk, 7), (2,), 0, max(1, 1024 // 4) + 1, jnp.int32)
        _lenS2 = 77 - jax.random.randint(jax.random.fold_in(_rk, 8), (2,), 0, max(1, 77 // 4) + 1, jnp.int32)
        _ctx_1024P = jax.random.normal(jax.random.fold_in(_rk, 11), (2, 16, 256), jnp.float32)
        _ctx_1024c = jax.random.dirichlet(jax.random.fold_in(_rk, 511), 0.3 * jnp.ones((16,), jnp.float32), (2, 77))
        _ctx_1024t = jnp.einsum('bsk,bkd->bsd', _ctx_1024c, _ctx_1024P)
        _ctx_1024t = _ctx_1024t * jax.lax.rsqrt(jnp.mean(jnp.square(_ctx_1024t)) + 1e-12) * 0.953939
        ctx_1024 = 4.13588e-05 + 0.999923 * (_ctx_1024t + 0.3 * jax.random.normal(jax.random.fold_in(_rk, 611), (2, 77, 256), jnp.float32))
        _validS = jnp.arange(1024)[None, :] < _lenS[:, None]
        _validS2 = jnp.arange(77)[None, :] < _lenS2[:, None]
        _causal = jnp.tril(jnp.ones((1024, 1024), dtype=bool))
        mask_BxS2_bf0 = jnp.logical_not(jnp.ones((2, 77), dtype=bool))
        _g = jax.random.normal(jax.random.fold_in(_rk, 9001), (2, 2), jnp.float32)
        _g = jnp.sign(_g) * jnp.maximum(jnp.abs(_g), 1.0) + (_g == 0) * 1.0
        g_xattn = _g[0]
        g_ffn = _g[1]
        return (x, ctx_1024, mask_BxS2_bf0, g_xattn, g_ffn)
    x, ctx_1024, mask_BxS2_bf0, g_xattn, g_ffn = _rec_inputs()

    def _L0_xattn_setup():
        import jax, jax.numpy as jnp
        import numpy as np
        B, LQ, LK = (4, 512, 512)
        DQ, DK, DO = (256, 256, 256)
        key = jax.random.key(seed)
        ks = jax.random.split(key, 9)
        s = 0.02
        return {'query_input': jax.random.normal(ks[0], (B, LQ, DQ), jnp.float32), 'key_input': jax.random.normal(ks[1], (B, LK, DK), jnp.float32), 'value_input': jax.random.normal(ks[2], (B, LK, DK), jnp.float32), 'Wq': jax.random.normal(ks[3], (DQ, DO), jnp.float32) * s, 'bq': jax.random.normal(ks[4], (DO,), jnp.float32) * s, 'Wk': jax.random.normal(ks[5], (DK, DO), jnp.float32) * s, 'bk': jax.random.normal(ks[6], (DO,), jnp.float32) * s, 'Wv': jax.random.normal(ks[7], (DK, DO), jnp.float32) * s, 'bv': jax.random.normal(ks[8], (DO,), jnp.float32) * s}
    _L0_xattn_all = _L0_xattn_setup()
    _L0_xattn_in = {k: v for k, v in _L0_xattn_all.items() if k in ('Wq', 'bq', 'Wk', 'bk', 'Wv', 'bv')}
    del _L0_xattn_all

    def _L0_ffn_setup():
        import jax, jax.numpy as jnp
        import numpy as np
        BLOCK = 32
        W_BITS = 4
        ACT_BITS = 16

        def act_qdq(x):
            qmax = 2.0 ** (ACT_BITS - 1) - 1.0
            scale = jnp.maximum(jnp.max(jnp.abs(x)) / qmax, 1e-12)
            return jnp.clip(jnp.round(x / scale), -qmax - 1.0, qmax) * scale

        def fixed_qdq_u16(x):
            scale = 1.0 / 65536.0
            return jnp.clip(jnp.round(x / scale), 0.0, 65535.0) * scale

        def lpbq_dequant(w):
            O, I = w.shape
            qmax = 2.0 ** (W_BITS - 1) - 1.0
            wb = w.reshape(O, I // BLOCK, BLOCK)
            s = jnp.maximum(jnp.max(jnp.abs(wb), axis=-1, keepdims=True) / qmax, 1e-12)
            wq = jnp.clip(jnp.round(wb / s), -qmax - 1.0, qmax) * s
            return wq.reshape(O, I)
        key = jax.random.key(seed)
        k1, k2, k3, k4 = jax.random.split(key, 4)
        B, S, H, I = (2, 1024, 256, 768)
        x = jax.random.normal(k1, (B, S, H), jnp.float32)
        w_gate = jax.random.normal(k2, (I, H), jnp.float32) * 0.02
        w_up = jax.random.normal(k3, (I, H), jnp.float32) * 0.02
        w_down = jax.random.normal(k4, (H, I), jnp.float32) * 0.02
        return {'x': x, 'w_gate': w_gate, 'w_up': w_up, 'w_down': w_down}
    _L0_ffn_all = _L0_ffn_setup()
    _L0_ffn_in = {k: v for k, v in _L0_ffn_all.items() if k in ('w_gate', 'w_up', 'w_down')}
    del _L0_ffn_all

    def _L1_xattn_setup():
        import jax, jax.numpy as jnp
        import numpy as np
        DIM = 256
        N_HEADS = 16
        HEAD_DIM = DIM // N_HEADS
        MAX_DIST = 128
        B, S = (2, 512)

        def _rel_bias(bias_table, q_len, k_len):
            q_pos = jnp.arange(q_len)
            k_pos = jnp.arange(k_len)
            rel = jnp.clip(k_pos[None, :] - q_pos[:, None], -MAX_DIST, MAX_DIST) + MAX_DIST
            bias = bias_table[rel]
            return jnp.transpose(bias, (2, 0, 1))
        key = jax.random.key(seed)
        ks = jax.random.split(key, 16)
        inp = {'query': jax.random.normal(ks[0], (B, S, DIM), jnp.float32), 'key': jax.random.normal(ks[1], (B, S, DIM), jnp.float32), 'value': jax.random.normal(ks[2], (B, S, DIM), jnp.float32), 'key_padding_mask': jnp.zeros((B, S), dtype=bool), 'Wq': jax.random.normal(ks[3], (DIM, DIM), jnp.float32) * DIM ** (-0.5), 'bq': jnp.zeros((DIM,), jnp.float32), 'Wk': jax.random.normal(ks[4], (DIM, DIM), jnp.float32) * DIM ** (-0.5), 'bk': jnp.zeros((DIM,), jnp.float32), 'Wv': jax.random.normal(ks[5], (DIM, DIM), jnp.float32) * DIM ** (-0.5), 'bv': jnp.zeros((DIM,), jnp.float32), 'Wo': jax.random.normal(ks[6], (DIM, DIM), jnp.float32) * DIM ** (-0.5), 'bo': jnp.zeros((DIM,), jnp.float32), 'logit_scale': jax.random.normal(ks[7], (N_HEADS,), jnp.float32) * 0.1, 'bias_table': jax.random.normal(ks[8], (2 * MAX_DIST + 1, N_HEADS), jnp.float32) * 0.02}
        return inp
    _L1_xattn_all = _L1_xattn_setup()
    _L1_xattn_in = {k: v for k, v in _L1_xattn_all.items() if k in ('Wq', 'bq', 'Wk', 'bk', 'Wv', 'bv', 'Wo', 'bo', 'logit_scale', 'bias_table')}
    del _L1_xattn_all

    def _L1_ffn_setup():
        import jax, jax.numpy as jnp
        import numpy as np
        B, T, E, C, H, G = (2, 512, 8, 256, 512, 16)
        key = jax.random.key(seed)
        ks = jax.random.split(key, 7)
        return {'hidden_states': jax.random.normal(ks[0], (B, T, C), jnp.float32), 'w_red': jax.random.normal(ks[1], (C, G), jnp.float32) * 0.02, 'wg': jax.random.normal(ks[2], (E, G), jnp.float32), 'W1': jax.random.normal(ks[3], (E, C, H), jnp.float32) * 0.02, 'b1': jax.random.normal(ks[4], (E, H), jnp.float32) * 0.02, 'W2': jax.random.normal(ks[5], (E, H, C), jnp.float32) * 0.02, 'b2': jax.random.normal(ks[6], (E, C), jnp.float32) * 0.02}
    _L1_ffn_all = _L1_ffn_setup()
    _L1_ffn_in = {k: v for k, v in _L1_ffn_all.items() if k in ('w_red', 'wg', 'W1', 'b1', 'W2', 'b2')}
    del _L1_ffn_all
    return {'x': x, 'ctx_1024': ctx_1024, 'mask_BxS2_bf0': mask_BxS2_bf0, 'g_xattn': g_xattn, 'g_ffn': g_ffn, 'L0_xattn_Wq': _L0_xattn_in['Wq'], 'L0_xattn_bq': _L0_xattn_in['bq'], 'L0_xattn_Wk': _L0_xattn_in['Wk'], 'L0_xattn_bk': _L0_xattn_in['bk'], 'L0_xattn_Wv': _L0_xattn_in['Wv'], 'L0_xattn_bv': _L0_xattn_in['bv'], 'L0_ffn_w_gate': _L0_ffn_in['w_gate'], 'L0_ffn_w_up': _L0_ffn_in['w_up'], 'L0_ffn_w_down': _L0_ffn_in['w_down'], 'L1_xattn_Wq': _L1_xattn_in['Wq'], 'L1_xattn_bq': _L1_xattn_in['bq'], 'L1_xattn_Wk': _L1_xattn_in['Wk'], 'L1_xattn_bk': _L1_xattn_in['bk'], 'L1_xattn_Wv': _L1_xattn_in['Wv'], 'L1_xattn_bv': _L1_xattn_in['bv'], 'L1_xattn_Wo': _L1_xattn_in['Wo'], 'L1_xattn_bo': _L1_xattn_in['bo'], 'L1_xattn_logit_scale': _L1_xattn_in['logit_scale'], 'L1_xattn_bias_table': _L1_xattn_in['bias_table'], 'L1_ffn_w_red': _L1_ffn_in['w_red'], 'L1_ffn_wg': _L1_ffn_in['wg'], 'L1_ffn_W1': _L1_ffn_in['W1'], 'L1_ffn_b1': _L1_ffn_in['b1'], 'L1_ffn_W2': _L1_ffn_in['W2'], 'L1_ffn_b2': _L1_ffn_in['b2']}

def reference(x, ctx_1024, mask_BxS2_bf0, g_xattn, g_ffn, L0_xattn_Wq, L0_xattn_bq, L0_xattn_Wk, L0_xattn_bk, L0_xattn_Wv, L0_xattn_bv, L0_ffn_w_gate, L0_ffn_w_up, L0_ffn_w_down, L1_xattn_Wq, L1_xattn_bq, L1_xattn_Wk, L1_xattn_bk, L1_xattn_Wv, L1_xattn_bv, L1_xattn_Wo, L1_xattn_bo, L1_xattn_logit_scale, L1_xattn_bias_table, L1_ffn_w_red, L1_ffn_wg, L1_ffn_W1, L1_ffn_b1, L1_ffn_W2, L1_ffn_b2):
    import jax
    import jax.numpy as jnp

    def _L0_xattn_ref(query_input, key_input, value_input, Wq, bq, Wk, bk, Wv, bv):
        import jax, jax.numpy as jnp
        import numpy as np
        B, LQ, LK = (4, 512, 512)
        DQ, DK, DO = (256, 256, 256)
        scale = jnp.asarray(DO, query_input.dtype) ** 0.5
        q = query_input @ Wq + bq
        k = key_input @ Wk + bk
        v = value_input @ Wv + bv
        attn = jnp.einsum('bqd,bkd->bqk', q, k) / scale
        attn = jax.nn.softmax(attn, axis=-1)
        return jnp.einsum('bqk,bkd->bqd', attn, v)

    def _L0_ffn_ref(x, w_gate, w_up, w_down):
        import jax, jax.numpy as jnp
        import numpy as np
        BLOCK = 32
        W_BITS = 4
        ACT_BITS = 16

        def act_qdq(x):
            qmax = 2.0 ** (ACT_BITS - 1) - 1.0
            scale = jnp.maximum(jnp.max(jnp.abs(x)) / qmax, 1e-12)
            return jnp.clip(jnp.round(x / scale), -qmax - 1.0, qmax) * scale

        def fixed_qdq_u16(x):
            scale = 1.0 / 65536.0
            return jnp.clip(jnp.round(x / scale), 0.0, 65535.0) * scale

        def lpbq_dequant(w):
            O, I = w.shape
            qmax = 2.0 ** (W_BITS - 1) - 1.0
            wb = w.reshape(O, I // BLOCK, BLOCK)
            s = jnp.maximum(jnp.max(jnp.abs(wb), axis=-1, keepdims=True) / qmax, 1e-12)
            wq = jnp.clip(jnp.round(wb / s), -qmax - 1.0, qmax) * s
            return wq.reshape(O, I)
        x = act_qdq(x)
        up = act_qdq(x @ lpbq_dequant(w_up).T)
        gate = act_qdq(x @ lpbq_dequant(w_gate).T)
        sig = fixed_qdq_u16(jax.nn.sigmoid(gate))
        gate = act_qdq(gate * sig)
        o = act_qdq(gate * up)
        return o @ lpbq_dequant(w_down).T

    def _L1_xattn_ref(query, key, value, key_padding_mask, Wq, bq, Wk, bk, Wv, bv, Wo, bo, logit_scale, bias_table):
        import jax, jax.numpy as jnp
        import numpy as np
        DIM = 256
        N_HEADS = 16
        HEAD_DIM = DIM // N_HEADS
        MAX_DIST = 128
        B, S = (2, 512)

        def _rel_bias(bias_table, q_len, k_len):
            q_pos = jnp.arange(q_len)
            k_pos = jnp.arange(k_len)
            rel = jnp.clip(k_pos[None, :] - q_pos[:, None], -MAX_DIST, MAX_DIST) + MAX_DIST
            bias = bias_table[rel]
            return jnp.transpose(bias, (2, 0, 1))
        b, tq, _ = query.shape
        tk = key.shape[1]

        def proj(x, W, bias):
            y = x @ W + bias
            return y.reshape(b, -1, N_HEADS, HEAD_DIM).transpose(0, 2, 1, 3)
        q = proj(query, Wq, bq)
        k = proj(key, Wk, bk)
        v = proj(value, Wv, bv)
        base_scale = HEAD_DIM ** (-0.5)
        scale = base_scale * jnp.minimum(jnp.exp(logit_scale), 4.0)
        scores = jnp.einsum('bhqd,bhkd->bhqk', q, k) * scale[None, :, None, None]
        scores = scores + _rel_bias(bias_table, tq, tk)[None]
        neg = -jnp.finfo(scores.dtype).max
        scores = jnp.where(key_padding_mask[:, None, None, :], neg, scores)
        attn = jax.nn.softmax(scores, axis=-1)
        out = jnp.einsum('bhqk,bhkd->bhqd', attn, v)
        out = out.transpose(0, 2, 1, 3).reshape(b, tq, DIM)
        out = out @ Wo + bo
        return out

    def _L1_ffn_ref(hidden_states, w_red, wg, W1, b1, W2, b2):
        import jax, jax.numpy as jnp
        import numpy as np
        B, T, E, C, H, G = (2, 512, 8, 256, 512, 16)
        b, t, c = hidden_states.shape
        x = hidden_states.reshape(-1, c)
        x_red = x @ w_red
        wg_n = wg / jnp.maximum(jnp.linalg.norm(wg, axis=1, keepdims=True), 0.0001)
        logits = x_red @ wg_n.T
        gates = jax.nn.softmax(logits, axis=1)
        scores = jnp.max(gates, axis=1)
        idx = jnp.argmax(gates, axis=1)
        h = jnp.einsum('nc,ech->neh', x, W1) + b1[None]
        h = jnp.take_along_axis(h, idx[:, None, None], axis=1)[:, 0, :]
        h = jax.nn.gelu(h, approximate=False)
        o = jnp.einsum('nh,ehc->nec', h, W2) + b2[None]
        o = jnp.take_along_axis(o, idx[:, None, None], axis=1)[:, 0, :]
        o = o * scores[:, None]
        return o.reshape(b, t, c)
    x = x + jnp.tanh(g_xattn[0]) * _L0_xattn_ref(_layernorm(x, axis=-1), ctx_1024, ctx_1024, L0_xattn_Wq, L0_xattn_bq, L0_xattn_Wk, L0_xattn_bk, L0_xattn_Wv, L0_xattn_bv)
    x = x + jnp.tanh(g_ffn[0]) * _L0_ffn_ref(_layernorm(x, axis=-1), L0_ffn_w_gate, L0_ffn_w_up, L0_ffn_w_down)
    x = x + jnp.tanh(g_xattn[1]) * _L1_xattn_ref(_layernorm(x, axis=-1), ctx_1024, ctx_1024, mask_BxS2_bf0, L1_xattn_Wq, L1_xattn_bq, L1_xattn_Wk, L1_xattn_bk, L1_xattn_Wv, L1_xattn_bv, L1_xattn_Wo, L1_xattn_bo, L1_xattn_logit_scale, L1_xattn_bias_table)
    x = x + jnp.tanh(g_ffn[1]) * _L1_ffn_ref(_layernorm(x, axis=-1), L1_ffn_w_red, L1_ffn_wg, L1_ffn_W1, L1_ffn_b1, L1_ffn_W2, L1_ffn_b2)
    return x

_drawn_inputs = setup_inputs


def setup_inputs(seed=0):
    import zlib

    import numpy as np

    out = dict(_drawn_inputs(seed))
    spreads = {'g_ffn': (-1.0, 0.6),
     'L1_xattn_bq': (0.0, 0.417),
     'L1_xattn_bk': (0.0, 0.8),
     'L1_xattn_bv': (0.0, 0.1),
     'L1_xattn_bo': (0.0, 0.1)}
    factors = {'L0_xattn_Wq': 8.0,
     'L0_xattn_bq': 8.0,
     'L0_xattn_Wk': 8.0,
     'L0_xattn_bk': 8.0,
     'L0_xattn_bv': 4.284,
     'L1_xattn_logit_scale': 2.679,
     'L1_xattn_bias_table': 8.0,
     'L1_ffn_w_red': 5.467,
     'L1_ffn_wg': 5.416,
     'L1_ffn_W1': 5.419,
     'L1_ffn_b1': 8.0,
     'L1_ffn_W2': 5.234,
     'L1_ffn_b2': 8.0}
    for name, (base, spread) in spreads.items():
        noise = np.random.default_rng([zlib.crc32(name.encode()), seed]).standard_normal(out[name].shape)
        drawn = base * np.exp(spread * noise) if base else spread * noise
        out[name] = jnp.asarray(drawn.astype(out[name].dtype))
    for name, factor in factors.items():
        out[name] = (out[name] * factor).astype(out[name].dtype)
    return out
```

```python
import numpy as np

import concourse.bass as bass
from concourse import mybir
from contextlib import ExitStack

F32 = mybir.dt.float32
BF16 = mybir.dt.bfloat16
I16 = mybir.dt.int16
U16 = mybir.dt.uint16
I32 = mybir.dt.int32
U8 = mybir.dt.uint8
ALU = mybir.AluOpType
ACT = mybir.ActivationFunctionType
AX = mybir.AxisListType
ds = bass.ds

P = 128
NB, S, D = 2, 1024, 256
NT = NB * S // P
TB = S // P
KEYS = 77
CH = D // P
H, HD = 16, 16
HK = H * KEYS
HQ = 4
HQK = HQ * KEYS
NQ = H // HQ
VE = HD + 1
F = 768
FJ = F // P
BLK = 32
QB = 512
NQB = NB * S // QB
E, HID, G = 8, 512, 16
HJ = HID // P
NS = NT + E - 1
MAXD = 128
NEAR = 2
EXT = NEAR * P + KEYS - 1
ROW = D + 4
NMR, RSTD, COEF, IDC = D, D + 1, D + 2, D + 3
EPS = 1e-5
MAGIC = 1.5 * 2.0 ** 23
QMAX = 32767.0
TINY = 1e-12
NEG = -(2.0 ** 126)
NOWHERE = 1 << 20


class Signals:

    def __init__(self, sem):
        self.ld_l0 = sem("ld_l0")
        self.ld_x = sem("ld_x")
        self.ld_ffn = sem("ld_ffn")
        self.ld_l1 = sem("ld_l1")
        self.ld_ext = sem("ld_ext")
        self.ld_near = sem("ld_near")
        self.ld_const = sem("ld_const")
        self.ld_w1 = sem("ld_w1")
        self.ld_w2 = sem("ld_w2")
        self.ld_b1 = sem("ld_b1")
        self.ld_b2 = sem("ld_b2")
        self.pads_written = sem("pads_written")
        self.ext_stored = sem("ext_stored")
        self.consts = sem("consts")
        self.pool_consts = sem("pool_consts")
        self.ctxT_ps = sem("ctxT_ps")
        self.ctxT_sb = sem("ctxT_sb")
        self.wq0T_ps = sem("wq0T_ps")
        self.wq0T_sb = sem("wq0T_sb")
        self.k0_ps = sem("k0_ps")
        self.k0_sb = sem("k0_sb")
        self.a0_ps = sem("a0_ps")
        self.a0_sb = sem("a0_sb")
        self.v0_ps = sem("v0_ps")
        self.v0_sb = sem("v0_sb")
        self.els_sb = sem("els_sb")
        self.hsc_sb = sem("hsc_sb")
        self.csc_ps = sem("csc_ps")
        self.k1_ps = sem("k1_ps")
        self.csc_sb = sem("csc_sb")
        self.k1_sb = sem("k1_sb")
        self.v1_ps = sem("v1_ps")
        self.v1_sb = sem("v1_sb")
        self.kbd_sb = sem("kbd_sb")
        self.ext_sb = sem("ext_sb")
        self.wrT_ps = sem("wrT_ps")
        self.wrT_sb = sem("wrT_sb")
        self.wss_sb = sem("wss_sb")
        self.wnorm_sb = sem("wnorm_sb")
        self.wgn_sb = sem("wgn_sb")
        self.wgT_ps = sem("wgT_ps")
        self.wgT_sb = sem("wgT_sb")
        self.gm_ps = sem("gm_ps")
        self.gm_sb = sem("gm_sb")
        self.tg_sb = sem("tg_sb")
        self.wo_sb = sem("wo_sb")
        self.wq_sb = sem("wq_sb")
        self.wT_ps = sem("wT_ps")
        self.wT_sb = sem("wT_sb")
        self.mv_a = sem("mv_a")
        self.rstd_a = sem("rstd_a")
        self.keep_sb = sem("keep_sb")
        self.slots_sb = sem("slots_sb")
        self.am_u = sem("am_u")
        self.ar_u = sem("ar_u")
        self.wn_sb = sem("wn_sb")
        self.scal_u = sem("scal_u")
        self.y_a = sem("y_a")
        self.yT_ps = sem("yT_ps")
        self.yT_sb = sem("yT_sb")
        self.s0_ps = sem("s0_ps")
        self.nmax_a = sem("nmax_a")
        self.p0 = sem("p0")
        self.pT0_ps = sem("pT0_ps")
        self.pT0_sb = sem("pT0_sb")
        self.o0_ps = sem("o0_ps")
        self.mv_b = sem("mv_b")
        self.rstd_b = sem("rstd_b")
        self.y_b = sem("y_b")
        self.y2T_ps = sem("y2T_ps")
        self.y2T_sb = sem("y2T_sb")
        self.ax_sb = sem("ax_sb")
        self.ar_x = sem("ar_x")
        self.scal_x = sem("scal_x")
        self.tq_y = sem("tq_y")
        self.nq = sem("nq")
        self.gu_ps = sem("gu_ps")
        self.gu_sb = sem("gu_sb")
        self.am_g = sem("am_g")
        self.ar_g = sem("ar_g")
        self.scal_g = sem("scal_g")
        self.sig_done = sem("sig_done")
        self.z_done = sem("z_done")
        self.am_z = sem("am_z")
        self.ar_z = sem("ar_z")
        self.scal_z = sem("scal_z")
        self.nzu_done = sem("nzu_done")
        self.p_done = sem("p_done")
        self.am_p = sem("am_p")
        self.ar_p = sem("ar_p")
        self.scal_p = sem("scal_p")
        self.tq_p = sem("tq_p")
        self.no_done = sem("no_done")
        self.dn_ps = sem("dn_ps")
        self.x2_done = sem("x2_done")
        self.mv_c = sem("mv_c")
        self.rstd_c = sem("rstd_c")
        self.y_c = sem("y_c")
        self.y3T_ps = sem("y3T_ps")
        self.y3T_sb = sem("y3T_sb")
        self.near_sb = sem("near_sb")
        self.const_sb = sem("const_sb")
        self.q_ps = sem("q_ps")
        self.q_sb = sem("q_sb")
        self.s_ps = sem("s_ps")
        self.e_sub = sem("e_sub")
        self.e_exp = sem("e_exp")
        self.pT_ps = sem("pT_ps")
        self.pT_sb = sem("pT_sb")
        self.o_ps = sem("o_ps")
        self.att_sb = sem("att_sb")
        self.attT_ps = sem("attT_ps")
        self.attT_sb = sem("attT_sb")
        self.wo_ps = sem("wo_ps")
        self.x3_done = sem("x3_done")
        self.mv_d = sem("mv_d")
        self.rstd_d = sem("rstd_d")
        self.y_d = sem("y_d")
        self.y4T_ps = sem("y4T_ps")
        self.y4T_sb = sem("y4T_sb")
        self.lg_ps = sem("lg_ps")
        self.lg_sb = sem("lg_sb")
        self.lx_sb = sem("lx_sb")
        self.ex_sb = sem("ex_sb")
        self.oh_sb = sem("oh_sb")
        self.cnt_ps = sem("cnt_ps")
        self.pos_sb = sem("pos_sb")
        self.scattered = sem("scattered")
        self.rows_in0 = sem("rows_in0")
        self.rows_in1 = sem("rows_in1")
        self.ys_sb = sem("ys_sb")
        self.ysT_ps = sem("ysT_ps")
        self.ysT_sb = sem("ysT_sb")
        self.h_ps = sem("h_ps")
        self.hb_sb = sem("hb_sb")
        self.gelu_sb = sem("gelu_sb")
        self.hT_ps = sem("hT_ps")
        self.hT_sb = sem("hT_sb")
        self.eo_ps = sem("eo_ps")
        self.res_sb = sem("res_sb")
        self.rows_out0 = sem("rows_out0")
        self.rows_out1 = sem("rows_out1")
        self.dve_step = sem("dve_step")
        self.act_step = sem("act_step")
        self.pool_step = sem("pool_step")
        self.dve_past = sem("dve_past")
        self.pool_past = sem("pool_past")


class Chain:

    def __init__(self, eng, sem):
        self.eng, self.sem, self.base, self.n = eng, sem, 0, 0

    def mark(self, ins):
        self.n += 1
        ins.then_inc(self.sem, 1)
        return self.base + self.n

    def link(self, ins):
        self.eng.wait_ge(self.sem, self.mark(ins))

    def enter(self, i, per):
        self.done, self.per = self.base + self.n, per
        self.base, self.n = self.done + i * per, 0

    def leave(self, times):
        assert self.n == self.per, (self.n, self.per)
        self.base, self.n = self.done + times * self.per, 0


def flamingo_kernel(nc, a, out):
    ctx = ExitStack()
    with ctx:
        def sb(name, shape, dt=F32):
            return ctx.enter_context(nc.sbuf_tensor(name, shape, dt))

        def sem(name):
            return ctx.enter_context(nc.semaphore(name))

        bank = [ctx.enter_context(nc.psum_tensor(f"bank{i}", [P, 512], F32)) for i in range(8)]
        pb = [b[:, :] for b in bank]

        rows_d = nc.dram_tensor("sorted_rows", [NS * P, ROW], F32).ap()
        ext_d = nc.dram_tensor("bias_by_distance", [H, EXT], F32).ap()

        X = sb("x_rows", [P, NT, ROW])
        XI = X[:, :, :].bitcast(I32)
        YT = sb("yT", [P, CH, NB * S])
        BIGG = sb("big_g", [P, FJ * NB * S])
        BIGU = sb("big_u", [P, FJ * NB * S])
        TMP = sb("tmp", [P, 6144])
        FW = sb("ffn_w", [P, 4608])
        GT = BIGG[:, :].rearrange("p (j n) -> p j n", j=FJ)
        UT_ = BIGU[:, :].rearrange("p (j n) -> p j n", j=FJ)

        def part(reg, off, shape, dt=F32):
            n = int(np.prod(shape[1:]))
            words = n if dt in (F32, I32) else n // 2
            v = reg[0:shape[0], off:off + words]
            if dt != F32:
                v = v.bitcast(dt)
            if len(shape) == 3:
                v = v.rearrange("p (a b) -> p a b", a=shape[1])
            if len(shape) == 4:
                v = v.rearrange("p (a b c) -> p a b c", a=shape[1], b=shape[2])
            return v

        ident = sb("ident", [P, P])
        flipb = sb("flipb", [P, P], BF16)
        ones = sb("ones", [P, P])
        onesb = sb("onesb", [P, P], BF16)
        before = sb("before", [P, P], BF16)
        headof = sb("headof", [P, 8])
        expand = part(BIGU, 10880, [H, D])
        mhalf = sb("mhalf", [P, 4])
        half = sb("half", [E, 1])
        ids = sb("ids", [P, NT], I32)
        slot_i = part(BIGG, 4608, [P, NS, E - 1], I32)
        slot = sb("slot", [P, NS, E - 1])
        rank_i = part(BIGG, 4800, [P, E], I32)
        rank = sb("rank", [P, E])
        gates = sb("gates", [P, 4])
        tg = sb("tg", [P, 4])

        CTX = part(BIGU, 8192, [KEYS, NB, D])
        WK0 = part(BIGU, 0, [P, CH, D])
        WQ0 = part(BIGU, 512, [P, CH, D])
        WV0 = part(BIGU, 1024, [P, CH, D])
        bq0 = sb("bq0", [P, CH])
        bk0 = sb("bk0", [P, CH])
        bv0 = part(BIGU, 8704, [1, D])
        CTXT = part(BIGU, 8960, [P, CH, NB * KEYS])
        WQ0T = part(BIGU, 1536, [P, CH, D])
        K0T = part(BIGU, 2048, [P, CH, NB * KEYS])
        A0 = sb("a0", [P, CH, NB * KEYS])
        R0 = sb("r0", [1, NB * KEYS])
        V0 = sb("v0", [KEYS, NB, D])
        ya = part(BIGU, 3072, [P, 4, D])
        y2a = part(BIGU, 4096, [P, 4, D])
        yTa = part(BIGU, 5120, [P, 4, D])
        pa = part(BIGU, 6144, [P, 4, KEYS])
        pTa = part(BIGU, 6528, [KEYS, 4, P])
        stat = sb("stat", [P, 4, 6])
        mv = sb("mv", [P, 4, 2])
        ve = sb("ve", [P, 4])
        rstd = sb("rstd", [P, 4])
        nmax = sb("nmax", [P, 4])
        den = sb("den", [P, 4])
        rden = sb("rden", [P, 4])

        WN = part(BIGG, 0, [P, 18 * 8, BLK])
        WUT = part(FW, 0, [P, CH, F])
        WGT = part(FW, CH * F, [P, CH, F])
        WDT = part(FW, 2 * CH * F, [P, FJ, D])
        wamax = sb("wamax", [P, 144])
        wscale = sb("wscale", [P, 144])
        wrec = sb("wrec", [P, 144])
        amY = sb("amY", [P, NT])
        amG = sb("amG", [P, NQB * FJ])
        amU = sb("amU", [P, NQB * FJ])
        amZ = sb("amZ", [P, 2 * NQB])
        amP = sb("amP", [P, 2 * NQB])
        sc = sb("scalars", [P, 32])
        HF = 3 * QB
        ng = part(TMP, 0, [P, 2, HF], I16)
        u16 = part(TMP, HF, [P, 2, HF], U16)
        sig = part(TMP, 2 * HF, [P, 2, HF])
        nz = part(TMP, 0, [P, 2, HF], I16)
        nu = part(TMP, HF, [P, 2, HF], I16)
        y3 = part(TMP, 0, [P, 4, D])

        WK1 = part(BIGU, 9280, [P, CH, D])
        WV1 = part(BIGU, 9792, [P, CH, D])
        WQ1 = sb("wq1", [P, CH, D])
        WO1 = sb("wo1", [P, CH, D])
        bq1 = sb("bq1", [P, CH])
        bk1 = sb("bk1", [P, CH])
        bv1 = part(BIGU, 10304, [1, D])
        bo1 = sb("bo1", [1, D])
        ls = sb("ls", [H, 1])
        els = sb("els", [H, 1])
        hscale = sb("hscale", [H, 1])
        cscale = sb("cscale", [P, CH])
        keep8 = sb("keep8", [P, NB * KEYS], U8)
        keep = part(BIGU, 10560, [P, NB * KEYS])
        K1T = sb("k1T", [P, CH, NB * KEYS])
        KBD = sb("k_blockdiag", [P, NB * CH * 8, KEYS])
        V1 = sb("v1", [KEYS, NB * H, VE])
        mrow8 = sb("mrow8", [1, NB * KEYS], U8)
        mrow = part(BIGU, 10720, [1, NB * KEYS])
        CM = sb("const_rows", [4, NB, HK], BF16)
        tab0 = sb("tab0", [1, H])
        tabT = part(BIGU, 7168, [H, 2 * MAXD + 1])
        ext = part(BIGU, 7680, [H, EXT])
        far3 = part(BIGG, 5376, [1, 3, HK], BF16)
        mask16 = part(BIGG, 7232, [1, NB, HK], BF16)
        BN = part(TMP, 1024, [P, NEAR * 3, HK], BF16)
        bstage = part(TMP, 4736, [P, HK])

        e_ = part(BIGG, 8192, [P, 2, HK])
        qT = part(BIGG, 10752, [P, 2, D])
        att = part(BIGG, 11264, [P, 2, D])
        attT = part(BIGG, 11776, [P, 2, D])
        pT = part(BIGU, 8192, [KEYS, 2, H * P])
        rd = sb("rd", [P, 2, H])
        mx = sb("mx", [P, 2, HQ])

        WR = part(BIGU, 11136, [P, CH, G])
        WRT = part(BIGU, 11168, [G, D])
        wg = sb("wg", [E, G])
        wg2 = sb("wg2", [E, G])
        wgn = sb("wgn", [E, G])
        wss = sb("wss", [E, 3])
        WGNT = sb("wgnT", [G, E])
        GM = sb("gm", [P, CH, E])
        W1 = part(BIGG, 0, [P, E * CH, HID])
        W2 = part(BIGU, 0, [P, E * HJ, D])
        B1 = part(FW, 0, [P, E * HID])
        B2 = part(TMP, 0, [P, E * D])
        y4 = part(BIGG, 8192, [P, 4, D])
        y4T = part(BIGG, 9216, [P, 4, D])
        LG = part(BIGU, 8192, [P, NT, E])
        LX = part(BIGU, 8320, [P, NT, E])
        LM = sb("lm", [P, NT])
        OH = part(BIGU, 8448, [P, NT, E])
        OHB = sb("onehotb", [P, NT, E], BF16)
        TOT = part(BIGU, 8576, [P, NT, E])
        CUM = part(BIGU, 8704, [P, NT + 1, E])
        cnt_i = sb("cnt_i", [P, E], I32)
        tiles_e = sb("tiles_e", [P, E])
        start_e = sb("start_e", [P, E])
        start128 = sb("start128", [P, E])
        pos_i = sb("pos_i", [P, NT], I32)
        rid = sb("row_ids", [P, 2], I32)
        eslot = sb("eslot", [P, NS])
        ob = part(BIGG, 8704, [P, 2, D])
        EXPS = sb("exp_of_slot", [P, NS], I32)
        YW = YT[:, :, :].rearrange("p a b -> p (a b)")
        rb = part(YW, 0, [P, 2, ROW])
        ys = part(YW, 520, [P, 2, D])
        ysT = part(YW, 1032, [P, 2, D])
        hb = part(YW, 1544, [P, 2, HID])
        hT = part(YW, 2568, [P, 2, HID])
        res = part(BIGG, 8192, [P, 2, D])
        pad = part(BIGG, 4864, [P, ROW])

        s = Signals(sem)
        block = ctx.enter_context(nc.Block())

        @block.sync
        def _(sp):
            def chunks(w):
                return w.rearrange("(c p) n -> p c n", p=P)

            def column(v):
                return v.rearrange("(c p) -> p c", p=P)

            def row(v):
                return v.rearrange("(a n) -> a n", a=1)

            sp.dma_start(CTX, a["ctx_1024"].rearrange("b k d -> k b d")).then_inc(s.ld_l0, 16)
            sp.dma_start(WK0, chunks(a["L0_xattn_Wk"])).then_inc(s.ld_l0, 16)
            sp.dma_start(WQ0, chunks(a["L0_xattn_Wq"])).then_inc(s.ld_l0, 16)
            sp.dma_start(WV0, chunks(a["L0_xattn_Wv"])).then_inc(s.ld_l0, 16)
            sp.dma_start(bk0[:, :], column(a["L0_xattn_bk"]), allow_slow_non_contiguous=True).then_inc(s.ld_l0, 16)
            sp.dma_start(bq0[:, :], column(a["L0_xattn_bq"]), allow_slow_non_contiguous=True).then_inc(s.ld_l0, 16)
            sp.dma_start(bv0, row(a["L0_xattn_bv"])).then_inc(s.ld_l0, 16)
            for n, g in enumerate(("g_xattn", "g_ffn")):
                sp.dma_start(gates[:, 2 * n:2 * n + 2], row(a[g]).to_broadcast([P, 2])).then_inc(s.ld_l0, 16)
            for b in range(NB):
                sp.dma_start(X[:, b * TB:(b + 1) * TB, 0:D],
                             a["x"][b].rearrange("(t p) d -> p t d", p=P)).then_inc(s.ld_x, 16)
            for n, w in enumerate(("L0_ffn_w_gate", "L0_ffn_w_up")):
                sp.dma_start(WN[:, n * 48:(n + 1) * 48, :].rearrange("p (j q) k -> p j (q k)", j=FJ),
                             a[w].rearrange("(j p) c -> p j c", p=P)).then_inc(s.ld_ffn, 16)
            sp.dma_start(WN[:, 96:144, :].rearrange("p (j q) k -> p j (q k)", j=CH),
                         a["L0_ffn_w_down"].rearrange("(j p) c -> p j c", p=P)).then_inc(s.ld_ffn, 16)
            sp.dma_start(WK1, chunks(a["L1_xattn_Wk"])).then_inc(s.ld_l1, 16)
            sp.dma_start(WV1, chunks(a["L1_xattn_Wv"])).then_inc(s.ld_l1, 16)
            sp.dma_start(WQ1[:, :, :], chunks(a["L1_xattn_Wq"])).then_inc(s.ld_l1, 16)
            sp.dma_start(WO1[:, :, :], chunks(a["L1_xattn_Wo"])).then_inc(s.ld_l1, 16)
            sp.dma_start(bq1[:, :], column(a["L1_xattn_bq"]), allow_slow_non_contiguous=True).then_inc(s.ld_l1, 16)
            sp.dma_start(bk1[:, :], column(a["L1_xattn_bk"]), allow_slow_non_contiguous=True).then_inc(s.ld_l1, 16)
            sp.dma_start(bv1, row(a["L1_xattn_bv"])).then_inc(s.ld_l1, 16)
            sp.dma_start(bo1[:, :], row(a["L1_xattn_bo"])).then_inc(s.ld_l1, 16)
            sp.dma_start(ls[:, :], a["L1_xattn_logit_scale"].rearrange("(h a) -> h a", a=1)).then_inc(s.ld_l1, 16)
            mask = a["mask_BxS2_bf0"].rearrange("b k -> (b k)").rearrange("(a n) -> a n", a=1)
            sp.dma_start(keep8[:, :], mask.to_broadcast([P, NB * KEYS])).then_inc(s.ld_l1, 16)
            sp.dma_start(mrow8[:, :], mask).then_inc(s.ld_l1, 16)
            sp.dma_start(WR, chunks(a["L1_ffn_w_red"])).then_inc(s.ld_l1, 16)
            sp.dma_start(wg[:, :], a["L1_ffn_wg"]).then_inc(s.ld_l1, 16)
            sp.dma_start(tab0[:, :], a["L1_xattn_bias_table"][0:1, :]).then_inc(s.ld_l1, 16)
            sp.dma_start(tabT, a["L1_xattn_bias_table"].rearrange("r h -> h r"), allow_slow_non_contiguous=True).then_inc(s.ld_ext, 16)
            sp.wait_ge(s.pool_consts, 1)
            sp.dma_start(rows_d.rearrange("(t p) c -> p t c", p=P),
                         pad.unsqueeze(1).to_broadcast([P, NS, ROW])).then_inc(s.pads_written, 16)
            sp.wait_ge(s.ext_sb, 1)
            sp.dma_start(ext_d, ext).then_inc(s.ext_stored, 16)
            sp.wait_ge(s.const_sb, 1)
            sp.dma_start(CM[0:1, :, :], mask16).then_inc(s.ld_const, 16)
            for b in range(NB):
                for k in range(3):
                    sp.dma_start(CM[k + 1:k + 2, b, :], far3[:, k, :]).then_inc(s.ld_const, 16)
            sp.wait_ge(s.ext_stored, 16)
            sp.wait_ge(s.p_done, 2 + 2 * NQB)
            for n in range(NEAR):
                if n:
                    sp.wait_ge(s.near_sb, n)
                sp.dma_start(bstage.rearrange("p (h k) -> p h k", h=H),
                             bass.AP(tensor=ext_d.tensor, offset=EXT - KEYS - n * P - (P - 1),
                                     ap=[[1, P], [EXT, H], [1, KEYS]])).then_inc(s.ld_near, 16)
            sp.wait_ge(s.dn_ps, NT)
            sp.dma_start(W1.rearrange("p (e c) h -> p e c h", e=E),
                         a["L1_ffn_W1"].rearrange("e (c p) h -> p e c h", p=P)).then_inc(s.ld_w1, 16)
            sp.dma_start(W2.rearrange("p (e c) h -> p e c h", e=E),
                         a["L1_ffn_W2"].rearrange("e (c p) h -> p e c h", p=P)).then_inc(s.ld_w2, 16)
            sp.dma_start(B1, row(a["L1_ffn_b1"].rearrange("e h -> (e h)")).to_broadcast([P, E * HID])).then_inc(s.ld_b1, 16)
            sp.wait_ge(s.x3_done, NT)
            sp.dma_start(B2, row(a["L1_ffn_b2"].rearrange("e h -> (e h)")).to_broadcast([P, E * D])).then_inc(s.ld_b2, 16)
            sp.wait_ge(s.scattered, 16 * NT)

            def rows_in(u, t, after):
                if after is not None:
                    sp.wait_ge(s.res_sb, after)
                sp.dma_start(rb[:, u, :], rows_d[ds(t * P, P), :]).then_inc(s.rows_in0 if u == 0 else s.rows_in1, 16)
            rows_in(0, 0, None)
            rows_in(1, 1, None)
            with sp.Fori(1, NS // 2) as i:
                rows_in(0, 2 * i, 2 * i - 1)
                rows_in(1, 2 * i + 1, 2 * i)
            rows_in(0, NS - 1, NS - 2)

        @block.gpsimd
        def _(pool):
            c = Chain(pool, s.pool_step)
            c.link(pool.memset(ident[:, :], 0.0))
            c.link(pool.memset(ones[:, :], 1.0))
            c.link(pool.affine_select(out=ident[:, :], in_=ident[:, :], compare_op=ALU.not_equal, fill=1.0,
                                      base=0, pattern=[[-1, P]], channel_multiplier=1))
            pool.tensor_copy(onesb[:, :], ones[:, :])
            c.link(pool.memset(flipb[:, :], 0.0))
            c.link(pool.affine_select(out=flipb[:, :], in_=flipb[:, :], compare_op=ALU.not_equal, fill=1.0,
                                      base=-(P - 1), pattern=[[1, P]], channel_multiplier=1))
            pool.memset(half[:, :], 0.5)
            pool.memset(mhalf[:, :], -0.5).then_inc(s.consts, 1)
            c.link(pool.affine_select(out=headof[:, :], in_=ones[:, 0:8], compare_op=ALU.is_ge, fill=0.0,
                                      base=0, pattern=[[-HD, 8]], channel_multiplier=1))
            c.link(pool.affine_select(out=headof[:, :], in_=headof[:, :], compare_op=ALU.is_ge, fill=0.0,
                                      base=HD - 1, pattern=[[HD, 8]], channel_multiplier=-1))
            c.link(pool.memset(expand, 1.0))
            c.link(pool.affine_select(out=expand, in_=expand, compare_op=ALU.is_ge, fill=0.0,
                                      base=0, pattern=[[1, D]], channel_multiplier=-HD))
            c.link(pool.affine_select(out=expand, in_=expand, compare_op=ALU.is_ge, fill=0.0,
                                      base=HD - 1, pattern=[[-1, D]], channel_multiplier=HD))
            c.link(pool.affine_select(out=before[:, :], in_=onesb[:, :], compare_op=ALU.is_gt, fill=0.0,
                                      base=0, pattern=[[1, P]], channel_multiplier=-1))
            c.link(pool.iota(ids[:, :], pattern=[[P, NT]], base=0, channel_multiplier=1))
            c.link(pool.iota(slot_i, pattern=[[1, NS], [0, E - 1]], base=0, channel_multiplier=0))
            c.link(pool.iota(rank_i, pattern=[[-1, E]], base=E, channel_multiplier=0))
            pool.tensor_copy(slot[:, :, :], slot_i)
            pool.tensor_copy(rank[:, :], rank_i)
            c.link(pool.memset(pad, 0.0))
            pool.iota(pad[:, IDC:IDC + 1].bitcast(I32), pattern=[[0, 1]], base=NOWHERE,
                      channel_multiplier=0).then_inc(s.pool_consts, 1)
            def rstds(t, mv_ready, done, per):
                pool.wait_ge(mv_ready, t + 4)
                pool.sem_inc(s.pool_past, 1)
                c.link(pool.tensor_scalar(ve[:, :], mv[:, :, 1], EPS, None, ALU.add))
                pool.tensor_tensor(rstd[:, :], ve[:, :], mhalf[:, :], ALU.pow).then_inc(done, 1)

            with pool.Fori(0, NT // 4) as i:
                c.enter(i, 2)
                rstds(4 * i, s.mv_a, s.rstd_a, 2)
                rstds(4 * i, s.mv_b, s.rstd_b, 2)
            c.leave(NT // 4)
            pool.wait_ge(s.ld_l1, 16 * 14)
            pool.tensor_scalar(keep, keep8[:, :], -1.0, 1.0, ALU.mult, ALU.add).then_inc(s.keep_sb, 1)
            c.link(pool.tensor_scalar(mrow, mrow8[:, :], NEG, None, ALU.mult))
            mrow3 = mrow.rearrange("p (b k) -> p b k", b=NB)
            for b in range(NB):
                pool.tensor_copy(mask16[:, b, :].rearrange("p (h k) -> p h k", h=H),
                                 mrow3[:, b, :].unsqueeze(1).to_broadcast([1, H, KEYS]))
            for k in range(3):
                f3 = far3[:, k, :].rearrange("p (h k) -> p h k", h=H)
                ins = pool.tensor_copy(f3, tab0[:, :].unsqueeze(2).to_broadcast([1, H, KEYS]))
                if k < 2:
                    c.link(ins)
                    c.link(pool.tensor_tensor(tab0[:, :], tab0[:, :], f3[:, :, 0], ALU.subtract))
            ins.then_inc(s.const_sb, 1)
            pool.wait_ge(s.ld_ext, 16)
            c.link(pool.tensor_copy(ext[:, 0:MAXD - 1], tabT[:, 0:1].to_broadcast([H, MAXD - 1])))
            pool.tensor_copy(ext[:, MAXD - 1:EXT], tabT[:, 0:EXT - MAXD + 1]).then_inc(s.ext_sb, 1)
            pool.wait_ge(s.wss_sb, 1)
            pool.tensor_tensor(wss[:, 1:2], wss[:, 0:1], half[:, :], ALU.pow).then_inc(s.wnorm_sb, 1)
            pool.wait_ge(s.k1_sb, 1)
            K1B = K1T[:, :, :].rearrange("p c (b k) -> p c b k", b=NB)
            for b in range(NB):
                for ci in range(CH):
                    n = (b * CH + ci) * 8
                    last = pool.tensor_tensor(KBD[:, n:n + 8, :],
                                              K1B[:, ci, b, :].unsqueeze(1).to_broadcast([P, 8, KEYS]),
                                              headof[:, :].unsqueeze(2).to_broadcast([P, 8, KEYS]), ALU.mult)
            last.then_inc(s.kbd_sb, 1)


            def all_max(k, ready, done):
                pool.wait_ge(ready, 1)
                pool.partition_all_reduce(sc[:, k + 1:k + 2], sc[:, k:k + 1], P,
                                          bass.bass_isa.ReduceOp.max).then_inc(done, 1)

            all_max(0, s.ax_sb, s.ar_x)
            all_max(2, s.am_g, s.ar_g)
            all_max(4, s.am_z, s.ar_z)
            all_max(6, s.am_u, s.ar_u)
            all_max(8, s.am_p, s.ar_p)
            for n in range(NEAR):
                pool.wait_ge(s.ld_near, 16 * (n + 1))
                for k in range(3):
                    ins = pool.tensor_copy(BN[:, 3 * n + k, :], bstage)
                    if k < 2:
                        c.link(ins)
                        c.link(pool.tensor_tensor(bstage, bstage, BN[:, 3 * n + k, :], ALU.subtract))
                ins.then_inc(s.near_sb, 1)
            with pool.Fori(0, NT // 4) as i:
                c.enter(i, 1)
                rstds(4 * i, s.mv_c, s.rstd_c, 1)
            c.leave(NT // 4)
            with pool.Fori(0, NT // 4) as i:
                c.enter(i, 1)
                rstds(4 * i, s.mv_d, s.rstd_d, 1)
            c.leave(NT // 4)
            pool.wait_ge(s.pads_written, 16)
            pool.wait_ge(s.pos_sb, 1)
            for t in range(NT):
                pool.indirect_dma_start(rows_d, bass.IndirectOffsetOnAxis(pos_i[:, t:t + 1], 0),
                                        X[:, t, :], None).then_inc(s.scattered, 16)

            def rows_out(u, t):
                pool.wait_ge(s.res_sb, t + 1)
                pool.sem_inc(s.pool_past, 1)
                pool.indirect_dma_start(out.rearrange("b s d -> (b s) d"),
                                        bass.IndirectOffsetOnAxis(rid[:, u:u + 1], 0),
                                        res[:, u, :], None, bounds_check=NB * S - 1,
                                        oob_is_err=False).then_inc(s.rows_out0 if u == 0 else s.rows_out1, 16)

            with pool.Fori(0, NS // 2) as i:
                rows_out(0, 2 * i)
                rows_out(1, 2 * i + 1)
            rows_out(0, NS - 1)
            pool.wait_ge(s.rows_out0, 16 * (NS // 2 + 1))
            pool.wait_ge(s.rows_out1, 16 * (NS // 2))

        @block.scalar
        def _(act):
            c = Chain(act, s.act_step)

            def copy(out_, in_, ready, n, done, **k):
                act.wait_ge(ready, n)
                act.activation(out_, in_, ACT.Copy, **k).then_inc(done, 1)

            act.wait_ge(s.ld_l0, 16 * 9)
            act.activation(tg[:, :], gates[:, :], ACT.Tanh).then_inc(s.tg_sb, 1)
            act.wait_ge(s.tg_sb, 1)
            copy(CTXT, pb[0][:, 0:2 * NB * KEYS].rearrange("p (c n) -> p c n", c=CH), s.ctxT_ps, 1, s.ctxT_sb)
            copy(WQ0T, pb[1].rearrange("p (c n) -> p c n", c=CH), s.wq0T_ps, 1, s.wq0T_sb)
            copy(A0[:, :, :], pb[3][:, 0:2 * NB * KEYS].rearrange("p (c n) -> p c n", c=CH), s.a0_ps, 1, s.a0_sb)
            copy(R0[:, :], pb[3][0:1, 320:320 + NB * KEYS], s.a0_ps, 1, s.a0_sb)
            copy(V0[:, :, :], pb[4][0:KEYS, :].rearrange("p (b n) -> p b n", b=NB), s.v0_ps, 1, s.v0_sb,
                 scale=tg[0:KEYS, 0:1])
            with act.Fori(0, NT // 4) as i:
                for u in range(4):
                    copy(yTa[:, u, :], pb[u][:, 0:D], s.yT_ps, 4 * i + u + 1, s.yT_sb)
                for u in range(4):
                    act.wait_ge(s.nmax_a, 4 * i + u + 1)
                    act.activation(pa[:, u, :], pb[4 + u][:, 0:KEYS], ACT.Exp, bias=nmax[:, u:u + 1],
                                   accum_out=den[:, u:u + 1]).then_inc(s.p0, 1)
                for u in range(4):
                    copy(pTa[:, u, :], pb[u][0:KEYS, 0:P], s.pT0_ps, 4 * i + u + 1, s.pT0_sb)
                for u in range(4):
                    copy(YT[:, :, ds((4 * i + u) * P, P)], pb[u][:, 0:D].rearrange("p (c n) -> p c n", c=CH),
                         s.y2T_ps, 4 * i + u + 1, s.y2T_sb)
            act.wait_ge(s.ld_l1, 16 * 14)
            act.activation(els[:, :], ls[:, :], ACT.Exp).then_inc(s.els_sb, 1)
            copy(V1[:, :, 0:HD], pb[7][0:KEYS, :].rearrange("p (n d) -> p n d", d=HD), s.v1_ps, 1, s.v1_sb)
            copy(WRT, pb[0][0:G, 0:D], s.wrT_ps, 1, s.wrT_sb)
            copy(WGNT[:, :], pb[0][0:G, D:D + E], s.wgT_ps, 1, s.wgT_sb)
            copy(GM[:, :, :], pb[1][:, 0:CH * E].rearrange("p (c e) -> p c e", c=CH), s.gm_ps, 1, s.gm_sb)
            for g in range(9):
                copy(FW[:, g * 512:(g + 1) * 512], pb[g % 8], s.wT_ps, g + 1, s.wT_sb)
            for q in range(NQB):
                copy(YT[:, :, q * QB:(q + 1) * QB], YT[:, :, q * QB:(q + 1) * QB], s.tq_y, q + 1, s.nq, bias=-MAGIC)
            act.sem_inc(s.gu_sb, FJ)
            act.wait_ge(s.ld_const, 16 * 7)
            act.wait_ge(s.pads_written, 16)
            act.wait_ge(s.ext_stored, 16)
            with act.Fori(0, NQB) as q:
                for j in range(FJ):
                    copy(GT[:, j, ds(q * QB, QB)], pb[j], s.gu_ps, FJ * q + j + 1, s.gu_sb)
            act.wait_ge(s.scal_g, 1)
            with act.Fori(0, NQB) as q:
                c.enter(q, 2)
                for h in range(2):
                    for j in range(3 * h, 3 * h + 3):
                        copy(UT_[:, j, ds(q * QB, QB)], pb[j], s.gu_ps, FJ * (NQB + q) + j + 1, s.gu_sb)
                    act.wait_ge(s.z_done, 2 * q + h + 1)
                    n3 = ng[:, h, :].rearrange("p (j n) -> p j n", j=3)
                    c.link(act.activation(n3, GT[:, 3 * h:3 * h + 3, ds(q * QB, QB)], ACT.Copy,
                                          scale=sc[:, 13:14]))
                    act.activation(sig[:, h, :], ng[:, h, :], ACT.Sigmoid, scale=sc[:, 12:13]).then_inc(s.sig_done, 1)
            c.leave(NQB)
            act.wait_ge(s.scal_u, 1)
            with act.Fori(0, NQB) as q:
                for h in range(2):
                    act.wait_ge(s.p_done, 2 * q + h + 1)
                    act.activation(nz[:, h, :].rearrange("p (j n) -> p j n", j=3),
                                   GT[:, 3 * h:3 * h + 3, ds(q * QB, QB)], ACT.Copy, scale=sc[:, 15:16])
                    act.activation(nu[:, h, :].rearrange("p (j n) -> p j n", j=3),
                                   UT_[:, 3 * h:3 * h + 3, ds(q * QB, QB)], ACT.Copy,
                                   scale=sc[:, 17:18]).then_inc(s.nzu_done, 1)

            def ints(q):
                copy(UT_[:, :, ds(q * QB, QB)], GT[:, :, ds(q * QB, QB)], s.tq_p, q + 1, s.no_done, bias=-MAGIC)

            def y3_out(q):
                for u in range(4):
                    copy(YT[:, :, ds((4 * q + u) * P, P)], pb[4 + u][:, 0:D].rearrange("p (c n) -> p c n", c=CH),
                         s.y3T_ps, 4 + 4 * q + u + 1, s.y3T_sb)
            ints(0)
            ints(1)
            with act.Fori(0, 2) as q:
                y3_out(q)
                ints(q + 2)
            with act.Fori(2, NQB) as q:
                y3_out(q)

            def pair(t):
                for u in range(2):
                    for ci in range(CH):
                        act.wait_ge(s.q_ps, t + u + 1)
                        ins = act.activation(qT[:, u, ci * P:(ci + 1) * P], pb[u][:, ci * P:(ci + 1) * P], ACT.Identity,
                                             bias=bq1[:, ci:ci + 1])
                    ins.then_inc(s.q_sb, 1)
                for k in range(2 * NQ + 2):
                    if k < 2 * NQ:
                        e4 = e_[:, k // NQ, (k % NQ) * HQK:(k % NQ + 1) * HQK]
                        act.wait_ge(s.e_sub, NQ * t + k + 1)
                        act.activation(e4, e4, ACT.Exp).then_inc(s.e_exp, 1)
                    if k >= 2:
                        m = k - 2
                        copy(pT[:, m // NQ, (m % NQ) * 512:(m % NQ + 1) * 512], pb[6 + m % 2][0:KEYS, :],
                             s.pT_ps, NQ * t + m + 1, s.pT_sb)
                        if m == NQ + 1:
                            copy(attT[:, 0, :], pb[0][:, 0:D], s.attT_ps, t + 1, s.attT_sb)
                copy(attT[:, 1, :], pb[1][:, 0:D], s.attT_ps, t + 2, s.attT_sb)

            for b in range(NB):
                pair(b * TB)
                with act.Fori(0, (TB - NEAR) // 2) as i:
                    pair(b * TB + NEAR + 2 * i)
            with act.Fori(0, NT // 4) as i:
                for u in range(4):
                    copy(y4T[:, u, :], pb[u][:, 0:D], s.y4T_ps, 4 * i + u + 1, s.y4T_sb)
            act.wait_ge(s.lx_sb, 1)
            act.activation(LX, LX, ACT.Exp).then_inc(s.ex_sb, 1)

            def expert(u, t, rows):
                act.wait_ge(s.rows_in0 if u == 0 else s.rows_in1, rows)
                act.activation(ys[:, u, :], rb[:, u, 0:D], ACT.Identity, scale=rb[:, u, RSTD:RSTD + 1],
                               bias=rb[:, u, NMR:NMR + 1]).then_inc(s.ys_sb, 1)

            def transposed(u, t):
                copy(ysT[:, u, :], pb[u][:, 0:D], s.ysT_ps, t + 1, s.ysT_sb)

            def gelu(u, t):
                act.wait_ge(s.hb_sb, t + 1)
                act.activation(hb[:, u, :], hb[:, u, :], ACT.Gelu).then_inc(s.gelu_sb, 1)

            with act.Fori(0, NS // 2) as i:
                for u in range(2):
                    expert(u, 2 * i + u, 16 * (i + 1))
                for u in range(2):
                    transposed(u, 2 * i + u)
                for u in range(2):
                    gelu(u, 2 * i + u)
            expert(0, NS - 1, 16 * (NS // 2 + 1))
            transposed(0, NS - 1)
            gelu(0, NS - 1)

        @block.vector
        def _(dve):
            c = Chain(dve, s.dve_step)

            def stats(tiles, ready, after=None):
                if after is not None:
                    dve.wait_ge(*after)
                    dve.sem_inc(s.dve_past, 1)
                marks = [c.mark(dve.bn_stats(stat[:, u, :], x)) for u, x in enumerate(tiles)]
                dve.wait_ge(s.dve_step, marks[3])
                dve.sem_inc(s.dve_past, 1)
                for u in range(4):
                    dve.bn_aggr(mv[:, u, :], stat[:, u, :]).then_inc(ready, 1)

            def normalise(u, y, x):
                return dve.tensor_scalar(y, x, mv[:, u, 0:1], rstd[:, u:u + 1], ALU.subtract, ALU.mult)

            def rows(t):
                return X[:, ds(t, 1), 0:D].rearrange("p a d -> p (a d)")

            dve.wait_ge(s.ld_l0, 16 * 9)
            dve.wait_ge(s.k0_ps, 1)
            for ci in range(CH):
                ins = dve.tensor_scalar(K0T[:, ci, :], pb[2][:, ci * NB * KEYS:(ci + 1) * NB * KEYS],
                                        bk0[:, ci:ci + 1], D ** -0.5, ALU.add, ALU.mult)
            ins.then_inc(s.k0_sb, 1)
            dve.wait_ge(s.pool_consts, 1)
            dve.tensor_copy(XI[:, :, IDC], ids[:, :])
            dve.wait_ge(s.ld_x, 16 * NB)
            with dve.Fori(0, NT // 4) as i:
                c.enter(i, 17)
                t = 4 * i
                stats([rows(t + u) for u in range(4)], s.mv_a)
                dve.wait_ge(s.rstd_a, i + 1)
                for u in range(4):
                    normalise(u, ya[:, u, :], rows(t + u)).then_inc(s.y_a, 1)
                for u in range(4):
                    dve.wait_ge(s.s0_ps, t + u + 1)
                    dve.tensor_reduce(nmax[:, u:u + 1], pb[4 + u][:, 0:KEYS], AX.X, ALU.max,
                                      negate=True).then_inc(s.nmax_a, 1)
                dve.wait_ge(s.p0, t + 4)
                c.link(dve.reciprocal(rden[:, :], den[:, :]))
                marks = []
                for u in range(4):
                    dve.wait_ge(s.o0_ps, t + u + 1)
                    marks.append(c.mark(dve.scalar_tensor_tensor(rows(t + u), pb[4 + u][:, 0:D], rden[:, u:u + 1],
                                                                 rows(t + u), ALU.mult, ALU.add)))
                stats([rows(t + u) for u in range(4)], s.mv_b, (s.dve_step, marks[3]))
                dve.wait_ge(s.rstd_b, i + 1)
                marks = []
                for u in range(4):
                    ins = normalise(u, y2a[:, u, :], rows(t + u))
                    ins.then_inc(s.y_b, 1)
                for u in range(4):
                    dve.wait_ge(s.y_b, t + u + 1)
                    c.mark(dve.tensor_reduce(amY[:, ds(t + u, 1)], y2a[:, u, :], AX.X, ALU.max,
                                             apply_absolute_value=True))
            c.leave(NT // 4)

            def scalar(k, in_, op0, s1, op1=None, s2=None):
                c.link(dve.tensor_scalar(sc[:, k:k + 1], in_, s1, s2, op0, op1 if op1 is not None else ALU.bypass))

            def step_of(k, amax, unit):
                if unit is None:
                    scalar(k, amax, ALU.mult, 1.0 / QMAX, ALU.max, TINY)
                    c.link(dve.reciprocal(sc[:, k + 1:k + 2], sc[:, k:k + 1]))
                else:
                    scalar(k, amax, ALU.mult, unit)
                    scalar(k, sc[:, k:k + 1], ALU.mult, 1.0 / QMAX, ALU.max, TINY)
                    c.link(dve.reciprocal(sc[:, k + 1:k + 2], sc[:, k:k + 1]))
                    scalar(k + 1, sc[:, k + 1:k + 2], ALU.mult, unit)

            dve.wait_ge(s.dve_step, c.base)
            dve.tensor_reduce(sc[:, 0:1], amY[:, :], AX.X, ALU.max).then_inc(s.ax_sb, 1)
            dve.wait_ge(s.ld_ffn, 16 * 3)
            c.link(dve.tensor_reduce(wamax[:, :], WN, AX.X, ALU.max, apply_absolute_value=True))
            c.link(dve.tensor_scalar(wscale[:, :], wamax[:, :], 1.0 / 7.0, TINY, ALU.mult, ALU.max))
            c.link(dve.reciprocal(wrec[:, :], wscale[:, :]))
            c.link(dve.tensor_tensor(WN, WN, wrec[:, :].unsqueeze(2).to_broadcast([P, 144, BLK]), ALU.mult))
            c.link(dve.tensor_scalar(WN, WN, MAGIC, MAGIC, ALU.add, ALU.subtract))
            dve.tensor_tensor(WN, WN, wscale[:, :].unsqueeze(2).to_broadcast([P, 144, BLK]),
                              ALU.mult).then_inc(s.wq_sb, 1)
            dve.wait_ge(s.els_sb, 1)
            dve.tensor_scalar(hscale[:, :], els[:, :], 4.0, HD ** -0.5, ALU.min, ALU.mult).then_inc(s.hsc_sb, 1)
            c.link(dve.tensor_tensor(wg2[:, :], wg[:, :], wg[:, :], ALU.mult))
            dve.tensor_reduce(wss[:, 0:1], wg2[:, :], AX.X, ALU.add).then_inc(s.wss_sb, 1)
            dve.memset(V1[:, :, HD:VE], 1.0)
            c.link(dve.tensor_scalar(WO1[:, :, :], WO1[:, :, :], tg[:, 1:2], None, ALU.mult))
            dve.tensor_scalar(bo1[:, :], bo1[:, :], tg[0:1, 1:2], None, ALU.mult).then_inc(s.wo_sb, 1)
            dve.wait_ge(s.csc_ps, 1)
            c.link(dve.tensor_copy(cscale[:, :], pb[5][:, 0:CH]))
            dve.wait_ge(s.k1_ps, 1)
            dve.wait_ge(s.keep_sb, 1)
            for ci in range(CH):
                c.link(dve.tensor_scalar(K1T[:, ci, :], pb[6][:, ci * NB * KEYS:(ci + 1) * NB * KEYS],
                                         bk1[:, ci:ci + 1], cscale[:, ci:ci + 1], ALU.add, ALU.mult))
            dve.tensor_tensor(K1T[:, :, :], K1T[:, :, :], keep.unsqueeze(1).to_broadcast([P, CH, NB * KEYS]),
                              ALU.mult).then_inc(s.k1_sb, 1)
            dve.wait_ge(s.wnorm_sb, 1)
            c.link(dve.tensor_scalar(wss[:, 1:2], wss[:, 1:2], 1e-4, None, ALU.max))
            c.link(dve.reciprocal(wss[:, 2:3], wss[:, 1:2]))
            dve.tensor_scalar(wgn[:, :], wg[:, :], wss[:, 2:3], None, ALU.mult).then_inc(s.wgn_sb, 1)
            dve.wait_ge(s.ar_x, 1)
            step_of(10, sc[:, 1:2], None)
            dve.wait_ge(s.y2T_sb, NT)
            for q in range(NQB):
                dve.tensor_scalar(YT[:, :, q * QB:(q + 1) * QB], YT[:, :, q * QB:(q + 1) * QB], sc[:, 11:12], MAGIC,
                                  ALU.mult, ALU.add).then_inc(s.tq_y, 1)
            with dve.Fori(0, NQB) as q:
                c.enter(q, FJ)
                for j in range(FJ):
                    dve.wait_ge(s.gu_sb, FJ + FJ * q + j + 1)
                    c.mark(dve.tensor_reduce(amG[:, ds(FJ * q + j, 1)], GT[:, j, ds(q * QB, QB)], AX.X, ALU.max,
                                             apply_absolute_value=True))
            c.leave(NQB)
            dve.wait_ge(s.dve_step, c.base)
            dve.tensor_reduce(sc[:, 2:3], amG[:, :], AX.X, ALU.max).then_inc(s.am_g, 1)
            dve.wait_ge(s.ar_g, 1)
            step_of(12, sc[:, 3:4], sc[:, 10:11])
            scalar(22, sc[:, 12:13], ALU.mult, 2.0 ** -16)
            dve.sem_inc(s.z_done, 2)
            dve.sem_inc(s.scal_g, 1)
            with dve.Fori(0, NQB) as q:
                c.enter(q, FJ + 4)
                for h in range(2):
                    for j in range(3 * h, 3 * h + 3):
                        dve.wait_ge(s.gu_sb, FJ + FJ * (NQB + q) + j + 1)
                        c.mark(dve.tensor_reduce(amU[:, ds(FJ * q + j, 1)], UT_[:, j, ds(q * QB, QB)], AX.X, ALU.max,
                                                 apply_absolute_value=True))
                    dve.wait_ge(s.sig_done, 2 * q + h + 1)
                    c.link(dve.tensor_scalar(u16[:, h, :], sig[:, h, :], 65536.0, 65535.0, ALU.mult, ALU.min))
                    z = GT[:, 3 * h:3 * h + 3, ds(q * QB, QB)]
                    dve.tensor_tensor(z, ng[:, h, :].rearrange("p (j n) -> p j n", j=3),
                                      u16[:, h, :].rearrange("p (j n) -> p j n", j=3), ALU.mult).then_inc(s.z_done, 1)
                    dve.wait_ge(s.z_done, 2 + 2 * q + h + 1)
                    c.mark(dve.tensor_reduce(amZ[:, ds(2 * q + h, 1)], z, AX.XY, ALU.max, apply_absolute_value=True))
            c.leave(NQB)
            dve.wait_ge(s.dve_step, c.base)
            dve.tensor_reduce(sc[:, 4:5], amZ[:, :], AX.X, ALU.max).then_inc(s.am_z, 1)
            dve.tensor_reduce(sc[:, 6:7], amU[:, :], AX.X, ALU.max).then_inc(s.am_u, 1)
            dve.wait_ge(s.ar_z, 1)
            step_of(14, sc[:, 5:6], sc[:, 22:23])
            dve.wait_ge(s.ar_u, 1)
            step_of(16, sc[:, 7:8], sc[:, 10:11])
            scalar(18, sc[:, 14:15], ALU.mult, sc[:, 16:17])
            dve.sem_inc(s.p_done, 2)
            dve.sem_inc(s.scal_u, 1)
            with dve.Fori(0, NQB) as q:
                c.enter(q, 2)
                for h in range(2):
                    dve.wait_ge(s.nzu_done, 2 * q + h + 1)
                    pr = GT[:, 3 * h:3 * h + 3, ds(q * QB, QB)]
                    dve.tensor_tensor(pr, nz[:, h, :].rearrange("p (j n) -> p j n", j=3),
                                      nu[:, h, :].rearrange("p (j n) -> p j n", j=3), ALU.mult).then_inc(s.p_done, 1)
                    dve.wait_ge(s.p_done, 2 + 2 * q + h + 1)
                    c.mark(dve.tensor_reduce(amP[:, ds(2 * q + h, 1)], pr, AX.XY, ALU.max, apply_absolute_value=True))
            c.leave(NQB)
            dve.wait_ge(s.dve_step, c.base)
            dve.tensor_reduce(sc[:, 8:9], amP[:, :], AX.X, ALU.max).then_inc(s.am_p, 1)
            dve.wait_ge(s.ar_p, 1)
            step_of(19, sc[:, 9:10], sc[:, 18:19])
            scalar(21, sc[:, 19:20], ALU.mult, tg[:, 2:3])
            with dve.Fori(0, NQB) as q:
                b = GT[:, :, ds(q * QB, QB)]
                dve.tensor_scalar(b, b, sc[:, 20:21], MAGIC, ALU.mult, ALU.add).then_inc(s.tq_p, 1)
            with dve.Fori(0, NT // 4) as i:
                c.enter(i, 8)
                t = 4 * i
                for u in range(4):
                    dve.wait_ge(s.dn_ps, t + u + 1)
                    mk = c.mark(dve.scalar_tensor_tensor(rows(t + u), pb[u][:, 0:D], sc[:, 21:22], rows(t + u),
                                                         ALU.mult, ALU.add))
                stats([rows(t + u) for u in range(4)], s.mv_c, (s.dve_step, mk))
                dve.wait_ge(s.rstd_c, i + 1)
                for u in range(4):
                    dve.wait_ge(s.y3T_ps, t + u + 1)
                    normalise(u, y3[:, u, :], rows(t + u)).then_inc(s.y_c, 1)
            c.leave(NT // 4)

            def pair(t, i, per):
                c.enter(i, per)

                def head_out(u):
                    dve.wait_ge(s.o_ps, t + u + 1)
                    o = pb[u][:, 0:H * VE].rearrange("p (h d) -> p h d", d=VE)
                    c.link(dve.reciprocal(rd[:, u, :], o[:, :, HD]))
                    dve.tensor_tensor(att[:, u, :].rearrange("p (h d) -> p h d", d=HD), o[:, :, 0:HD],
                                      rd[:, u, :].unsqueeze(2).to_broadcast([P, H, HD]), ALU.mult).then_inc(s.att_sb, 1)

                def residual(u):
                    dve.wait_ge(s.wo_ps, t + u + 1)
                    dve.tensor_tensor(rows(t + u), pb[u][:, 0:D], rows(t + u), ALU.add).then_inc(s.x3_done, 1)

                for k in range(2 * NQ):
                    u, hq = k // NQ, k % NQ
                    if k == NQ + 3:
                        head_out(0)
                    s4 = pb[2 + k % 4][:, 0:HQK].rearrange("p (h k) -> p h k", h=HQ)
                    m4 = mx[:, k % 2, :]
                    dve.wait_ge(s.s_ps, NQ * t + k + 1)
                    c.link(dve.tensor_reduce(m4, s4, AX.X, ALU.max))
                    dve.tensor_tensor(e_[:, u, hq * HQK:(hq + 1) * HQK].rearrange("p (h k) -> p h k", h=HQ), s4,
                                      m4.unsqueeze(2).to_broadcast([P, HQ, KEYS]), ALU.subtract).then_inc(s.e_sub, 1)
                residual(0)
                head_out(1)
                residual(1)

            per = 2 * NQ + 2
            for b in range(NB):
                pair(b * TB, 0, per)
                c.leave(1)
                with dve.Fori(0, (TB - NEAR) // 2) as i:
                    pair(b * TB + NEAR + 2 * i, i, per)
                c.leave((TB - NEAR) // 2)
            with dve.Fori(0, NT // 4) as i:
                c.enter(i, 8)
                t = 4 * i
                stats([rows(t + u) for u in range(4)], s.mv_d, (s.x3_done, t + 4))
                dve.wait_ge(s.rstd_d, i + 1)
                for u in range(4):
                    normalise(u, y4[:, u, :], rows(t + u)).then_inc(s.y_d, 1)
                dve.tensor_copy(X[:, ds(t, 4), RSTD], rstd[:, :])
                dve.scalar_tensor_tensor(X[:, ds(t, 4), NMR], mv[:, :, 0], -1.0, rstd[:, :], ALU.mult, ALU.mult)
                for u in range(4):
                    dve.wait_ge(s.lg_ps, t + u + 1)
                    c.mark(dve.tensor_copy(LG[:, ds(t + u, 1), :].rearrange("p a e -> p (a e)"), pb[4 + u][:, 0:E]))
            c.leave(NT // 4)
            dve.wait_ge(s.dve_step, c.base)
            c.link(dve.tensor_reduce(LM[:, :], LG, AX.X, ALU.max))
            LMB = LM[:, :].unsqueeze(2).to_broadcast([P, NT, E])
            dve.tensor_tensor(LX, LG, LMB, ALU.subtract).then_inc(s.lx_sb, 1)
            c.link(dve.tensor_tensor(OH, LG, LMB, ALU.is_ge))
            c.link(dve.tensor_tensor(OH, OH, rank[:, :].unsqueeze(1).to_broadcast([P, NT, E]), ALU.mult))
            c.link(dve.tensor_reduce(LM[:, :], OH, AX.X, ALU.max))
            c.link(dve.tensor_tensor(OH, OH, LMB, ALU.is_equal))
            dve.tensor_copy(OHB[:, :, :], OH).then_inc(s.oh_sb, 1)
            dve.wait_ge(s.ex_sb, 1)
            c.link(dve.tensor_reduce(LM[:, :], LX, AX.X, ALU.add))
            c.link(dve.reciprocal(LM[:, :], LM[:, :]))
            dve.tensor_scalar(X[:, :, COEF], LM[:, :], tg[:, 3:4], None, ALU.mult)
            dve.wait_ge(s.cnt_ps, 1)
            dve.memset(CUM[:, 0, :], 0.0)
            c.link(dve.tensor_copy(TOT, pb[1][:, 0:NT * E].rearrange("p (t e) -> p t e", e=E)))
            for t in range(NT):
                c.link(dve.tensor_tensor(CUM[:, t + 1, :], CUM[:, t, :], TOT[:, t, :], ALU.add))
            c.link(dve.tensor_scalar(cnt_i[:, :], CUM[:, NT, :], float(P - 1), None, ALU.add))
            c.link(dve.tensor_scalar(cnt_i[:, :], cnt_i[:, :], 7, None, ALU.arith_shift_right))
            c.link(dve.tensor_copy(tiles_e[:, :], cnt_i[:, :]))
            c.link(dve.memset(start_e[:, 0:1], 0.0))
            for e in range(1, E):
                c.link(dve.tensor_tensor(start_e[:, e:e + 1], start_e[:, e - 1:e], tiles_e[:, e - 1:e], ALU.add))
            c.link(dve.tensor_scalar(start128[:, :], start_e[:, :], float(P), None, ALU.mult))
            c.link(dve.tensor_tensor(CUM[:, 0:NT, :], CUM[:, 0:NT, :],
                                     start128[:, :].unsqueeze(1).to_broadcast([P, NT, E]), ALU.add))
            c.link(dve.tensor_tensor(CUM[:, 0:NT, :], CUM[:, 0:NT, :],
                                     pb[0][:, 0:NT * E].rearrange("p (t e) -> p t e", e=E), ALU.add))
            c.link(dve.tensor_tensor(CUM[:, 0:NT, :], CUM[:, 0:NT, :], OH, ALU.mult))
            c.link(dve.tensor_reduce(LM[:, :], CUM[:, 0:NT, :], AX.X, ALU.add))
            dve.tensor_copy(pos_i[:, :], LM[:, :]).then_inc(s.pos_sb, 1)
            c.link(dve.tensor_tensor(slot[:, :, :], slot[:, :, :],
                                     start_e[:, 1:E].unsqueeze(1).to_broadcast([P, NS, E - 1]), ALU.is_ge))
            c.link(dve.tensor_reduce(eslot[:, :], slot[:, :, :], AX.X, ALU.add))
            dve.tensor_copy(EXPS[:, :], eslot[:, :]).then_inc(s.slots_sb, 1)
            dve.wait_ge(s.slots_sb, 1)
            dve.wait_ge(s.ld_b1, 16)
            dve.wait_ge(s.ld_b2, 16)

            def bias1(u, t, e):
                dve.wait_ge(s.h_ps, t + 1)
                dve.tensor_tensor(hb[:, u, :], pb[2 + u], B1[:, ds(e * HID, HID)], ALU.add).then_inc(s.hb_sb, 1)

            def hidden(u, t):
                dve.wait_ge(s.hT_ps, t + 1)
                dve.tensor_copy(hT[:, u, :], pb[4 + u]).then_inc(s.hT_sb, 1)

            def result(u, t, e):
                dve.wait_ge(s.eo_ps, t + 1)
                dve.tensor_copy(rid[:, u:u + 1], rb[:, u, IDC:IDC + 1].bitcast(I32))
                c.link(dve.tensor_tensor(ob[:, u, :], pb[6 + u][:, 0:D], B2[:, ds(e * D, D)], ALU.add))
                dve.scalar_tensor_tensor(res[:, u, :], ob[:, u, :], rb[:, u, COEF:COEF + 1], rb[:, u, 0:D],
                                         ALU.mult, ALU.add).then_inc(s.res_sb, 1)

            def experts(us, t, waits):
                es = [dve.value_load(EXPS[0:1, ds(t + u, 1)], min_val=0, max_val=E - 1) for u in us]
                for u in us:
                    bias1(u, t + u, es[u])
                for u in us:
                    hidden(u, t + u)
                for u in us:
                    if waits is not None:
                        dve.wait_ge(s.rows_out0 if u == 0 else s.rows_out1, waits)
                    result(u, t + u, es[u])

            c.enter(0, 2)
            experts((0, 1), 0, None)
            c.leave(1)
            with dve.Fori(1, NS // 2) as i:
                c.enter(i - 1, 2)
                experts((0, 1), 2 * i, 16 * i)
            c.leave(NS // 2 - 1)
            c.enter(0, 1)
            experts((0,), NS - 1, 16 * (NS // 2))
            c.leave(1)

        @block.tensor
        def _(pe):
            def mm(out_, lhsT, rhs, first, last):
                return pe.matmul(out_, lhsT=lhsT, rhs=rhs, start=first, stop=last)

            pe.wait_ge(s.consts, 1)
            pe.wait_ge(s.ld_l0, 16 * 9)
            for ci in range(CH):
                for b in range(NB):
                    o = (ci * NB + b) * KEYS
                    ins = pe.transpose(pb[0][:, o:o + KEYS], CTX[:, b, ci * P:(ci + 1) * P], ident[0:KEYS, 0:KEYS])
            ins.then_inc(s.ctxT_ps, 1)
            for dj in range(CH):
                for ci in range(CH):
                    ins = pe.transpose(pb[1][:, dj * D + ci * P:dj * D + (ci + 1) * P],
                                       WQ0[:, ci, dj * P:(dj + 1) * P], ident[:, :])
            ins.then_inc(s.wq0T_ps, 1)

            def keysT(ps, w, done):
                for dj in range(CH):
                    for ci in range(CH):
                        ins = mm(ps[:, dj * NB * KEYS:(dj + 1) * NB * KEYS], w[:, ci, dj * P:(dj + 1) * P],
                                 CTXT[:, ci, :], ci == 0, ci == CH - 1)
                ins.then_inc(done, 1)

            def values(ps, w, bias, done):
                for b in range(NB):
                    for ci in range(CH):
                        mm(ps[0:KEYS, b * D:(b + 1) * D], CTXT[:, ci, b * KEYS:(b + 1) * KEYS], w[:, ci, :], ci == 0, False)
                    ins = mm(ps[0:KEYS, b * D:(b + 1) * D], ones[0:1, 0:KEYS], bias, False, True)
                ins.then_inc(done, 1)

            pe.wait_ge(s.ctxT_sb, 1)
            keysT(pb[2], WK0, s.k0_ps)
            values(pb[4], WV0, bv0, s.v0_ps)
            pe.wait_ge(s.wq0T_sb, 1)
            pe.wait_ge(s.k0_sb, 1)
            for ci in range(CH):
                for dj in range(CH):
                    mm(pb[3][:, ci * NB * KEYS:(ci + 1) * NB * KEYS], WQ0T[:, dj, ci * P:(ci + 1) * P], K0T[:, dj, :],
                       dj == 0, dj == CH - 1)
            for dj in range(CH):
                ins = mm(pb[3][0:1, 320:320 + NB * KEYS], bq0[:, dj:dj + 1], K0T[:, dj, :], dj == 0, dj == CH - 1)
            ins.then_inc(s.a0_ps, 1)
            pe.wait_ge(s.a0_sb, 2)
            pe.wait_ge(s.v0_sb, 1)

            def transposed(ps, y, done):
                for ci in range(CH):
                    ins = pe.transpose(ps[:, ci * P:(ci + 1) * P], y[:, ci * P:(ci + 1) * P], ident[:, :])
                ins.then_inc(done, 1)

            for b in range(NB):
                with pe.Fori(0, TB // 4) as i:
                    t = b * TB + 4 * i
                    for u in range(4):
                        pe.wait_ge(s.y_a, t + u + 1)
                        transposed(pb[u], ya[:, u, :], s.yT_ps)
                    for u in range(4):
                        pe.wait_ge(s.yT_sb, t + u + 1)
                        sl = slice(b * KEYS, (b + 1) * KEYS)
                        for ci in range(CH):
                            mm(pb[4 + u][:, 0:KEYS], yTa[:, u, ci * P:(ci + 1) * P], A0[:, ci, sl], ci == 0, False)
                        mm(pb[4 + u][:, 0:KEYS], ones[0:1, :], R0[:, sl], False, True).then_inc(s.s0_ps, 1)
                    for u in range(4):
                        pe.wait_ge(s.p0, t + u + 1)
                        pe.transpose(pb[u][0:KEYS, 0:P], pa[:, u, :], ident[:, :]).then_inc(s.pT0_ps, 1)
                    for u in range(4):
                        pe.wait_ge(s.pT0_sb, t + u + 1)
                        mm(pb[4 + u][:, 0:D], pTa[:, u, :], V0[:, b, :], True, True).then_inc(s.o0_ps, 1)
                    for u in range(4):
                        pe.wait_ge(s.y_b, t + u + 1)
                        transposed(pb[u], y2a[:, u, :], s.y2T_ps)
                    pe.wait_ge(s.y2T_sb, t + 4)
            pe.wait_ge(s.ld_l1, 16 * 14)
            pe.wait_ge(s.pool_consts, 1)
            pe.wait_ge(s.hsc_sb, 1)
            for ci in range(CH):
                ins = mm(pb[5][:, ci:ci + 1], expand[:, ci * P:(ci + 1) * P], hscale[:, :], True, True)
            ins.then_inc(s.csc_ps, 1)
            keysT(pb[6], WK1, s.k1_ps)
            values(pb[7], WV1, bv1, s.v1_ps)
            for ci in range(CH):
                ins = pe.transpose(pb[0][0:G, ci * P:(ci + 1) * P], WR[:, ci, :], ident[:, :])
            ins.then_inc(s.wrT_ps, 1)
            pe.wait_ge(s.wgn_sb, 1)
            pe.wait_ge(s.wrT_sb, 1)
            pe.transpose(pb[0][0:G, D:D + E], wgn[:, :], ident[0:E, 0:E]).then_inc(s.wgT_ps, 1)
            pe.wait_ge(s.wgT_sb, 1)
            for ci in range(CH):
                ins = mm(pb[1][:, ci * E:(ci + 1) * E], WRT[:, ci * P:(ci + 1) * P], WGNT[:, :], True, True)
            ins.then_inc(s.gm_ps, 1)
            pe.wait_ge(s.gm_sb, 1)
            pe.wait_ge(s.k1_sb, 1)
            pe.wait_ge(s.v1_sb, 1)
            pe.wait_ge(s.wq_sb, 1)
            WF = BIGG[:, 0:4608]
            src = [1536 + j * D + ci * P for ci in range(CH) for j in range(FJ)]
            src += [j * D + ci * P for ci in range(CH) for j in range(FJ)]
            src += [3072 + o * F + j * P for j in range(FJ) for o in range(CH)]
            for g in range(9):
                if g == 8:
                    pe.wait_ge(s.wT_sb, 1)
                for k in range(4):
                    ins = pe.transpose(pb[g % 8][:, k * P:(k + 1) * P], WF[:, src[4 * g + k]:src[4 * g + k] + P], ident[:, :])
                ins.then_inc(s.wT_ps, 1)
            pe.wait_ge(s.wT_sb, 9)

            for n, w in enumerate((WGT, WUT)):
                with pe.Fori(0, NQB) as q:
                    if n == 0:
                        pe.wait_ge(s.nq, q + 1)
                    for j in range(FJ):
                        pe.wait_ge(s.gu_sb, FJ * (n * NQB + q) + j + 1)
                        for ci in range(CH):
                            ins = mm(pb[j], w[:, ci, j * P:(j + 1) * P], YT[:, ci, ds(q * QB, QB)], ci == 0, ci == CH - 1)
                        ins.then_inc(s.gu_ps, 1)

            def down(q):
                pe.wait_ge(s.no_done, q + 1)
                for u in range(4):
                    t = 4 * q + u
                    if q:
                        pe.wait_ge(s.mv_c, t - 3)
                    for j in range(FJ):
                        ins = mm(pb[u][:, 0:D], UT_[:, j, t * P:(t + 1) * P], WDT[:, j, :], j == 0, j == FJ - 1)
                    ins.then_inc(s.dn_ps, 1)

            def y3_in(q):
                for u in range(4):
                    pe.wait_ge(s.y_c, 4 * q + u + 1)
                    if q:
                        pe.wait_ge(s.y3T_sb, 4 * q + u - 3)
                    transposed(pb[4 + u], y3[:, u, :], s.y3T_ps)
            pe.wait_ge(s.gu_sb, FJ + 2 * FJ * NQB)
            pe.sem_inc(s.y3T_ps, 4)
            for q in range(NQB):
                down(q)
                if q:
                    y3_in(q - 1)
            y3_in(NQB - 1)

            def pair(b, t, near):
                for u in range(2):
                    pe.wait_ge(s.y3T_sb, NT)
                    for dj in range(CH):
                        for ci in range(CH):
                            ins = mm(pb[u][:, dj * P:(dj + 1) * P], WQ1[:, ci, dj * P:(dj + 1) * P],
                                     YT[:, ci, ds((t + u) * P, P)], ci == 0, ci == CH - 1)
                    ins.then_inc(s.q_ps, 1)

                def scores(k):
                    u, hq = k // NQ, k % NQ
                    ps = pb[2 + k % 4][:, 0:HQK]
                    cols = slice(hq * HQK, (hq + 1) * HQK)
                    ci, n = hq // 2, (b * CH + hq // 2) * 8 + (hq % 2) * HQ
                    mm(ps, qT[:, u, ci * P:(ci + 1) * P], KBD[:, n:n + HQ, :].rearrange("p h k -> p (h k)"), True, False)
                    if near:
                        for m in range(3):
                            mm(ps, flipb[:, :], BN[:, 3 * u + m, cols], False, False)
                    ins = mm(ps, onesb[0:1 if near else 4, :], CM[0:1 if near else 4, b, cols], False, True)
                    ins.then_inc(s.s_ps, 1)

                def weightsT(k):
                    u, hq = k // NQ, k % NQ
                    pe.wait_ge(s.e_exp, NQ * t + k + 1)
                    for h in range(HQ):
                        ins = pe.transpose(pb[6 + k % 2][0:KEYS, h * P:(h + 1) * P],
                                           e_[:, u, hq * HQK + h * KEYS:hq * HQK + (h + 1) * KEYS], ident[:, :])
                    ins.then_inc(s.pT_ps, 1)

                def heads(k):
                    u, hq = k // NQ, k % NQ
                    pe.wait_ge(s.pT_sb, NQ * t + k + 1)
                    for h in range(hq * HQ, (hq + 1) * HQ):
                        ins = mm(pb[u][:, h * VE:(h + 1) * VE], pT[:, u, h * P:(h + 1) * P], V1[:, b * H + h, :], True, True)
                    if hq == NQ - 1:
                        ins.then_inc(s.o_ps, 1)

                def project_in(u):
                    pe.wait_ge(s.att_sb, t + u + 1)
                    transposed(pb[u], att[:, u, :], s.attT_ps)

                def project(u):
                    pe.wait_ge(s.attT_sb, t + u + 1)
                    for ci in range(CH):
                        mm(pb[u][:, 0:D], attT[:, u, ci * P:(ci + 1) * P], WO1[:, ci, :], ci == 0, False)
                    mm(pb[u][:, 0:D], ones[0:1, :], bo1[:, :], False, True).then_inc(s.wo_ps, 1)

                for k in range(2 * NQ + 3):
                    if k < 2 * NQ:
                        if k % NQ == 0:
                            pe.wait_ge(s.q_sb, t + k // NQ + 1)
                        scores(k)
                    if 2 <= k < 2 * NQ + 2:
                        weightsT(k - 2)
                    if k >= 3:
                        heads(k - 3)
                    if k == NQ + 3:
                        project_in(0)
                    if k == NQ + 4:
                        project(0)
                project_in(1)
                project(1)
                pe.wait_ge(s.x3_done, t + 2)

            pe.wait_ge(s.kbd_sb, 1)
            pe.wait_ge(s.wo_sb, 1)
            pe.wait_ge(s.ld_const, 16 * 7)
            pe.wait_ge(s.near_sb, NEAR)
            for b in range(NB):
                pair(b, b * TB, True)
                with pe.Fori(0, (TB - NEAR) // 2) as i:
                    pair(b, b * TB + NEAR + 2 * i, False)
            with pe.Fori(0, NT // 4) as i:
                for u in range(4):
                    pe.wait_ge(s.y_d, 4 * i + u + 1)
                    transposed(pb[u], y4[:, u, :], s.y4T_ps)
                for u in range(4):
                    pe.wait_ge(s.y4T_sb, 4 * i + u + 1)
                    for ci in range(CH):
                        ins = mm(pb[4 + u][:, 0:E], y4T[:, u, ci * P:(ci + 1) * P], GM[:, ci, :], ci == 0, ci == CH - 1)
                    ins.then_inc(s.lg_ps, 1)
            pe.wait_ge(s.oh_sb, 1)
            oh = OHB[:, :, :].rearrange("p t e -> p (t e)")
            mm(pb[0][:, 0:NT * E], before[:, :], oh, True, True)
            mm(pb[1][:, 0:NT * E], onesb[:, :], oh, True, True).then_inc(s.cnt_ps, 1)
            pe.wait_ge(s.pos_sb, 1)
            pe.wait_ge(s.slots_sb, 1)
            pe.wait_ge(s.ld_w1, 16)
            pe.wait_ge(s.ld_w2, 16)

            def experts(us, t):
                es = [pe.value_load(EXPS[0:1, ds(t + u, 1)], min_val=0, max_val=E - 1) for u in us]
                W1f = W1.rearrange("p n h -> p (n h)")
                W2f = W2.rearrange("p n h -> p (n h)")
                for u in us:
                    pe.wait_ge(s.ys_sb, t + u + 1)
                    transposed(pb[u], ys[:, u, :], s.ysT_ps)
                for u in us:
                    pe.wait_ge(s.ysT_sb, t + u + 1)
                    for ci in range(CH):
                        ins = mm(pb[2 + u], ysT[:, u, ci * P:(ci + 1) * P], W1f[:, ds(es[u] * (CH * HID) + ci * HID, HID)],
                                 ci == 0, ci == CH - 1)
                    ins.then_inc(s.h_ps, 1)
                for u in us:
                    pe.wait_ge(s.gelu_sb, t + u + 1)
                    for j in range(HJ):
                        ins = pe.transpose(pb[4 + u][:, j * P:(j + 1) * P], hb[:, u, j * P:(j + 1) * P], ident[:, :])
                    ins.then_inc(s.hT_ps, 1)
                for u in us:
                    pe.wait_ge(s.hT_sb, t + u + 1)
                    for j in range(HJ):
                        ins = mm(pb[6 + u][:, 0:D], hT[:, u, j * P:(j + 1) * P], W2f[:, ds(es[u] * (HJ * D) + j * D, D)],
                                 j == 0, j == HJ - 1)
                    ins.then_inc(s.eo_ps, 1)
                pe.wait_ge(s.res_sb, t + len(us))

            with pe.Fori(0, NS // 2) as i:
                experts((0, 1), 2 * i)
            experts((0,), NS - 1)


_INS = ["x", "ctx_1024", "mask_BxS2_bf0", "g_xattn", "g_ffn",
        "L0_xattn_Wq", "L0_xattn_bq", "L0_xattn_Wk", "L0_xattn_bk", "L0_xattn_Wv", "L0_xattn_bv",
        "L0_ffn_w_gate", "L0_ffn_w_up", "L0_ffn_w_down",
        "L1_xattn_Wq", "L1_xattn_bq", "L1_xattn_Wk", "L1_xattn_bk", "L1_xattn_Wv", "L1_xattn_bv",
        "L1_xattn_Wo", "L1_xattn_bo", "L1_xattn_logit_scale", "L1_xattn_bias_table",
        "L1_ffn_w_red", "L1_ffn_wg", "L1_ffn_W1", "L1_ffn_b1", "L1_ffn_W2", "L1_ffn_b2"]


def kernel(**inputs):
    import concourse.bacc as bacc
    from concourse.bass_utils import run_bass_kernel_spmd

    nc = bacc.Bacc("TRN2", target_bir_lowering=False, num_devices=1)
    arrays, args = {}, {}
    for name in _INS:
        v = np.ascontiguousarray(inputs[name])
        arrays[f"in_{name}"] = v
        args[name] = nc.dram_tensor(f"in_{name}", v.shape, mybir.dt.from_np(v.dtype), kind="ExternalInput").ap()
    out = nc.dram_tensor("out_0", (NB, S, D), F32, kind="ExternalOutput").ap()
    flamingo_kernel(nc, args, out)
    r = run_bass_kernel_spmd(nc, [arrays], core_ids=[0])
    return r.results[0]["out_0"]
```

```python
import numpy as np

import concourse.bass as bass
from concourse import mybir
from contextlib import ExitStack

F32 = mybir.dt.float32
BF16 = mybir.dt.bfloat16
I16 = mybir.dt.int16
U16 = mybir.dt.uint16
I32 = mybir.dt.int32
U8 = mybir.dt.uint8
ALU = mybir.AluOpType
ACT = mybir.ActivationFunctionType
AX = mybir.AxisListType
ds = bass.ds

P = 128
NB, S, D = 2, 1024, 256
NT = NB * S // P
TB = S // P
KEYS = 77
CH = D // P
H, HD = 16, 16
HK = H * KEYS
HQ = 4
HQK = HQ * KEYS
NQ = H // HQ
VE = HD + 1
F = 768
FJ = F // P
BLK = 32
QB = 512
NQB = NB * S // QB
E, HID, G = 8, 512, 16
HJ = HID // P
NS = NT + E - 1
NP = NS // 2
MAXD = 128
NEAR = 2
EXT = NEAR * P + KEYS - 1
ROW = D + 4
NMR, RSTD, COEF, IDC = D, D + 1, D + 2, D + 3
EPS = 1e-5
MAGIC = 1.5 * 2.0 ** 23
QMAX = 32767.0
TINY = 1e-12
NEG = -(2.0 ** 126)
NOWHERE = 1 << 20


class Signals:

    def __init__(self, sem):
        self.ld_l0 = sem("ld_l0")
        self.ld_x = sem("ld_x")
        self.ld_x1 = sem("ld_x1")
        self.ld_ffn = sem("ld_ffn")
        self.ld_l1 = sem("ld_l1")
        self.ld_ext = sem("ld_ext")
        self.ld_near = sem("ld_near")
        self.ld_const = sem("ld_const")
        self.ld_w1 = sem("ld_w1")
        self.ld_w2 = sem("ld_w2")
        self.ld_b1 = sem("ld_b1")
        self.ld_b2 = sem("ld_b2")
        self.pads_written = sem("pads_written")
        self.ext_stored = sem("ext_stored")
        self.consts = sem("consts")
        self.pool_consts = sem("pool_consts")
        self.ctxT_ps = sem("ctxT_ps")
        self.ctxT_sb = sem("ctxT_sb")
        self.wq0T_ps = sem("wq0T_ps")
        self.wq0T_sb = sem("wq0T_sb")
        self.k0_ps = sem("k0_ps")
        self.k0_sb = sem("k0_sb")
        self.a0_ps = sem("a0_ps")
        self.a0_sb = sem("a0_sb")
        self.v0_ps = sem("v0_ps")
        self.v0_sb = sem("v0_sb")
        self.els_sb = sem("els_sb")
        self.hsc_sb = sem("hsc_sb")
        self.csc_ps = sem("csc_ps")
        self.k1_ps = sem("k1_ps")
        self.csc_sb = sem("csc_sb")
        self.k1_sb = sem("k1_sb")
        self.v1_ps = sem("v1_ps")
        self.v1_sb = sem("v1_sb")
        self.kbd_sb = sem("kbd_sb")
        self.ext_sb = sem("ext_sb")
        self.wrT_ps = sem("wrT_ps")
        self.wrT_sb = sem("wrT_sb")
        self.wss_sb = sem("wss_sb")
        self.wnorm_sb = sem("wnorm_sb")
        self.wgn_sb = sem("wgn_sb")
        self.wgT_ps = sem("wgT_ps")
        self.wgT_sb = sem("wgT_sb")
        self.gm_ps = sem("gm_ps")
        self.gm_sb = sem("gm_sb")
        self.tg_sb = sem("tg_sb")
        self.wo_sb = sem("wo_sb")
        self.wstep_sb = sem("wstep_sb")
        self.wsteps_sb = sem("wsteps_sb")
        self.wround_sb = sem("wround_sb")
        self.wq_sb = sem("wq_sb")
        self.wT_ps = sem("wT_ps")
        self.wT_sb = sem("wT_sb")
        self.mv_a = sem("mv_a")
        self.rstd_a = sem("rstd_a")
        self.keep_sb = sem("keep_sb")
        self.slots_sb = sem("slots_sb")
        self.am_u = sem("am_u")
        self.ar_u = sem("ar_u")
        self.wn_sb = sem("wn_sb")
        self.scal_u = sem("scal_u")
        self.y_a = sem("y_a")
        self.yT_ps = sem("yT_ps")
        self.yT_sb = sem("yT_sb")
        self.s0_ps = sem("s0_ps")
        self.nmax_a = sem("nmax_a")
        self.p0 = sem("p0")
        self.pT0_ps = sem("pT0_ps")
        self.pT0_sb = sem("pT0_sb")
        self.o0_ps = sem("o0_ps")
        self.mv_b = sem("mv_b")
        self.rstd_b = sem("rstd_b")
        self.y_b = sem("y_b")
        self.y2T_ps = sem("y2T_ps")
        self.y2T_sb = sem("y2T_sb")
        self.ax_sb = sem("ax_sb")
        self.ar_x = sem("ar_x")
        self.scal_x = sem("scal_x")
        self.tq_y = sem("tq_y")
        self.nq = sem("nq")
        self.gu_ps = sem("gu_ps")
        self.gu_sb = sem("gu_sb")
        self.am_g = sem("am_g")
        self.ar_g = sem("ar_g")
        self.scal_g = sem("scal_g")
        self.sig_done = sem("sig_done")
        self.z_done = sem("z_done")
        self.am_z = sem("am_z")
        self.ar_z = sem("ar_z")
        self.scal_z = sem("scal_z")
        self.nzu_done = sem("nzu_done")
        self.p_done = sem("p_done")
        self.am_p = sem("am_p")
        self.ar_p = sem("ar_p")
        self.scal_p = sem("scal_p")
        self.tq_p = sem("tq_p")
        self.no_done = sem("no_done")
        self.dn_ps = sem("dn_ps")
        self.x2_done = sem("x2_done")
        self.mv_c = sem("mv_c")
        self.rstd_c = sem("rstd_c")
        self.y_c = sem("y_c")
        self.y3T_ps = sem("y3T_ps")
        self.y3T_sb = sem("y3T_sb")
        self.bo_added = sem("bo_added")
        self.near_sb = sem("near_sb")
        self.const_sb = sem("const_sb")
        self.q_ps = sem("q_ps")
        self.q_sb = sem("q_sb")
        self.s_ps = sem("s_ps")
        self.e_sub = sem("e_sub")
        self.e_exp = sem("e_exp")
        self.pT_ps = sem("pT_ps")
        self.pT_sb = sem("pT_sb")
        self.o_ps = sem("o_ps")
        self.att_sb = sem("att_sb")
        self.attT_ps = sem("attT_ps")
        self.attT_sb = sem("attT_sb")
        self.wo_ps = sem("wo_ps")
        self.x3_done = sem("x3_done")
        self.mv_d = sem("mv_d")
        self.rstd_d = sem("rstd_d")
        self.y_d = sem("y_d")
        self.y4T_ps = sem("y4T_ps")
        self.y4T_sb = sem("y4T_sb")
        self.lg_ps = sem("lg_ps")
        self.lx_sb = sem("lx_sb")
        self.ex_sb = sem("ex_sb")
        self.oh_sb = sem("oh_sb")
        self.cnt_ps = sem("cnt_ps")
        self.pos_sb = sem("pos_sb")
        self.scattered = sem("scattered")
        self.rows_in = sem("rows_in")
        self.more_rows_in = sem("more_rows_in")
        self.ys_sb = sem("ys_sb")
        self.ysT_ps = sem("ysT_ps")
        self.ysT_sb = sem("ysT_sb")
        self.h_ps = sem("h_ps")
        self.hb_sb = sem("hb_sb")
        self.gelu_sb = sem("gelu_sb")
        self.hT_ps = sem("hT_ps")
        self.hT_sb = sem("hT_sb")
        self.eo_ps = sem("eo_ps")
        self.res_sb = sem("res_sb")
        self.rows_out0 = sem("rows_out0")
        self.rows_out1 = sem("rows_out1")
        self.dve_step = sem("dve_step")
        self.act_step = sem("act_step")
        self.pool_step = sem("pool_step")
        self.dve_past = sem("dve_past")
        self.pool_past = sem("pool_past")


class Chain:

    def __init__(self, eng, sem):
        self.eng, self.sem, self.base, self.n = eng, sem, 0, 0

    def mark(self, ins):
        self.n += 1
        ins.then_inc(self.sem, 1)
        return self.base + self.n

    def link(self, ins):
        self.eng.wait_ge(self.sem, self.mark(ins))

    def enter(self, i, per):
        self.done, self.per = self.base + self.n, per
        self.base, self.n = self.done + i * per, 0

    def leave(self, times):
        assert self.n == self.per, (self.n, self.per)
        self.base, self.n = self.done + times * self.per, 0


def flamingo_kernel(nc, a, out):
    ctx = ExitStack()
    with ctx:
        def sb(name, shape, dt=F32):
            return ctx.enter_context(nc.sbuf_tensor(name, shape, dt))

        def sem(name):
            return ctx.enter_context(nc.semaphore(name))

        bank = [ctx.enter_context(nc.psum_tensor(f"bank{i}", [P, 512], F32)) for i in range(8)]
        pb = [b[:, :] for b in bank]

        rows_d = nc.dram_tensor("sorted_rows", [NS * P, ROW], F32).ap()
        ext_d = nc.dram_tensor("bias_by_distance", [H, EXT], F32).ap()

        X = sb("x_rows", [P, NT, ROW])
        XI = X[:, :, :].bitcast(I32)
        YT = sb("yT", [P, CH, NB * S])
        BIGG = sb("big_g", [P, FJ * NB * S])
        BIGU = sb("big_u", [P, FJ * NB * S])
        TMP = sb("tmp", [P, 6144])
        FW = sb("ffn_w", [P, 4608])
        GT = BIGG[:, :].rearrange("p (j n) -> p j n", j=FJ)
        UT_ = BIGU[:, :].rearrange("p (j n) -> p j n", j=FJ)

        def part(reg, off, shape, dt=F32):
            n = int(np.prod(shape[1:]))
            words = n if dt in (F32, I32) else n // 2
            v = reg[0:shape[0], off:off + words]
            if dt != F32:
                v = v.bitcast(dt)
            if len(shape) == 3:
                v = v.rearrange("p (a b) -> p a b", a=shape[1])
            if len(shape) == 4:
                v = v.rearrange("p (a b c) -> p a b c", a=shape[1], b=shape[2])
            return v

        ident = sb("ident", [P, P])
        flipb = sb("flipb", [P, P], BF16)
        ones = sb("ones", [P, P])
        onesb = sb("onesb", [P, P], BF16)
        before = sb("before", [P, P], BF16)
        headof = sb("headof", [P, 8])
        expand = part(BIGU, 10880, [H, D])
        mhalf = sb("mhalf", [P, NT])
        half = sb("half", [E, 1])
        warm = sb("warm", [1, 1])
        ids = sb("ids", [P, NT], I32)
        slot_i = part(BIGG, 4608, [P, NS, E - 1], I32)
        slot = sb("slot", [P, NS, E - 1])
        rank_i = part(BIGG, 4800, [P, E], I32)
        rank = sb("rank", [P, E])
        gates = sb("gates", [P, 4])
        tg = sb("tg", [P, 4])

        CTX = part(BIGU, 8192, [KEYS, NB, D])
        WK0 = part(BIGU, 0, [P, CH, D])
        WQ0 = part(BIGU, 512, [P, CH, D])
        WV0 = part(BIGU, 1024, [P, CH, D])
        bq0 = sb("bq0", [P, CH])
        bk0 = sb("bk0", [P, CH])
        bv0 = part(BIGU, 8704, [1, D])
        CTXT = part(BIGU, 8960, [P, CH, NB * KEYS])
        WQ0T = part(BIGU, 1536, [P, CH, D])
        K0T = part(BIGU, 2048, [P, CH, NB * KEYS])
        A0 = sb("a0", [P, CH, NB * KEYS])
        R0 = sb("r0", [1, NB * KEYS])
        V0 = sb("v0", [KEYS, NB, D])
        ya = part(BIGU, 3072, [P, 4, D])
        y2a = part(BIGU, 4096, [P, 4, D])
        yTa = part(BIGU, 5120, [P, 4, D])
        pa = part(BIGU, 6144, [P, 4, KEYS])
        pTa = part(BIGU, 6528, [KEYS, 4, P])
        stat = sb("stat", [P, 4, 6])
        mv = sb("mv", [P, 4, 2])
        ve = sb("ve", [P, 4])
        rstd = sb("rstd", [P, 4])
        nmax = sb("nmax", [P, 4])
        den = sb("den", [P, 4])
        rden = sb("rden", [P, 4])

        WN = part(BIGG, 0, [P, 18 * 8, BLK])
        WUT = part(FW, 0, [P, CH, F])
        WGT = part(FW, CH * F, [P, CH, F])
        WDT = part(FW, 2 * CH * F, [P, FJ, D])
        WNI = part(BIGG, 8192, [P, 48, BLK])
        wamax = sb("wamax", [P, 144])
        wscale = sb("wscale", [P, 144])
        wrec = sb("wrec", [P, 144])
        amY = sb("amY", [P, NT])
        amG = sb("amG", [P, NQB * FJ])
        amU = sb("amU", [P, NQB * FJ])
        amZ = sb("amZ", [P, 2 * NQB])
        amP = sb("amP", [P, 2 * NQB])
        sc = sb("scalars", [P, 32])
        HF = 3 * QB
        ng = part(TMP, 0, [P, 2, HF], I16)
        u16 = part(TMP, HF, [P, 2, HF], U16)
        sig = part(TMP, 2 * HF, [P, 2, HF])
        nz = part(TMP, 0, [P, 2, HF], I16)
        nu = part(TMP, HF, [P, 2, HF], I16)
        y3 = part(TMP, 0, [P, 4, D])

        WK1 = part(BIGU, 9280, [P, CH, D])
        WV1 = part(BIGU, 9792, [P, CH, D])
        WQ1 = sb("wq1", [P, CH, D])
        WO1 = sb("wo1", [P, CH, D])
        bq1 = sb("bq1", [P, CH])
        bk1 = sb("bk1", [P, CH])
        bv1 = part(BIGU, 10304, [1, D])
        bo1 = sb("bo1", [P, D])
        ls = sb("ls", [H, 1])
        els = sb("els", [H, 1])
        hscale = sb("hscale", [H, 1])
        cscale = sb("cscale", [P, CH])
        keep8 = sb("keep8", [P, NB * KEYS], U8)
        keep = part(BIGU, 10560, [P, NB * KEYS])
        K1T = sb("k1T", [P, CH, NB * KEYS])
        KBD = sb("k_blockdiag", [P, NB * CH * 8, KEYS])
        V1 = sb("v1", [KEYS, NB * H, VE])
        mrow8 = sb("mrow8", [1, NB * KEYS], U8)
        mrow = part(BIGU, 10720, [1, NB * KEYS])
        CM = sb("const_rows", [4, NB, HK], BF16)
        tab0 = sb("tab0", [1, H])
        tabT = part(BIGU, 7168, [H, 2 * MAXD + 1])
        ext = part(BIGU, 7680, [H, EXT])
        far3 = part(TMP, 0, [1, 3, HK], BF16)
        mask16 = part(TMP, 1856, [1, NB, HK], BF16)
        BN = part(TMP, 1024, [P, NEAR * 3, HK], BF16)
        bstage = part(TMP, 4736, [P, HK])

        e_ = part(BIGG, 8192, [P, 2, HK])
        qT = part(BIGG, 10752, [P, CH, 2 * P])
        att = part(BIGG, 11264, [P, 2, D])
        attT = part(BIGG, 11776, [P, 2, D])
        pT = part(BIGU, 8192, [KEYS, 2, H * P])
        rd = sb("rd", [P, 2, H])
        mx = sb("mx", [P, 2, HQ])

        WR = part(BIGU, 11136, [P, CH, G])
        WRT = part(BIGU, 11168, [G, D])
        wg = sb("wg", [E, G])
        wg2 = sb("wg2", [E, G])
        wgn = sb("wgn", [E, G])
        wss = sb("wss", [E, 3])
        WGNT = sb("wgnT", [G, E])
        GM = sb("gm", [P, CH, E])
        W1 = part(BIGG, 0, [P, E * CH, HID])
        W2 = part(BIGU, 0, [P, E * HJ, D])
        B1 = part(FW, 0, [P, E * HID])
        B2 = part(TMP, 0, [P, E * D])
        y4 = part(BIGG, 8192, [P, 4, D])
        y4T = part(BIGG, 9216, [P, 4, D])
        LG = part(BIGU, 8192, [P, NT, E])
        LX = part(BIGU, 8320, [P, NT, E])
        LM = sb("lm", [P, NT])
        OH = part(BIGU, 8448, [P, NT, E])
        OHB = sb("onehotb", [P, NT, E], BF16)
        TOT = part(BIGU, 8576, [P, NT, E])
        CUM = part(BIGU, 8704, [P, NT + 1, E])
        cnt_i = sb("cnt_i", [P, E], I32)
        tiles_e = sb("tiles_e", [P, E])
        start_e = sb("start_e", [P, E])
        start128 = sb("start128", [P, E])
        pos_i = sb("pos_i", [P, NT], I32)
        rid = sb("row_ids", [P, 2], I32)
        mv4 = sb("mv4", [P, NT, 2])
        ve4 = sb("ve4", [P, NT])
        rstd4 = sb("rstd4", [P, NT])
        eslot = sb("eslot", [P, NS])
        EXPS = sb("exp_of_slot", [P, NS], I32)
        YW = YT[:, :, :].rearrange("p a b -> p (a b)")
        rb = [part(BIGG, 8192, [P, NP + 1, ROW]), part(BIGU, 8192, [P, NP, ROW])]
        ys = part(YW, 0, [P, 2, D])
        ysT = part(YW, 512, [P, 2, D])
        hb = part(YW, 1024, [P, 2, HID])
        hT = part(YW, 2048, [P, 2, HID])
        res = part(YW, 3072, [P, 2, D])
        ob = part(YW, 3584, [P, 2, D])
        pad = part(BIGG, 4864, [P, ROW])

        NPB = TB // 2
        FAR = NPB - NEAR // 2

        def position(t):
            return t // TB * TB + (t - NEAR) % TB

        s = Signals(sem)
        block = ctx.enter_context(nc.Block())

        @block.sync
        def _(sp):
            def chunks(w):
                return w.rearrange("(c p) n -> p c n", p=P)

            def column(v):
                return v.rearrange("(c p) -> p c", p=P)

            def row(v):
                return v.rearrange("(a n) -> a n", a=1)

            sp.dma_start(CTX, a["ctx_1024"].rearrange("b k d -> k b d")).then_inc(s.ld_l0, 16)
            sp.dma_start(WK0, chunks(a["L0_xattn_Wk"])).then_inc(s.ld_l0, 16)
            sp.dma_start(WQ0, chunks(a["L0_xattn_Wq"])).then_inc(s.ld_l0, 16)
            sp.dma_start(WV0, chunks(a["L0_xattn_Wv"])).then_inc(s.ld_l0, 16)
            sp.dma_start(bk0[:, :], column(a["L0_xattn_bk"]), allow_slow_non_contiguous=True).then_inc(s.ld_l0, 16)
            sp.dma_start(bq0[:, :], column(a["L0_xattn_bq"]), allow_slow_non_contiguous=True).then_inc(s.ld_l0, 16)
            sp.dma_start(bv0, row(a["L0_xattn_bv"])).then_inc(s.ld_l0, 16)
            for n, g in enumerate(("g_xattn", "g_ffn")):
                sp.dma_start(gates[:, 2 * n:2 * n + 2], row(a[g]).to_broadcast([P, 2])).then_inc(s.ld_l0, 16)
            for b in range(NB):
                sp.dma_start(X[:, b * TB:(b + 1) * TB, 0:D],
                             a["x"][b].rearrange("(t p) d -> p t d", p=P)).then_inc((s.ld_x, s.ld_x1)[b], 16)
            for n, w in enumerate(("L0_ffn_w_gate", "L0_ffn_w_up")):
                sp.dma_start(WN[:, n * 48:(n + 1) * 48, :].rearrange("p (j q) k -> p j (q k)", j=FJ),
                             a[w].rearrange("(j p) c -> p j c", p=P)).then_inc(s.ld_ffn, 16)
            sp.dma_start(WN[:, 96:144, :].rearrange("p (j q) k -> p j (q k)", j=CH),
                         a["L0_ffn_w_down"].rearrange("(j p) c -> p j c", p=P)).then_inc(s.ld_ffn, 16)
            sp.dma_start(WK1, chunks(a["L1_xattn_Wk"])).then_inc(s.ld_l1, 16)
            sp.dma_start(WV1, chunks(a["L1_xattn_Wv"])).then_inc(s.ld_l1, 16)
            sp.dma_start(WQ1[:, :, :], chunks(a["L1_xattn_Wq"])).then_inc(s.ld_l1, 16)
            sp.dma_start(WO1[:, :, :], chunks(a["L1_xattn_Wo"])).then_inc(s.ld_l1, 16)
            sp.dma_start(bq1[:, :], column(a["L1_xattn_bq"]), allow_slow_non_contiguous=True).then_inc(s.ld_l1, 16)
            sp.dma_start(bk1[:, :], column(a["L1_xattn_bk"]), allow_slow_non_contiguous=True).then_inc(s.ld_l1, 16)
            sp.dma_start(bv1, row(a["L1_xattn_bv"])).then_inc(s.ld_l1, 16)
            sp.dma_start(bo1[:, :], row(a["L1_xattn_bo"]).to_broadcast([P, D])).then_inc(s.ld_l1, 16)
            sp.dma_start(ls[:, :], a["L1_xattn_logit_scale"].rearrange("(h a) -> h a", a=1)).then_inc(s.ld_l1, 16)
            mask = a["mask_BxS2_bf0"].rearrange("b k -> (b k)").rearrange("(a n) -> a n", a=1)
            sp.dma_start(keep8[:, :], mask.to_broadcast([P, NB * KEYS])).then_inc(s.ld_l1, 16)
            sp.dma_start(mrow8[:, :], mask).then_inc(s.ld_l1, 16)
            sp.dma_start(WR, chunks(a["L1_ffn_w_red"])).then_inc(s.ld_l1, 16)
            sp.dma_start(wg[:, :], a["L1_ffn_wg"]).then_inc(s.ld_l1, 16)
            sp.dma_start(tab0[:, :], a["L1_xattn_bias_table"][0:1, :]).then_inc(s.ld_l1, 16)
            sp.dma_start(tabT, a["L1_xattn_bias_table"].rearrange("r h -> h r"), allow_slow_non_contiguous=True).then_inc(s.ld_ext, 16)
            sp.wait_ge(s.pool_consts, 1)
            sp.dma_start(rows_d.rearrange("(t p) c -> p t c", p=P),
                         pad.unsqueeze(1).to_broadcast([P, NS, ROW])).then_inc(s.pads_written, 16)
            sp.wait_ge(s.ext_sb, 1)
            sp.dma_start(ext_d, ext).then_inc(s.ext_stored, 16)
            sp.wait_ge(s.const_sb, 1)
            sp.dma_start(CM[0:1, :, :], mask16).then_inc(s.ld_const, 16)
            for b in range(NB):
                for k in range(3):
                    sp.dma_start(CM[k + 1:k + 2, b, :], far3[:, k, :]).then_inc(s.ld_const, 16)
            sp.wait_ge(s.ext_stored, 16)
            sp.wait_ge(s.p_done, 2 + 2 * NQB)
            for n in range(NEAR):
                if n:
                    sp.wait_ge(s.near_sb, n)
                sp.dma_start(bstage.rearrange("p (h k) -> p h k", h=H),
                             bass.AP(tensor=ext_d.tensor, offset=EXT - KEYS - n * P - (P - 1),
                                     ap=[[1, P], [EXT, H], [1, KEYS]])).then_inc(s.ld_near, 16)
            sp.wait_ge(s.dn_ps, NT)
            sp.dma_start(W1.rearrange("p (e c) h -> p e c h", e=E),
                         a["L1_ffn_W1"].rearrange("e (c p) h -> p e c h", p=P)).then_inc(s.ld_w1, 16)
            sp.dma_start(W2.rearrange("p (e c) h -> p e c h", e=E),
                         a["L1_ffn_W2"].rearrange("e (c p) h -> p e c h", p=P)).then_inc(s.ld_w2, 16)
            sp.dma_start(B1, row(a["L1_ffn_b1"].rearrange("e h -> (e h)")).to_broadcast([P, E * HID])).then_inc(s.ld_b1, 16)
            sp.wait_ge(s.x3_done, NT)
            sp.dma_start(B2, row(a["L1_ffn_b2"].rearrange("e h -> (e h)")).to_broadcast([P, E * D])).then_inc(s.ld_b2, 16)
            sp.wait_ge(s.scattered, 16 * NT)
            rows_t = rows_d.rearrange("(t p) c -> p t c", p=P)
            for u in range(2):
                sp.dma_start(rb[u][:, 0, :], rows_t[:, u, :]).then_inc(s.rows_in, 16)
            for u in range(2):
                sp.dma_start(rb[u][:, 1:, :], rows_t[:, 2 + u::2, :]).then_inc(s.more_rows_in, 16)

        @block.gpsimd
        def _(pool):
            c = Chain(pool, s.pool_step)
            c.link(pool.memset(ident[:, :], 0.0))
            c.link(pool.memset(ones[:, :], 1.0))
            c.link(pool.affine_select(out=ident[:, :], in_=ident[:, :], compare_op=ALU.not_equal, fill=1.0,
                                      base=0, pattern=[[-1, P]], channel_multiplier=1))
            pool.tensor_copy(onesb[:, :], ones[:, :])
            c.link(pool.memset(flipb[:, :], 0.0))
            c.link(pool.affine_select(out=flipb[:, :], in_=flipb[:, :], compare_op=ALU.not_equal, fill=1.0,
                                      base=-(P - 1), pattern=[[1, P]], channel_multiplier=1))
            pool.memset(half[:, :], 0.5)
            pool.memset(warm[:, :], 0.0)
            pool.memset(mhalf[:, :], -0.5).then_inc(s.consts, 1)
            c.link(pool.affine_select(out=headof[:, :], in_=ones[:, 0:8], compare_op=ALU.is_ge, fill=0.0,
                                      base=0, pattern=[[-HD, 8]], channel_multiplier=1))
            c.link(pool.affine_select(out=headof[:, :], in_=headof[:, :], compare_op=ALU.is_ge, fill=0.0,
                                      base=HD - 1, pattern=[[HD, 8]], channel_multiplier=-1))
            c.link(pool.memset(expand, 1.0))
            c.link(pool.affine_select(out=expand, in_=expand, compare_op=ALU.is_ge, fill=0.0,
                                      base=0, pattern=[[1, D]], channel_multiplier=-HD))
            c.link(pool.affine_select(out=expand, in_=expand, compare_op=ALU.is_ge, fill=0.0,
                                      base=HD - 1, pattern=[[-1, D]], channel_multiplier=HD))
            c.link(pool.affine_select(out=before[:, :], in_=onesb[:, :], compare_op=ALU.is_gt, fill=0.0,
                                      base=0, pattern=[[1, P]], channel_multiplier=-1))
            c.link(pool.iota(ids[:, :], pattern=[[P, NT]], base=0, channel_multiplier=1))
            c.link(pool.iota(slot_i, pattern=[[1, NS], [0, E - 1]], base=0, channel_multiplier=0))
            c.link(pool.iota(rank_i, pattern=[[-1, E]], base=E, channel_multiplier=0))
            pool.tensor_copy(slot[:, :, :], slot_i)
            pool.tensor_copy(rank[:, :], rank_i)
            c.link(pool.memset(pad, 0.0))
            pool.iota(pad[:, IDC:IDC + 1].bitcast(I32), pattern=[[0, 1]], base=NOWHERE,
                      channel_multiplier=0).then_inc(s.pool_consts, 1)
            def rstds(t, mv_ready, done, per):
                pool.wait_ge(mv_ready, t + 4)
                pool.sem_inc(s.pool_past, 1)
                c.link(pool.tensor_scalar(ve[:, :], mv[:, :, 1], EPS, None, ALU.add))
                pool.tensor_tensor(rstd[:, :], ve[:, :], mhalf[:, 0:4], ALU.pow).then_inc(done, 1)

            def rstds_all(ready, done):
                pool.wait_ge(ready, NT)
                c.link(pool.tensor_scalar(ve4[:, :], mv4[:, :, 1], EPS, None, ALU.add))
                pool.tensor_tensor(rstd4[:, :], ve4[:, :], mhalf[:, :], ALU.pow).then_inc(done, 1)

            def quantised(n, part_):
                b = slice(48 * n, 48 * (n + 1))
                if part_ == 0:
                    if n:
                        pool.wait_ge(s.wq_sb, n)
                    pool.tensor_tensor(WNI, WN[:, b, :], wrec[:, b].unsqueeze(2).to_broadcast([P, 48, BLK]),
                                       ALU.mult).then_inc(s.wsteps_sb, 1)
                else:
                    pool.wait_ge(s.wround_sb, n + 1)
                    (pool.tensor_tensor(WN[:, b, :], WNI, wscale[:, b].unsqueeze(2).to_broadcast([P, 48, BLK]),
                                              ALU.mult)).then_inc(s.wq_sb, 1)

            rstds_all(s.mv_a, s.rstd_a)
            pool.wait_ge(s.wstep_sb, 1)
            quantised(0, 0)
            quantised(0, 1)
            for g in range(NT // 4):
                rstds(4 * g, s.mv_b, s.rstd_b, 2)
                quantised(1 + g // 2, g % 2)
            pool.wait_ge(s.ld_l1, 16 * 14)
            pool.tensor_scalar(keep, keep8[:, :], -1.0, 1.0, ALU.mult, ALU.add).then_inc(s.keep_sb, 1)
            pool.wait_ge(s.wss_sb, 1)
            pool.tensor_tensor(wss[:, 1:2], wss[:, 0:1], half[:, :], ALU.pow).then_inc(s.wnorm_sb, 1)

            def all_max(k, ready, done):
                pool.wait_ge(ready, 1)
                pool.partition_all_reduce(sc[:, k + 1:k + 2], sc[:, k:k + 1], P,
                                          bass.bass_isa.ReduceOp.max).then_inc(done, 1)

            all_max(0, s.ax_sb, s.ar_x)
            c.link(pool.tensor_scalar(mrow, mrow8[:, :], NEG, None, ALU.mult))
            mrow3 = mrow.rearrange("p (b k) -> p b k", b=NB)
            for b in range(NB):
                pool.tensor_copy(mask16[:, b, :].rearrange("p (h k) -> p h k", h=H),
                                 mrow3[:, b, :].unsqueeze(1).to_broadcast([1, H, KEYS]))
            for k in range(3):
                f3 = far3[:, k, :].rearrange("p (h k) -> p h k", h=H)
                ins = pool.tensor_copy(f3, tab0[:, :].unsqueeze(2).to_broadcast([1, H, KEYS]))
                if k < 2:
                    c.link(ins)
                    c.link(pool.tensor_tensor(tab0[:, :], tab0[:, :], f3[:, :, 0], ALU.subtract))
            ins.then_inc(s.const_sb, 1)
            pool.wait_ge(s.ld_ext, 16)
            c.link(pool.tensor_copy(ext[:, 0:MAXD - 1], tabT[:, 0:1].to_broadcast([H, MAXD - 1])))
            pool.tensor_copy(ext[:, MAXD - 1:EXT], tabT[:, 0:EXT - MAXD + 1]).then_inc(s.ext_sb, 1)
            pool.wait_ge(s.k1_sb, 1)
            K1B = K1T[:, :, :].rearrange("p c (b k) -> p c b k", b=NB)
            for b in range(NB):
                for ci in range(CH):
                    n = (b * CH + ci) * 8
                    last = pool.tensor_tensor(KBD[:, n:n + 8, :],
                                              K1B[:, ci, b, :].unsqueeze(1).to_broadcast([P, 8, KEYS]),
                                              headof[:, :].unsqueeze(2).to_broadcast([P, 8, KEYS]), ALU.mult)
            last.then_inc(s.kbd_sb, 1)
            all_max(2, s.am_g, s.ar_g)
            all_max(4, s.am_z, s.ar_z)
            all_max(6, s.am_u, s.ar_u)
            all_max(8, s.am_p, s.ar_p)
            with pool.Fori(0, NT // 4) as i:
                c.enter(i, 1)
                rstds(4 * i, s.mv_c, s.rstd_c, 1)
            c.leave(NT // 4)
            pool.wait_ge(s.wo_sb, 1)
            pool.wait_ge(s.y_c, NT)
            pool.tensor_tensor(X[:, :, 0:D], X[:, :, 0:D], bo1[:, :].unsqueeze(1).to_broadcast([P, NT, D]),
                               ALU.add).then_inc(s.bo_added, 1)
            for n in range(NEAR):
                pool.wait_ge(s.ld_near, 16 * (n + 1))
                for k in range(3):
                    ins = pool.tensor_copy(BN[:, 3 * n + k, :], bstage)
                    if k < 2:
                        c.link(ins)
                        c.link(pool.tensor_tensor(bstage, bstage, BN[:, 3 * n + k, :], ALU.subtract))
                ins.then_inc(s.near_sb, 1)
            rstds_all(s.mv_d, s.rstd_d)
            pool.wait_ge(s.pads_written, 16)
            pool.wait_ge(s.pos_sb, 1)
            for t in range(NT):
                pool.indirect_dma_start(rows_d, bass.IndirectOffsetOnAxis(pos_i[:, t:t + 1], 0),
                                        X[:, t, :], None).then_inc(s.scattered, 16)

            def rows_out(u, t):
                pool.wait_ge(s.res_sb, 2 + t + 1)
                pool.sem_inc(s.pool_past, 1)
                pool.indirect_dma_start(out.rearrange("b s d -> (b s) d"),
                                        bass.IndirectOffsetOnAxis(rid[:, u:u + 1], 0),
                                        res[:, u, :], None, bounds_check=NB * S - 1,
                                        oob_is_err=False).then_inc(s.rows_out0 if u == 0 else s.rows_out1, 16)

            with pool.Fori(0, NS // 2) as i:
                rows_out(0, 2 * i)
                rows_out(1, 2 * i + 1)
            rows_out(0, NS - 1)
            pool.wait_ge(s.rows_out0, 16 * (NS // 2 + 1))
            pool.wait_ge(s.rows_out1, 16 * (NS // 2))

        @block.scalar
        def _(act):
            c = Chain(act, s.act_step)

            def copy(out_, in_, ready, n, done, **k):
                act.wait_ge(ready, n)
                act.activation(out_, in_, ACT.Copy, **k).then_inc(done, 1)

            act.wait_ge(s.consts, 1)
            act.wait_ge(s.ld_l0, 16 * 9)
            act.activation(tg[:, :], gates[:, :], ACT.Tanh).then_inc(s.tg_sb, 1)
            act.wait_ge(s.tg_sb, 1)
            copy(CTXT, pb[0][:, 0:2 * NB * KEYS].rearrange("p (c n) -> p c n", c=CH), s.ctxT_ps, 1, s.ctxT_sb)
            copy(WQ0T, pb[1].rearrange("p (c n) -> p c n", c=CH), s.wq0T_ps, 1, s.wq0T_sb)
            copy(A0[:, :, :], pb[3][:, 0:2 * NB * KEYS].rearrange("p (c n) -> p c n", c=CH), s.a0_ps, 1, s.a0_sb)
            copy(R0[:, :], pb[3][0:1, 320:320 + NB * KEYS], s.a0_ps, 1, s.a0_sb)
            copy(V0[:, :, :], pb[4][0:KEYS, :].rearrange("p (b n) -> p b n", b=NB), s.v0_ps, 1, s.v0_sb,
                 scale=tg[0:KEYS, 0:1])
            def yT_out(g):
                for u in range(4):
                    copy(yTa[:, u, :], pb[u][:, 0:D], s.yT_ps, 4 * g + u + 1, s.yT_sb)

            def y2T_out(g):
                for u in range(4):
                    t = 4 * g + u
                    copy(YT[:, :, t * P:(t + 1) * P], pb[u][:, 0:D].rearrange("p (c n) -> p c n", c=CH),
                         s.y2T_ps, t + 1, s.y2T_sb)
            def rounded(n):
                act.wait_ge(s.wsteps_sb, n + 1)
                c.link(act.activation(WNI, WNI, ACT.Copy, bias=MAGIC))
                act.activation(WNI, WNI, ACT.Copy, bias=-MAGIC).then_inc(s.wround_sb, 1)
            yT_out(0)
            rounded(0)
            for g in range(NT // 4):
                for u in range(4):
                    act.wait_ge(s.nmax_a, 4 * g + u + 1)
                    act.activation(pa[:, u, :], pb[4 + u][:, 0:KEYS], ACT.Exp, bias=nmax[:, u:u + 1],
                                   accum_out=den[:, u:u + 1]).then_inc(s.p0, 1)
                if g:
                    y2T_out(g - 1)
                for u in range(4):
                    copy(pTa[:, u, :], pb[u][0:KEYS, 0:P], s.pT0_ps, 4 * g + u + 1, s.pT0_sb)
                if g < NT // 4 - 1:
                    yT_out(g + 1)
                if g % 2:
                    rounded(1 + g // 2)
            y2T_out(NT // 4 - 1)
            act.wait_ge(s.ld_l1, 16 * 14)
            act.activation(els[:, :], ls[:, :], ACT.Exp).then_inc(s.els_sb, 1)
            copy(V1[:, :, 0:HD], pb[7][0:KEYS, :].rearrange("p (n d) -> p n d", d=HD), s.v1_ps, 1, s.v1_sb)
            copy(WRT, pb[0][0:G, 0:D], s.wrT_ps, 1, s.wrT_sb)
            copy(WGNT[:, :], pb[0][0:G, D:D + E], s.wgT_ps, 1, s.wgT_sb)
            copy(GM[:, :, :], pb[1][:, 0:CH * E].rearrange("p (c e) -> p c e", c=CH), s.gm_ps, 1, s.gm_sb)
            for g in range(9):
                copy(FW[:, g * 512:(g + 1) * 512], pb[g % 8], s.wT_ps, g + 1, s.wT_sb)
            for q in range(NQB):
                copy(YT[:, :, q * QB:(q + 1) * QB], YT[:, :, q * QB:(q + 1) * QB], s.tq_y, q + 1, s.nq, bias=-MAGIC)
            act.sem_inc(s.gu_sb, FJ)
            act.wait_ge(s.pads_written, 16)
            with act.Fori(0, NQB) as q:
                for j in range(FJ):
                    copy(GT[:, j, ds(q * QB, QB)], pb[j], s.gu_ps, FJ * q + j + 1, s.gu_sb)
            act.activation(warm[:, :], warm[:, :], ACT.Sigmoid)
            act.wait_ge(s.ld_const, 16 * 7)
            act.wait_ge(s.ext_stored, 16)
            act.wait_ge(s.scal_g, 1)
            with act.Fori(0, NQB) as q:
                c.enter(q, 2)
                for h in range(2):
                    for j in range(3 * h, 3 * h + 3):
                        copy(UT_[:, j, ds(q * QB, QB)], pb[j], s.gu_ps, FJ * (NQB + q) + j + 1, s.gu_sb)
                    act.wait_ge(s.z_done, 2 * q + h + 1)
                    n3 = ng[:, h, :].rearrange("p (j n) -> p j n", j=3)
                    c.link(act.activation(n3, GT[:, 3 * h:3 * h + 3, ds(q * QB, QB)], ACT.Copy,
                                          scale=sc[:, 13:14]))
                    act.activation(sig[:, h, :], ng[:, h, :], ACT.Sigmoid, scale=sc[:, 12:13]).then_inc(s.sig_done, 1)
            c.leave(NQB)
            act.wait_ge(s.scal_u, 1)
            with act.Fori(0, NQB) as q:
                for h in range(2):
                    act.wait_ge(s.p_done, 2 * q + h + 1)
                    act.activation(nz[:, h, :].rearrange("p (j n) -> p j n", j=3),
                                   GT[:, 3 * h:3 * h + 3, ds(q * QB, QB)], ACT.Copy, scale=sc[:, 15:16])
                    act.activation(nu[:, h, :].rearrange("p (j n) -> p j n", j=3),
                                   UT_[:, 3 * h:3 * h + 3, ds(q * QB, QB)], ACT.Copy,
                                   scale=sc[:, 17:18]).then_inc(s.nzu_done, 1)

            def ints(q):
                copy(UT_[:, :, ds(q * QB, QB)], GT[:, :, ds(q * QB, QB)], s.tq_p, q + 1, s.no_done, bias=-MAGIC)

            def y3_out(q):
                for u in range(4):
                    o = position(4 * q + u) * P
                    copy(YT[:, :, o:o + P], pb[4 + u][:, 0:D].rearrange("p (c n) -> p c n", c=CH),
                         s.y3T_ps, 4 + 4 * q + u + 1, s.y3T_sb)
            ints(0)
            ints(1)
            for q in range(NQB):
                y3_out(q)
                if q < 2:
                    ints(q + 2)

            def queries(t):
                act.wait_ge(s.q_ps, t + 2)
                for ci in range(CH):
                    ins = act.activation(qT[:, ci, :], pb[4][:, ci * 2 * P:(ci + 1) * 2 * P], ACT.Identity,
                                         bias=bq1[:, ci:ci + 1])
                ins.then_inc(s.q_sb, 2)

            def weightsT(t, m):
                copy(pT[:, m // NQ, (m % NQ) * 512:(m % NQ + 1) * 512], pb[6 + m % 2][0:KEYS, :],
                     s.pT_ps, NQ * t + m + 1, s.pT_sb)

            def pair(t, first=False, last=False):
                for k in range(2 * NQ):
                    if k >= 2:
                        weightsT(t, k - 2)
                    elif not first:
                        weightsT(t - 2, k + 6)
                    if k == 7 and not last:
                        queries(t + 2)
                    e4 = e_[:, k // NQ, (k % NQ) * HQK:(k % NQ + 1) * HQK]
                    act.wait_ge(s.e_sub, NQ * t + k + 1)
                    act.activation(e4, e4, ACT.Exp).then_inc(s.e_exp, 1)
                    if k == 3 and not first:
                        copy(attT[:, 1, :], pb[5][:, 0:D], s.attT_ps, t, s.attT_sb)
                    if k == 7:
                        copy(attT[:, 0, :], pb[5][:, 0:D], s.attT_ps, t + 1, s.attT_sb)

            queries(0)
            for b in range(NB):
                pair(b * TB, first=b == 0)
                with act.Fori(1, FAR) as i:
                    pair(b * TB + 2 * i)
                pair(b * TB + 2 * FAR, last=b == NB - 1)
            for k in range(2):
                weightsT(NT - 2, k + 6)
            copy(attT[:, 1, :], pb[5][:, 0:D], s.attT_ps, NT, s.attT_sb)
            with act.Fori(0, NT // 4) as i:
                for u in range(4):
                    copy(y4T[:, u, :], pb[u][:, 0:D], s.y4T_ps, 4 + 4 * i + u + 1, s.y4T_sb)
            act.wait_ge(s.lx_sb, 1)
            act.activation(LX, LX, ACT.Exp).then_inc(s.ex_sb, 1)

            def normalised(u, i):
                row = rb[u][:, ds(i, 1), :].rearrange("p a c -> p (a c)")
                act.activation(ys[:, u, :], row[:, 0:D], ACT.Identity, scale=row[:, RSTD:RSTD + 1],
                               bias=row[:, NMR:NMR + 1]).then_inc(s.ys_sb, 1)

            def transposed(u, i):
                copy(ysT[:, u, :], pb[u][:, 0:D], s.ysT_ps, 2 * i + u + 1, s.ysT_sb)

            def gelu(u, i):
                act.wait_ge(s.hb_sb, 2 * i + u + 1)
                act.activation(hb[:, u, :], hb[:, u, :], ACT.Gelu).then_inc(s.gelu_sb, 1)

            act.activation(warm[:, :], warm[:, :], ACT.Gelu)
            act.wait_ge(s.rows_in, 16 * 2)
            for u in range(2):
                normalised(u, 0)
            for u in range(2):
                transposed(u, 0)
            act.wait_ge(s.more_rows_in, 16 * 2)
            for u in range(2):
                normalised(u, 1)

            def step(i, now, nxt, nxt2):
                gelu(0, i)
                for u in nxt:
                    transposed(u, i + 1)
                if len(now) > 1:
                    gelu(1, i)
                for u in nxt2:
                    normalised(u, i + 2)
            with act.Fori(0, NP - 2) as i:
                step(i, (0, 1), (0, 1), (0, 1))
            step(NP - 2, (0, 1), (0, 1), (0,))
            step(NP - 1, (0, 1), (0,), ())
            step(NP, (0,), (), ())

        @block.vector
        def _(dve):
            c = Chain(dve, s.dve_step)

            def stats(tiles, ready, after=None):
                if after is not None:
                    dve.wait_ge(*after)
                    dve.sem_inc(s.dve_past, 1)
                marks = [c.mark(dve.bn_stats(stat[:, u, :], x)) for u, x in enumerate(tiles)]
                dve.wait_ge(s.dve_step, marks[3])
                dve.sem_inc(s.dve_past, 1)
                for u in range(4):
                    dve.bn_aggr(mv[:, u, :], stat[:, u, :]).then_inc(ready, 1)

            def normalise(u, y, x):
                return dve.tensor_scalar(y, x, mv[:, u, 0:1], rstd[:, u:u + 1], ALU.subtract, ALU.mult)

            def rows(t):
                return X[:, ds(t, 1), 0:D].rearrange("p a d -> p (a d)")

            dve.wait_ge(s.ld_l0, 16 * 9)
            dve.wait_ge(s.k0_ps, 1)
            for ci in range(CH):
                ins = dve.tensor_scalar(K0T[:, ci, :], pb[2][:, ci * NB * KEYS:(ci + 1) * NB * KEYS],
                                        bk0[:, ci:ci + 1], D ** -0.5, ALU.add, ALU.mult)
            ins.then_inc(s.k0_sb, 1)
            dve.wait_ge(s.pool_consts, 1)
            dve.tensor_copy(XI[:, :, IDC], ids[:, :])
            for t in range(NT):
                if t % TB == 0:
                    dve.wait_ge((s.ld_x, s.ld_x1)[t // TB], 16)
                if t % 4 == 0 and t:
                    dve.wait_ge(s.mv_a, t)
                c.mark(dve.bn_stats(stat[:, t % 4, :], X[:, t, 0:D]))
                if t % 4 == 3:
                    dve.wait_ge(s.dve_step, c.base + c.n)
                    for u in range(t - 3, t + 1):
                        dve.bn_aggr(mv4[:, u, :], stat[:, u % 4, :]).then_inc(s.mv_a, 1)
            dve.wait_ge(s.ld_ffn, 16 * 3)
            c.link(dve.tensor_reduce(wamax[:, :], WN, AX.X, ALU.max, apply_absolute_value=True))
            c.link(dve.tensor_scalar(wscale[:, :], wamax[:, :], 1.0 / 7.0, TINY, ALU.mult, ALU.max))
            dve.reciprocal(wrec[:, :], wscale[:, :]).then_inc(s.wstep_sb, 1)

            def y_in(g):
                for t in range(4 * g, 4 * g + 4):
                    if g:
                        dve.wait_ge(s.yT_ps, t - 3)
                    dve.tensor_scalar(ya[:, t % 4, :], X[:, t, 0:D], mv4[:, t, 0:1], rstd4[:, t:t + 1],
                                      ALU.subtract, ALU.mult).then_inc(s.y_a, 1)

            def y2_in(g):
                dve.wait_ge(s.rstd_b, g + 1)
                for u in range(4):
                    if g:
                        dve.wait_ge(s.y2T_ps, 4 * g + u - 3)
                    normalise(u, y2a[:, u, :], X[:, 4 * g + u, 0:D]).then_inc(s.y_b, 1)
                for u in range(4):
                    dve.wait_ge(s.y_b, 4 * g + u + 1)
                    c.mark(dve.tensor_reduce(amY[:, 4 * g + u:4 * g + u + 1], y2a[:, u, :], AX.X, ALU.max,
                                             apply_absolute_value=True))
            dve.wait_ge(s.rstd_a, 1)
            y_in(0)
            for g in range(NT // 4):
                for u in range(4):
                    dve.wait_ge(s.s0_ps, 4 * g + u + 1)
                    dve.tensor_reduce(nmax[:, u:u + 1], pb[4 + u][:, 0:KEYS], AX.X, ALU.max,
                                      negate=True).then_inc(s.nmax_a, 1)
                if g:
                    y2_in(g - 1)
                if g < NT // 4 - 1:
                    y_in(g + 1)
                dve.wait_ge(s.p0, 4 * g + 4)
                c.link(dve.reciprocal(rden[:, :], den[:, :]))
                for u in range(4):
                    x = X[:, 4 * g + u, 0:D]
                    dve.wait_ge(s.o0_ps, 4 * g + u + 1)
                    mk = c.mark(dve.scalar_tensor_tensor(x, pb[4 + u][:, 0:D], rden[:, u:u + 1], x, ALU.mult, ALU.add))
                stats([X[:, 4 * g + u, 0:D] for u in range(4)], s.mv_b, (s.dve_step, mk))
            y2_in(NT // 4 - 1)

            def scalar(k, in_, op0, s1, op1=None, s2=None):
                c.link(dve.tensor_scalar(sc[:, k:k + 1], in_, s1, s2, op0, op1 if op1 is not None else ALU.bypass))

            def step_of(k, amax, unit):
                if unit is None:
                    scalar(k, amax, ALU.mult, 1.0 / QMAX, ALU.max, TINY)
                    c.link(dve.reciprocal(sc[:, k + 1:k + 2], sc[:, k:k + 1]))
                else:
                    scalar(k, amax, ALU.mult, unit)
                    scalar(k, sc[:, k:k + 1], ALU.mult, 1.0 / QMAX, ALU.max, TINY)
                    c.link(dve.reciprocal(sc[:, k + 1:k + 2], sc[:, k:k + 1]))
                    scalar(k + 1, sc[:, k + 1:k + 2], ALU.mult, unit)

            dve.wait_ge(s.dve_step, c.base + c.n)
            dve.tensor_reduce(sc[:, 0:1], amY[:, :], AX.X, ALU.max).then_inc(s.ax_sb, 1)
            dve.wait_ge(s.els_sb, 1)
            dve.tensor_scalar(hscale[:, :], els[:, :], 4.0, HD ** -0.5, ALU.min, ALU.mult).then_inc(s.hsc_sb, 1)
            c.link(dve.tensor_tensor(wg2[:, :], wg[:, :], wg[:, :], ALU.mult))
            dve.tensor_reduce(wss[:, 0:1], wg2[:, :], AX.X, ALU.add).then_inc(s.wss_sb, 1)
            dve.memset(V1[:, :, HD:VE], 1.0)
            c.link(dve.tensor_scalar(WO1[:, :, :], WO1[:, :, :], tg[:, 1:2], None, ALU.mult))
            dve.tensor_scalar(bo1[:, :], bo1[:, :], tg[:, 1:2], None, ALU.mult).then_inc(s.wo_sb, 1)
            dve.wait_ge(s.csc_ps, 1)
            c.link(dve.tensor_copy(cscale[:, :], pb[5][:, 0:CH]))
            dve.wait_ge(s.k1_ps, 1)
            dve.wait_ge(s.keep_sb, 1)
            for ci in range(CH):
                c.link(dve.tensor_scalar(K1T[:, ci, :], pb[6][:, ci * NB * KEYS:(ci + 1) * NB * KEYS],
                                         bk1[:, ci:ci + 1], cscale[:, ci:ci + 1], ALU.add, ALU.mult))
            dve.tensor_tensor(K1T[:, :, :], K1T[:, :, :], keep.unsqueeze(1).to_broadcast([P, CH, NB * KEYS]),
                              ALU.mult).then_inc(s.k1_sb, 1)
            dve.wait_ge(s.wnorm_sb, 1)
            c.link(dve.tensor_scalar(wss[:, 1:2], wss[:, 1:2], 1e-4, None, ALU.max))
            c.link(dve.reciprocal(wss[:, 2:3], wss[:, 1:2]))
            dve.tensor_scalar(wgn[:, :], wg[:, :], wss[:, 2:3], None, ALU.mult).then_inc(s.wgn_sb, 1)
            dve.wait_ge(s.ar_x, 1)
            step_of(10, sc[:, 1:2], None)
            dve.wait_ge(s.y2T_sb, NT)
            for q in range(NQB):
                dve.tensor_scalar(YT[:, :, q * QB:(q + 1) * QB], YT[:, :, q * QB:(q + 1) * QB], sc[:, 11:12], MAGIC,
                                  ALU.mult, ALU.add).then_inc(s.tq_y, 1)
            with dve.Fori(0, NQB) as q:
                c.enter(q, FJ)
                for j in range(FJ):
                    dve.wait_ge(s.gu_sb, FJ + FJ * q + j + 1)
                    c.mark(dve.tensor_reduce(amG[:, ds(FJ * q + j, 1)], GT[:, j, ds(q * QB, QB)], AX.X, ALU.max,
                                             apply_absolute_value=True))
            c.leave(NQB)
            dve.wait_ge(s.dve_step, c.base)
            dve.tensor_reduce(sc[:, 2:3], amG[:, :], AX.X, ALU.max).then_inc(s.am_g, 1)
            dve.wait_ge(s.ar_g, 1)
            step_of(12, sc[:, 3:4], sc[:, 10:11])
            scalar(22, sc[:, 12:13], ALU.mult, 2.0 ** -16)
            dve.sem_inc(s.z_done, 2)
            dve.sem_inc(s.scal_g, 1)
            with dve.Fori(0, NQB) as q:
                c.enter(q, FJ + 4)
                for h in range(2):
                    for j in range(3 * h, 3 * h + 3):
                        dve.wait_ge(s.gu_sb, FJ + FJ * (NQB + q) + j + 1)
                        c.mark(dve.tensor_reduce(amU[:, ds(FJ * q + j, 1)], UT_[:, j, ds(q * QB, QB)], AX.X, ALU.max,
                                                 apply_absolute_value=True))
                    dve.wait_ge(s.sig_done, 2 * q + h + 1)
                    c.link(dve.tensor_scalar(u16[:, h, :], sig[:, h, :], 65536.0, 65535.0, ALU.mult, ALU.min))
                    z = GT[:, 3 * h:3 * h + 3, ds(q * QB, QB)]
                    dve.tensor_tensor(z, ng[:, h, :].rearrange("p (j n) -> p j n", j=3),
                                      u16[:, h, :].rearrange("p (j n) -> p j n", j=3), ALU.mult).then_inc(s.z_done, 1)
                    dve.wait_ge(s.z_done, 2 + 2 * q + h + 1)
                    c.mark(dve.tensor_reduce(amZ[:, ds(2 * q + h, 1)], z, AX.XY, ALU.max, apply_absolute_value=True))
            c.leave(NQB)
            dve.wait_ge(s.dve_step, c.base)
            dve.tensor_reduce(sc[:, 4:5], amZ[:, :], AX.X, ALU.max).then_inc(s.am_z, 1)
            dve.tensor_reduce(sc[:, 6:7], amU[:, :], AX.X, ALU.max).then_inc(s.am_u, 1)
            dve.wait_ge(s.ar_z, 1)
            step_of(14, sc[:, 5:6], sc[:, 22:23])
            dve.wait_ge(s.ar_u, 1)
            step_of(16, sc[:, 7:8], sc[:, 10:11])
            scalar(18, sc[:, 14:15], ALU.mult, sc[:, 16:17])
            dve.sem_inc(s.p_done, 2)
            dve.sem_inc(s.scal_u, 1)
            with dve.Fori(0, NQB) as q:
                c.enter(q, 2)
                for h in range(2):
                    dve.wait_ge(s.nzu_done, 2 * q + h + 1)
                    pr = GT[:, 3 * h:3 * h + 3, ds(q * QB, QB)]
                    dve.tensor_tensor(pr, nz[:, h, :].rearrange("p (j n) -> p j n", j=3),
                                      nu[:, h, :].rearrange("p (j n) -> p j n", j=3), ALU.mult).then_inc(s.p_done, 1)
                    dve.wait_ge(s.p_done, 2 + 2 * q + h + 1)
                    c.mark(dve.tensor_reduce(amP[:, ds(2 * q + h, 1)], pr, AX.XY, ALU.max, apply_absolute_value=True))
            c.leave(NQB)
            dve.wait_ge(s.dve_step, c.base)
            dve.tensor_reduce(sc[:, 8:9], amP[:, :], AX.X, ALU.max).then_inc(s.am_p, 1)
            dve.wait_ge(s.ar_p, 1)
            step_of(19, sc[:, 9:10], sc[:, 18:19])
            scalar(21, sc[:, 19:20], ALU.mult, tg[:, 2:3])
            with dve.Fori(0, NQB) as q:
                b = GT[:, :, ds(q * QB, QB)]
                dve.tensor_scalar(b, b, sc[:, 20:21], MAGIC, ALU.mult, ALU.add).then_inc(s.tq_p, 1)
            with dve.Fori(0, NT // 4) as i:
                c.enter(i, 8)
                t = 4 * i
                for u in range(4):
                    dve.wait_ge(s.dn_ps, t + u + 1)
                    mk = c.mark(dve.scalar_tensor_tensor(rows(t + u), pb[u][:, 0:D], sc[:, 21:22], rows(t + u),
                                                         ALU.mult, ALU.add))
                stats([rows(t + u) for u in range(4)], s.mv_c, (s.dve_step, mk))
                dve.wait_ge(s.rstd_c, i + 1)
                for u in range(4):
                    dve.wait_ge(s.y3T_ps, t + u + 1)
                    normalise(u, y3[:, u, :], rows(t + u)).then_inc(s.y_c, 1)
            c.leave(NT // 4)

            def head_out(t, u):
                dve.wait_ge(s.o_ps, t + u + 1)
                o = pb[u][:, 0:H * VE].rearrange("p (h d) -> p h d", d=VE)
                c.link(dve.reciprocal(rd[:, u, :], o[:, :, HD]))
                dve.tensor_tensor(att[:, u, :].rearrange("p (h d) -> p h d", d=HD), o[:, :, 0:HD],
                                  rd[:, u, :].unsqueeze(2).to_broadcast([P, H, HD]), ALU.mult).then_inc(s.att_sb, 1)

            def residual(t, tile, u):
                dve.wait_ge(s.wo_ps, t + u + 1)
                dve.tensor_tensor(rows(tile + u), pb[5][:, 0:D], rows(tile + u), ALU.add).then_inc(s.x3_done, 1)

            def moments(t, tile):
                dve.wait_ge(s.x3_done, t + 2)
                dve.sem_inc(s.dve_past, 1)
                for u in range(2):
                    mk = c.mark(dve.bn_stats(stat[:, u, :], rows(tile + u)))
                dve.wait_ge(s.dve_step, mk)
                dve.sem_inc(s.dve_past, 1)
                for u in range(2):
                    mk = c.mark(dve.bn_aggr(mv[:, u, :], stat[:, u, :]))
                dve.wait_ge(s.dve_step, mk)
                dve.tensor_copy(mv4[:, ds(tile, 2), :], mv[:, 0:2, :]).then_inc(s.mv_d, 2)

            def pair(t, before):
                for k in range(2 * NQ):
                    u, hq = k // NQ, k % NQ
                    if before is not None and k == 1:
                        residual(t - 2, before, 0)
                    if before is not None and k == 3:
                        head_out(t - 2, 1)
                    if before is not None and k == 5:
                        residual(t - 2, before, 1)
                    if k == 7:
                        head_out(t, 0)
                    s4 = pb[2 + k % 2][:, 0:HQK].rearrange("p (h k) -> p h k", h=HQ)
                    m4 = mx[:, k % 2, :]
                    dve.wait_ge(s.s_ps, NQ * t + k + 1)
                    c.link(dve.tensor_reduce(m4, s4, AX.X, ALU.max))
                    dve.tensor_tensor(e_[:, u, hq * HQK:(hq + 1) * HQK].rearrange("p (h k) -> p h k", h=HQ), s4,
                                      m4.unsqueeze(2).to_broadcast([P, HQ, KEYS]), ALU.subtract).then_inc(s.e_sub, 1)
                    if before is not None and k == 6:
                        moments(t - 2, before)

            per = 2 * NQ + 6
            dve.wait_ge(s.bo_added, 1)
            for b in range(NB):
                pair(b * TB, (b - 1) * TB if b else None)
                with dve.Fori(1, FAR) as i:
                    c.enter(i - 1, per)
                    pair(b * TB + 2 * i, b * TB + NEAR + 2 * i - 2)
                c.leave(FAR - 1)
                pair(b * TB + 2 * FAR, b * TB + TB - 2)
            residual(NT - 2, (NB - 1) * TB, 0)
            head_out(NT - 2, 1)
            residual(NT - 2, (NB - 1) * TB, 1)
            moments(NT - 2, (NB - 1) * TB)
            dve.sem_inc(s.y4T_ps, 4)
            dve.wait_ge(s.rstd_d, 1)
            with dve.Fori(0, NT // 4) as i:
                c.enter(i, 1)
                for u in range(4):
                    t = 4 * i + u
                    dve.wait_ge(s.y4T_ps, t + 1)
                    dve.tensor_scalar(y4[:, u, :], rows(t), mv4[:, ds(t, 1), 0], rstd4[:, ds(t, 1)],
                                      ALU.subtract, ALU.mult).then_inc(s.y_d, 1)
                dve.wait_ge(s.lg_ps, i + 1)
                c.mark(dve.tensor_copy(LG[:, ds(4 * i, 4), :],
                                       pb[4][:, 0:4 * E].rearrange("p (t e) -> p t e", e=E)))
            c.leave(NT // 4)
            dve.tensor_copy(X[:, :, RSTD], rstd4[:, :])
            dve.scalar_tensor_tensor(X[:, :, NMR], mv4[:, :, 0], -1.0, rstd4[:, :], ALU.mult, ALU.mult)
            dve.wait_ge(s.dve_step, c.base)
            c.link(dve.tensor_reduce(LM[:, :], LG, AX.X, ALU.max))
            LMB = LM[:, :].unsqueeze(2).to_broadcast([P, NT, E])
            dve.tensor_tensor(LX, LG, LMB, ALU.subtract).then_inc(s.lx_sb, 1)
            c.link(dve.tensor_tensor(OH, LG, LMB, ALU.is_ge))
            c.link(dve.tensor_tensor(OH, OH, rank[:, :].unsqueeze(1).to_broadcast([P, NT, E]), ALU.mult))
            c.link(dve.tensor_reduce(LM[:, :], OH, AX.X, ALU.max))
            c.link(dve.tensor_tensor(OH, OH, LMB, ALU.is_equal))
            dve.tensor_copy(OHB[:, :, :], OH).then_inc(s.oh_sb, 1)
            dve.wait_ge(s.ex_sb, 1)
            c.link(dve.tensor_reduce(LM[:, :], LX, AX.X, ALU.add))
            c.link(dve.reciprocal(LM[:, :], LM[:, :]))
            dve.tensor_scalar(X[:, :, COEF], LM[:, :], tg[:, 3:4], None, ALU.mult)
            dve.wait_ge(s.cnt_ps, 1)
            dve.memset(CUM[:, 0, :], 0.0)
            c.link(dve.tensor_copy(TOT, pb[1][:, 0:NT * E].rearrange("p (t e) -> p t e", e=E)))
            for t in range(NT):
                c.link(dve.tensor_tensor(CUM[:, t + 1, :], CUM[:, t, :], TOT[:, t, :], ALU.add))
            c.link(dve.tensor_scalar(cnt_i[:, :], CUM[:, NT, :], float(P - 1), None, ALU.add))
            c.link(dve.tensor_scalar(cnt_i[:, :], cnt_i[:, :], 7, None, ALU.arith_shift_right))
            c.link(dve.tensor_copy(tiles_e[:, :], cnt_i[:, :]))
            c.link(dve.memset(start_e[:, 0:1], 0.0))
            for e in range(1, E):
                c.link(dve.tensor_tensor(start_e[:, e:e + 1], start_e[:, e - 1:e], tiles_e[:, e - 1:e], ALU.add))
            c.link(dve.tensor_scalar(start128[:, :], start_e[:, :], float(P), None, ALU.mult))
            c.link(dve.tensor_tensor(CUM[:, 0:NT, :], CUM[:, 0:NT, :],
                                     start128[:, :].unsqueeze(1).to_broadcast([P, NT, E]), ALU.add))
            c.link(dve.tensor_tensor(CUM[:, 0:NT, :], CUM[:, 0:NT, :],
                                     pb[0][:, 0:NT * E].rearrange("p (t e) -> p t e", e=E), ALU.add))
            c.link(dve.tensor_tensor(CUM[:, 0:NT, :], CUM[:, 0:NT, :], OH, ALU.mult))
            c.link(dve.tensor_reduce(LM[:, :], CUM[:, 0:NT, :], AX.X, ALU.add))
            dve.tensor_copy(pos_i[:, :], LM[:, :]).then_inc(s.pos_sb, 1)
            c.link(dve.tensor_tensor(slot[:, :, :], slot[:, :, :],
                                     start_e[:, 1:E].unsqueeze(1).to_broadcast([P, NS, E - 1]), ALU.is_ge))
            c.link(dve.tensor_reduce(eslot[:, :], slot[:, :, :], AX.X, ALU.add))
            dve.tensor_copy(EXPS[:, :], eslot[:, :]).then_inc(s.slots_sb, 1)
            dve.wait_ge(s.slots_sb, 1)
            dve.wait_ge(s.ld_b1, 16)
            dve.wait_ge(s.ld_b2, 16)

            def bias1(u, i):
                e = dve.value_load(EXPS[0:1, ds(2 * i + u, 1)], min_val=0, max_val=E - 1)
                dve.wait_ge(s.h_ps, 2 * i + u + 1)
                dve.tensor_tensor(hb[:, u, :], pb[2 + u], B1[:, ds(e * HID, HID)], ALU.add).then_inc(s.hb_sb, 1)

            def hidden(u, i):
                dve.wait_ge(s.hT_ps, 2 * i + u + 1)
                dve.tensor_copy(hT[:, u, :], pb[4 + u]).then_inc(s.hT_sb, 1)

            def result(u, i, first=False):
                row = rb[u][:, ds(i, 1), :].rearrange("p a c -> p (a c)")
                e = dve.value_load(EXPS[0:1, ds(2 * i + u, 1)], min_val=0, max_val=E - 1)
                if not first:
                    dve.wait_ge(s.rows_out0 if u == 0 else s.rows_out1, 16 * i)
                dve.tensor_copy(rid[:, u:u + 1], row[:, IDC:IDC + 1].bitcast(I32))
                dve.wait_ge(s.eo_ps, 2 * i + u + 1)
                c.link(dve.tensor_tensor(ob[:, u, :], pb[6 + u][:, 0:D], B2[:, ds(e * D, D)], ALU.add))
                dve.scalar_tensor_tensor(res[:, u, :], ob[:, u, :], row[:, COEF:COEF + 1], row[:, 0:D],
                                         ALU.mult, ALU.add).then_inc(s.res_sb, 1)

            def step(i, now, prev, first=False):
                for u in now:
                    bias1(u, i)
                for u in prev:
                    result(u, i - 1, first)
                for u in now:
                    hidden(u, i)
            dve.sem_inc(s.res_sb, 2)
            dve.wait_ge(s.rows_in, 16 * 2)
            dve.wait_ge(s.more_rows_in, 16 * 2)
            step(0, (0, 1), ())
            c.enter(0, 2)
            step(1, (0, 1), (0, 1), True)
            c.leave(1)
            with dve.Fori(2, NP) as i:
                c.enter(i - 2, 2)
                step(i, (0, 1), (0, 1))
            c.leave(NP - 2)
            c.enter(0, 3)
            step(NP, (0,), (0, 1))
            step(NP + 1, (), (0,))
            c.leave(1)

        @block.tensor
        def _(pe):
            def mm(out_, lhsT, rhs, first, last):
                return pe.matmul(out_, lhsT=lhsT, rhs=rhs, start=first, stop=last)

            pe.wait_ge(s.consts, 1)
            pe.wait_ge(s.ld_l0, 16 * 9)
            for ci in range(CH):
                for b in range(NB):
                    o = (ci * NB + b) * KEYS
                    ins = pe.transpose(pb[0][:, o:o + KEYS], CTX[:, b, ci * P:(ci + 1) * P], ident[0:KEYS, 0:KEYS])
            ins.then_inc(s.ctxT_ps, 1)
            for dj in range(CH):
                for ci in range(CH):
                    ins = pe.transpose(pb[1][:, dj * D + ci * P:dj * D + (ci + 1) * P],
                                       WQ0[:, ci, dj * P:(dj + 1) * P], ident[:, :])
            ins.then_inc(s.wq0T_ps, 1)

            def keysT(ps, w, done):
                for dj in range(CH):
                    for ci in range(CH):
                        ins = mm(ps[:, dj * NB * KEYS:(dj + 1) * NB * KEYS], w[:, ci, dj * P:(dj + 1) * P],
                                 CTXT[:, ci, :], ci == 0, ci == CH - 1)
                ins.then_inc(done, 1)

            def values(ps, w, bias, done):
                for b in range(NB):
                    for ci in range(CH):
                        mm(ps[0:KEYS, b * D:(b + 1) * D], CTXT[:, ci, b * KEYS:(b + 1) * KEYS], w[:, ci, :], ci == 0, False)
                    ins = mm(ps[0:KEYS, b * D:(b + 1) * D], ones[0:1, 0:KEYS], bias, False, True)
                ins.then_inc(done, 1)

            pe.wait_ge(s.ctxT_sb, 1)
            keysT(pb[2], WK0, s.k0_ps)
            values(pb[4], WV0, bv0, s.v0_ps)
            pe.wait_ge(s.wq0T_sb, 1)
            pe.wait_ge(s.k0_sb, 1)
            for ci in range(CH):
                for dj in range(CH):
                    mm(pb[3][:, ci * NB * KEYS:(ci + 1) * NB * KEYS], WQ0T[:, dj, ci * P:(ci + 1) * P], K0T[:, dj, :],
                       dj == 0, dj == CH - 1)
            for dj in range(CH):
                ins = mm(pb[3][0:1, 320:320 + NB * KEYS], bq0[:, dj:dj + 1], K0T[:, dj, :], dj == 0, dj == CH - 1)
            ins.then_inc(s.a0_ps, 1)
            pe.wait_ge(s.a0_sb, 2)
            pe.wait_ge(s.v0_sb, 1)

            def transposed(ps, y, done):
                for ci in range(CH):
                    ins = pe.transpose(ps[:, ci * P:(ci + 1) * P], y[:, ci * P:(ci + 1) * P], ident[:, :])
                ins.then_inc(done, 1)

            def y_in(g):
                for t in range(4 * g, 4 * g + 4):
                    pe.wait_ge(s.y_a, t + 1)
                    transposed(pb[t % 4], ya[:, t % 4, :], s.yT_ps)

            def y2_in(g):
                for t in range(4 * g, 4 * g + 4):
                    pe.wait_ge(s.y_b, t + 1)
                    transposed(pb[t % 4], y2a[:, t % 4, :], s.y2T_ps)
            y_in(0)
            for g in range(NT // 4):
                b = 4 * g // TB
                sl = slice(b * KEYS, (b + 1) * KEYS)
                for u in range(4):
                    pe.wait_ge(s.yT_sb, 4 * g + u + 1)
                    if g:
                        pe.wait_ge(s.mv_b, 4 * g - 3 + u)
                    for ci in range(CH):
                        mm(pb[4 + u][:, 0:KEYS], yTa[:, u, ci * P:(ci + 1) * P], A0[:, ci, sl], ci == 0, False)
                    mm(pb[4 + u][:, 0:KEYS], ones[0:1, :], R0[:, sl], False, True).then_inc(s.s0_ps, 1)
                if g:
                    y2_in(g - 1)
                for u in range(4):
                    if g:
                        pe.wait_ge(s.y2T_sb, 4 * g - 3 + u)
                    pe.wait_ge(s.p0, 4 * g + u + 1)
                    pe.transpose(pb[u][0:KEYS, 0:P], pa[:, u, :], ident[:, :]).then_inc(s.pT0_ps, 1)
                for u in range(4):
                    pe.wait_ge(s.pT0_sb, 4 * g + u + 1)
                    mm(pb[4 + u][:, 0:D], pTa[:, u, :], V0[:, b, :], True, True).then_inc(s.o0_ps, 1)
                if g < NT // 4 - 1:
                    y_in(g + 1)
            y2_in(NT // 4 - 1)
            pe.wait_ge(s.y2T_sb, NT)
            pe.wait_ge(s.ld_l1, 16 * 14)
            pe.wait_ge(s.pool_consts, 1)
            pe.wait_ge(s.hsc_sb, 1)
            for ci in range(CH):
                ins = mm(pb[5][:, ci:ci + 1], expand[:, ci * P:(ci + 1) * P], hscale[:, :], True, True)
            ins.then_inc(s.csc_ps, 1)
            keysT(pb[6], WK1, s.k1_ps)
            values(pb[7], WV1, bv1, s.v1_ps)
            for ci in range(CH):
                ins = pe.transpose(pb[0][0:G, ci * P:(ci + 1) * P], WR[:, ci, :], ident[:, :])
            ins.then_inc(s.wrT_ps, 1)
            pe.wait_ge(s.wgn_sb, 1)
            pe.wait_ge(s.wrT_sb, 1)
            pe.transpose(pb[0][0:G, D:D + E], wgn[:, :], ident[0:E, 0:E]).then_inc(s.wgT_ps, 1)
            pe.wait_ge(s.wgT_sb, 1)
            for ci in range(CH):
                ins = mm(pb[1][:, ci * E:(ci + 1) * E], WRT[:, ci * P:(ci + 1) * P], WGNT[:, :], True, True)
            ins.then_inc(s.gm_ps, 1)
            pe.wait_ge(s.gm_sb, 1)
            pe.wait_ge(s.k1_sb, 1)
            pe.wait_ge(s.v1_sb, 1)
            pe.wait_ge(s.wq_sb, 3)
            WF = BIGG[:, 0:4608]
            src = [1536 + j * D + ci * P for ci in range(CH) for j in range(FJ)]
            src += [j * D + ci * P for ci in range(CH) for j in range(FJ)]
            src += [3072 + o * F + j * P for j in range(FJ) for o in range(CH)]
            for g in range(9):
                if g == 8:
                    pe.wait_ge(s.wT_sb, 1)
                for k in range(4):
                    ins = pe.transpose(pb[g % 8][:, k * P:(k + 1) * P], WF[:, src[4 * g + k]:src[4 * g + k] + P], ident[:, :])
                ins.then_inc(s.wT_ps, 1)
            pe.wait_ge(s.wT_sb, 9)

            for n, w in enumerate((WGT, WUT)):
                with pe.Fori(0, NQB) as q:
                    if n == 0:
                        pe.wait_ge(s.nq, q + 1)
                    for j in range(FJ):
                        pe.wait_ge(s.gu_sb, FJ * (n * NQB + q) + j + 1)
                        for ci in range(CH):
                            ins = mm(pb[j], w[:, ci, j * P:(j + 1) * P], YT[:, ci, ds(q * QB, QB)], ci == 0, ci == CH - 1)
                        ins.then_inc(s.gu_ps, 1)

            def down(q):
                pe.wait_ge(s.no_done, q + 1)
                for u in range(4):
                    t = 4 * q + u
                    if q:
                        pe.wait_ge(s.mv_c, t - 3)
                    for j in range(FJ):
                        ins = mm(pb[u][:, 0:D], UT_[:, j, t * P:(t + 1) * P], WDT[:, j, :], j == 0, j == FJ - 1)
                    ins.then_inc(s.dn_ps, 1)

            def y3_in(q):
                for u in range(4):
                    pe.wait_ge(s.y_c, 4 * q + u + 1)
                    if q:
                        pe.wait_ge(s.y3T_sb, 4 * q + u - 3)
                    transposed(pb[4 + u], y3[:, u, :], s.y3T_ps)
            pe.wait_ge(s.gu_sb, FJ + 2 * FJ * NQB)
            pe.sem_inc(s.y3T_ps, 4)
            for q in range(NQB):
                down(q)
                if q:
                    y3_in(q - 1)
            y3_in(NQB - 1)

            def queries(t):
                for dj in range(CH):
                    for ci in range(CH):
                        ins = mm(pb[4][:, dj * 2 * P:(dj + 1) * 2 * P], WQ1[:, ci, dj * P:(dj + 1) * P],
                                 YT[:, ci, ds(t * P, 2 * P)], ci == 0, ci == CH - 1)
                ins.then_inc(s.q_ps, 2)

            def scores(b, k, near):
                u, hq = k // NQ, k % NQ
                ps = pb[2 + k % 2][:, 0:HQK]
                cols = slice(hq * HQK, (hq + 1) * HQK)
                ci, n = hq // 2, (b * CH + hq // 2) * 8 + (hq % 2) * HQ
                mm(ps, qT[:, ci, u * P:(u + 1) * P], KBD[:, n:n + HQ, :].rearrange("p h k -> p (h k)"), True, False)
                if near:
                    for m in range(3):
                        mm(ps, flipb[:, :], BN[:, 3 * u + m, cols], False, False)
                ins = mm(ps, onesb[0:1 if near else 4, :], CM[0:1 if near else 4, b, cols], False, True)
                ins.then_inc(s.s_ps, 1)

            def weightsT(t, k):
                u, hq = k // NQ, k % NQ
                pe.wait_ge(s.e_exp, NQ * t + k + 1)
                for h in range(HQ):
                    ins = pe.transpose(pb[6 + k % 2][0:KEYS, h * P:(h + 1) * P],
                                       e_[:, u, hq * HQK + h * KEYS:hq * HQK + (h + 1) * KEYS], ident[:, :])
                ins.then_inc(s.pT_ps, 1)

            def heads(b, t, k):
                u, hq = k // NQ, k % NQ
                pe.wait_ge(s.pT_sb, NQ * t + k + 1)
                for h in range(hq * HQ, (hq + 1) * HQ):
                    ins = mm(pb[u][:, h * VE:(h + 1) * VE], pT[:, u, h * P:(h + 1) * P], V1[:, b * H + h, :], True, True)
                if hq == NQ - 1:
                    ins.then_inc(s.o_ps, 1)

            def project_in(t, u, first=False):
                if not first:
                    pe.wait_ge(s.x3_done, t + u)
                pe.wait_ge(s.att_sb, t + u + 1)
                transposed(pb[5], att[:, u, :], s.attT_ps)

            def project(t, u):
                pe.wait_ge(s.attT_sb, t + u + 1)
                for ci in range(CH):
                    ins = mm(pb[5][:, 0:D], attT[:, u, ci * P:(ci + 1) * P], WO1[:, ci, :], ci == 0, ci == CH - 1)
                ins.then_inc(s.wo_ps, 1)

            def end_of_pair(b, t, k):
                if k < 3:
                    heads(b, t, k + 5)
                if k == 0:
                    project(t, 0)
                if k == 3:
                    project_in(t, 1)
                if k == 4:
                    project(t, 1)

            def pair(b, t, near, before, last=False):
                pe.wait_ge(s.q_sb, t + 2)
                for k in range(2 * NQ):
                    if k >= 2:
                        weightsT(t, k - 2)
                    elif before is not None:
                        weightsT(t - 2, k + 6)
                    scores(b, k, near)
                    if k == 7 and not last:
                        queries(t + 2)
                    if k >= 3:
                        heads(b, t, k - 3)
                    if before is not None:
                        end_of_pair(before, t - 2, k)
                    if k == 7:
                        project_in(t, 0, before is None)

            pe.wait_ge(s.kbd_sb, 1)
            pe.wait_ge(s.wo_sb, 1)
            pe.wait_ge(s.ld_const, 16 * 7)
            pe.wait_ge(s.y3T_sb, NT)
            queries(0)
            for b in range(NB):
                pair(b, b * TB, False, b - 1 if b else None)
                with pe.Fori(1, FAR) as i:
                    pair(b, b * TB + 2 * i, False, b)
                pe.wait_ge(s.near_sb, NEAR)
                pair(b, b * TB + 2 * FAR, True, b, b == NB - 1)
            for k in range(5):
                if k < 2:
                    weightsT(NT - 2, k + 6)
                end_of_pair(NB - 1, NT - 2, k)
            with pe.Fori(0, NT // 4) as i:
                for u in range(4):
                    pe.wait_ge(s.y_d, 4 * i + u + 1)
                    transposed(pb[u], y4[:, u, :], s.y4T_ps)
                for u in range(4):
                    pe.wait_ge(s.y4T_sb, 4 * i + u + 1)
                    for ci in range(CH):
                        ins = mm(pb[4][:, u * E:(u + 1) * E], y4T[:, u, ci * P:(ci + 1) * P], GM[:, ci, :],
                                 ci == 0, ci == CH - 1)
                ins.then_inc(s.lg_ps, 1)
            pe.wait_ge(s.oh_sb, 1)
            oh = OHB[:, :, :].rearrange("p t e -> p (t e)")
            mm(pb[0][:, 0:NT * E], before[:, :], oh, True, True)
            mm(pb[1][:, 0:NT * E], onesb[:, :], oh, True, True).then_inc(s.cnt_ps, 1)
            pe.wait_ge(s.pos_sb, 1)
            pe.wait_ge(s.slots_sb, 1)
            pe.wait_ge(s.ld_w1, 16)
            pe.wait_ge(s.ld_w2, 16)

            W1f = W1.rearrange("p n h -> p (n h)")
            W2f = W2.rearrange("p n h -> p (n h)")

            def inputs(u, i):
                pe.wait_ge(s.ys_sb, 2 * i + u + 1)
                transposed(pb[u], ys[:, u, :], s.ysT_ps)

            def layer1(u, i):
                e = pe.value_load(EXPS[0:1, ds(2 * i + u, 1)], min_val=0, max_val=E - 1)
                pe.wait_ge(s.ysT_sb, 2 * i + u + 1)
                for ci in range(CH):
                    ins = mm(pb[2 + u], ysT[:, u, ci * P:(ci + 1) * P], W1f[:, ds(e * (CH * HID) + ci * HID, HID)],
                             ci == 0, ci == CH - 1)
                ins.then_inc(s.h_ps, 1)

            def hiddenT(u, i):
                pe.wait_ge(s.gelu_sb, 2 * i + u + 1)
                for j in range(HJ):
                    ins = pe.transpose(pb[4 + u][:, j * P:(j + 1) * P], hb[:, u, j * P:(j + 1) * P], ident[:, :])
                ins.then_inc(s.hT_ps, 1)

            def layer2(u, i):
                e = pe.value_load(EXPS[0:1, ds(2 * i + u, 1)], min_val=0, max_val=E - 1)
                pe.wait_ge(s.res_sb, 2 * i + u + 1)
                pe.wait_ge(s.hT_sb, 2 * i + u + 1)
                for j in range(HJ):
                    ins = mm(pb[6 + u][:, 0:D], hT[:, u, j * P:(j + 1) * P], W2f[:, ds(e * (HJ * D) + j * D, D)],
                             j == 0, j == HJ - 1)
                ins.then_inc(s.eo_ps, 1)

            def step(i, now, nxt, prev):
                for u in now:
                    layer1(u, i)
                for u in nxt:
                    inputs(u, i + 1)
                for u in prev:
                    layer2(u, i - 1)
                for u in now:
                    hiddenT(u, i)
            for u in range(2):
                inputs(u, 0)
            step(0, (0, 1), (0, 1), ())
            with pe.Fori(1, NP - 1) as i:
                step(i, (0, 1), (0, 1), (0, 1))
            step(NP - 1, (0, 1), (0,), (0, 1))
            step(NP, (0,), (), (0, 1))
            step(NP + 1, (), (), (0,))


_INS = ["x", "ctx_1024", "mask_BxS2_bf0", "g_xattn", "g_ffn",
        "L0_xattn_Wq", "L0_xattn_bq", "L0_xattn_Wk", "L0_xattn_bk", "L0_xattn_Wv", "L0_xattn_bv",
        "L0_ffn_w_gate", "L0_ffn_w_up", "L0_ffn_w_down",
        "L1_xattn_Wq", "L1_xattn_bq", "L1_xattn_Wk", "L1_xattn_bk", "L1_xattn_Wv", "L1_xattn_bv",
        "L1_xattn_Wo", "L1_xattn_bo", "L1_xattn_logit_scale", "L1_xattn_bias_table",
        "L1_ffn_w_red", "L1_ffn_wg", "L1_ffn_W1", "L1_ffn_b1", "L1_ffn_W2", "L1_ffn_b2"]


def kernel(**inputs):
    import concourse.bacc as bacc
    from concourse.bass_utils import run_bass_kernel_spmd

    nc = bacc.Bacc("TRN2", target_bir_lowering=False, num_devices=1)
    arrays, args = {}, {}
    for name in _INS:
        v = np.ascontiguousarray(inputs[name])
        arrays[f"in_{name}"] = v
        args[name] = nc.dram_tensor(f"in_{name}", v.shape, mybir.dt.from_np(v.dtype), kind="ExternalInput").ap()
    out = nc.dram_tensor("out_0", (NB, S, D), F32, kind="ExternalOutput").ap()
    flamingo_kernel(nc, args, out)
    r = run_bass_kernel_spmd(nc, [arrays], core_ids=[0])
    return r.results[0]["out_0"]
```

```python
import numpy as np

import concourse.bass as bass
from concourse import mybir
from contextlib import ExitStack

F32 = mybir.dt.float32
BF16 = mybir.dt.bfloat16
I16 = mybir.dt.int16
I32 = mybir.dt.int32
U8 = mybir.dt.uint8
ALU = mybir.AluOpType
ACT = mybir.ActivationFunctionType
AX = mybir.AxisListType
ds = bass.ds

P = 128
NB, S, D = 2, 1024, 256
NT = NB * S // P
TB = S // P
KEYS = 77
CH = D // P
H, HD = 16, 16
HK = H * KEYS
HQ = 4
HQK = HQ * KEYS
NQ = H // HQ
VE = 2 * HD
F = 768
FJ = F // P
BLK = 32
QB = 512
NQB = NB * S // QB
HB = QB // 2
E, HID, G = 8, 512, 16
HJ = HID // P
NS = NT + E - 1
NP = NS // 2
MAXD = 128
NEAR = 2
EXT = NEAR * P + KEYS - 1
ROW = D + 4
NMR, RSTD, COEF, IDC = D, D + 1, D + 2, D + 3
EPS = 1e-5
MAGIC = 1.5 * 2.0 ** 23
U16 = 2.0 ** 16
QMAX = 32767.0
TINY = 1e-12
NEG = -(2.0 ** 126)
NOWHERE = 1 << 20


class Signals:

    def __init__(self, sem):
        self.ld_l0 = sem("ld_l0")
        self.ld_x = sem("ld_x")
        self.ld_x1 = sem("ld_x1")
        self.ld_ffn = sem("ld_ffn")
        self.ld_l1 = sem("ld_l1")
        self.ld_ext = sem("ld_ext")
        self.ld_near = sem("ld_near")
        self.ld_const = sem("ld_const")
        self.ld_w1 = sem("ld_w1")
        self.ld_w2 = sem("ld_w2")
        self.ld_b1 = sem("ld_b1")
        self.ld_b2 = sem("ld_b2")
        self.pads_written = sem("pads_written")
        self.ext_stored = sem("ext_stored")
        self.consts = sem("consts")
        self.pool_consts = sem("pool_consts")
        self.ctxT_ps = sem("ctxT_ps")
        self.ctxT_sb = sem("ctxT_sb")
        self.wq0T_ps = sem("wq0T_ps")
        self.wq0T_sb = sem("wq0T_sb")
        self.k0_ps = sem("k0_ps")
        self.k0_sb = sem("k0_sb")
        self.a0_ps = sem("a0_ps")
        self.a0_sb = sem("a0_sb")
        self.v0_ps = sem("v0_ps")
        self.v0_sb = sem("v0_sb")
        self.els_sb = sem("els_sb")
        self.hsc_sb = sem("hsc_sb")
        self.csc_ps = sem("csc_ps")
        self.k1_ps = sem("k1_ps")
        self.csc_sb = sem("csc_sb")
        self.k1_sb = sem("k1_sb")
        self.v1_ps = sem("v1_ps")
        self.v1_sb = sem("v1_sb")
        self.kbd_sb = sem("kbd_sb")
        self.ext_sb = sem("ext_sb")
        self.wrT_ps = sem("wrT_ps")
        self.wrT_sb = sem("wrT_sb")
        self.wss_sb = sem("wss_sb")
        self.wnorm_sb = sem("wnorm_sb")
        self.wgn_sb = sem("wgn_sb")
        self.wgT_ps = sem("wgT_ps")
        self.wgT_sb = sem("wgT_sb")
        self.gm_ps = sem("gm_ps")
        self.gm_sb = sem("gm_sb")
        self.tg_sb = sem("tg_sb")
        self.wo_sb = sem("wo_sb")
        self.wstep_sb = sem("wstep_sb")
        self.wsteps_sb = sem("wsteps_sb")
        self.wround_sb = sem("wround_sb")
        self.wq_sb = sem("wq_sb")
        self.wT_ps = sem("wT_ps")
        self.wT_sb = sem("wT_sb")
        self.mv_a = sem("mv_a")
        self.rstd_a = sem("rstd_a")
        self.keep_sb = sem("keep_sb")
        self.slots_sb = sem("slots_sb")
        self.am_u = sem("am_u")
        self.ar_u = sem("ar_u")
        self.wn_sb = sem("wn_sb")
        self.scal_u = sem("scal_u")
        self.y_a = sem("y_a")
        self.yT_ps = sem("yT_ps")
        self.yT_sb = sem("yT_sb")
        self.s0_ps = sem("s0_ps")
        self.nmax_a = sem("nmax_a")
        self.p0 = sem("p0")
        self.pT0_ps = sem("pT0_ps")
        self.pT0_sb = sem("pT0_sb")
        self.o0_ps = sem("o0_ps")
        self.x1_done = sem("x1_done")
        self.mv_b = sem("mv_b")
        self.rstd_b = sem("rstd_b")
        self.y_b = sem("y_b")
        self.y2T_ps = sem("y2T_ps")
        self.y2T_sb = sem("y2T_sb")
        self.ax_sb = sem("ax_sb")
        self.ar_x = sem("ar_x")
        self.scal_x = sem("scal_x")
        self.tq_y = sem("tq_y")
        self.nq = sem("nq")
        self.gu_ps = sem("gu_ps")
        self.gu_sb = sem("gu_sb")
        self.am_g = sem("am_g")
        self.ar_g = sem("ar_g")
        self.scal_g = sem("scal_g")
        self.sig_done = sem("sig_done")
        self.z_done = sem("z_done")
        self.am_z = sem("am_z")
        self.ar_z = sem("ar_z")
        self.scal_z = sem("scal_z")
        self.nzu_done = sem("nzu_done")
        self.p_done = sem("p_done")
        self.am_p = sem("am_p")
        self.ar_p = sem("ar_p")
        self.scal_p = sem("scal_p")
        self.tq_p = sem("tq_p")
        self.no_done = sem("no_done")
        self.dn_ps = sem("dn_ps")
        self.x2_done = sem("x2_done")
        self.mv_c = sem("mv_c")
        self.rstd_c = sem("rstd_c")
        self.y_c = sem("y_c")
        self.y3T_ps = sem("y3T_ps")
        self.y3T_sb = sem("y3T_sb")
        self.bo_added = sem("bo_added")
        self.near_sb = sem("near_sb")
        self.const_sb = sem("const_sb")
        self.q_ps = sem("q_ps")
        self.q_sb = sem("q_sb")
        self.s_ps = sem("s_ps")
        self.e_sub = sem("e_sub")
        self.e_exp = sem("e_exp")
        self.pT_ps = sem("pT_ps")
        self.pT_sb = sem("pT_sb")
        self.oT_ps = sem("oT_ps")
        self.oT_sb = sem("oT_sb")
        self.o_ps = sem("o_ps")
        self.att_sb = sem("att_sb")
        self.attT_ps = sem("attT_ps")
        self.attT_sb = sem("attT_sb")
        self.wo_ps = sem("wo_ps")
        self.x3_done = sem("x3_done")
        self.mv_d = sem("mv_d")
        self.rstd_d = sem("rstd_d")
        self.y_d = sem("y_d")
        self.y4T_ps = sem("y4T_ps")
        self.y4T_sb = sem("y4T_sb")
        self.lT_ps = sem("lT_ps")
        self.lT_sb = sem("lT_sb")
        self.lg_ps = sem("lg_ps")
        self.lx_sb = sem("lx_sb")
        self.ex_sb = sem("ex_sb")
        self.oh_sb = sem("oh_sb")
        self.cnt_ps = sem("cnt_ps")
        self.pos_sb = sem("pos_sb")
        self.scattered = sem("scattered")
        self.rows_in = sem("rows_in")
        self.more_rows_in = sem("more_rows_in")
        self.ys_sb = sem("ys_sb")
        self.ysT_ps = sem("ysT_ps")
        self.ysT_sb = sem("ysT_sb")
        self.h_ps = sem("h_ps")
        self.hb_sb = sem("hb_sb")
        self.gelu_sb = sem("gelu_sb")
        self.hT_ps = sem("hT_ps")
        self.hT_sb = sem("hT_sb")
        self.eo_ps = sem("eo_ps")
        self.res_sb = sem("res_sb")
        self.rows_out0 = sem("rows_out0")
        self.rows_out1 = sem("rows_out1")
        self.dve_step = sem("dve_step")
        self.act_step = sem("act_step")
        self.pool_step = sem("pool_step")
        self.dve_past = sem("dve_past")
        self.pool_past = sem("pool_past")


class Chain:

    def __init__(self, eng, sem):
        self.eng, self.sem, self.base, self.n = eng, sem, 0, 0

    def mark(self, ins):
        self.n += 1
        ins.then_inc(self.sem, 1)
        return self.base + self.n

    def link(self, ins):
        self.eng.wait_ge(self.sem, self.mark(ins))

    def enter(self, i, per):
        self.done, self.per = self.base + self.n, per
        self.base, self.n = self.done + i * per, 0

    def leave(self, times):
        assert self.n == self.per, (self.n, self.per)
        self.base, self.n = self.done + times * self.per, 0


def flamingo_kernel(nc, a, out):
    ctx = ExitStack()
    with ctx:
        def sb(name, shape, dt=F32):
            return ctx.enter_context(nc.sbuf_tensor(name, shape, dt))

        def sem(name):
            return ctx.enter_context(nc.semaphore(name))

        bank = [ctx.enter_context(nc.psum_tensor(f"bank{i}", [P, 512], F32)) for i in range(8)]
        pb = [b[:, :] for b in bank]

        rows_d = nc.dram_tensor("sorted_rows", [NS * P, ROW], F32).ap()
        ext_d = nc.dram_tensor("bias_by_distance", [H, EXT], F32).ap()

        X = sb("x_rows", [P, NT, ROW])
        XI = X[:, :, :].bitcast(I32)
        YT = sb("yT", [P, CH, NB * S])
        BIGG = sb("big_g", [P, FJ * NB * S])
        BIGU = sb("big_u", [P, FJ * NB * S])
        TMP = sb("tmp", [P, 6144])
        FW = sb("ffn_w", [P, 4608])
        GT = BIGG[:, :].rearrange("p (j n) -> p j n", j=FJ)
        UT_ = BIGU[:, :].rearrange("p (j n) -> p j n", j=FJ)

        def part(reg, off, shape, dt=F32):
            n = int(np.prod(shape[1:]))
            words = n if dt in (F32, I32) else n // 2
            v = reg[0:shape[0], off:off + words]
            if dt != F32:
                v = v.bitcast(dt)
            if len(shape) == 3:
                v = v.rearrange("p (a b) -> p a b", a=shape[1])
            if len(shape) == 4:
                v = v.rearrange("p (a b c) -> p a b c", a=shape[1], b=shape[2])
            return v

        ident = sb("ident", [P, P])
        flipb = sb("flipb", [P, P], BF16)
        ones = sb("ones", [P, P])
        onesb = sb("onesb", [P, P], BF16)
        before = sb("before", [P, P], BF16)
        headof = sb("headof", [P, 8])
        expand = part(BIGU, 10880, [H, D])
        mhalf = sb("mhalf", [P, NT])
        half = sb("half", [E, 1])
        warm = sb("warm", [1, 1])
        ids = sb("ids", [P, NT], I32)
        earlier = sb("earlier", [P, E, E])
        slot_i = part(BIGG, 4608, [P, NS, E - 1], I32)
        slot = sb("slot", [P, NS, E - 1])
        rank_i = part(BIGG, 4800, [P, E], I32)
        rank = sb("rank", [P, E])
        gates = sb("gates", [P, 4])
        tg = sb("tg", [P, 4])

        CTX = part(BIGU, 8192, [KEYS, NB, D])
        WK0 = part(BIGU, 0, [P, CH, D])
        WQ0 = part(BIGU, 512, [P, CH, D])
        WV0 = part(BIGU, 1024, [P, CH, D])
        bq0 = sb("bq0", [P, CH])
        bk0 = sb("bk0", [P, CH])
        bv0 = part(BIGU, 8704, [1, D])
        CTXT = part(BIGU, 8960, [P, CH, NB * KEYS])
        WQ0T = part(BIGU, 1536, [P, CH, D])
        K0T = part(BIGU, 2048, [P, CH, NB * KEYS])
        A0 = sb("a0", [P, CH, NB * KEYS])
        R0 = sb("r0", [1, NB * KEYS])
        V0 = sb("v0", [KEYS, NB, D])
        ya = part(BIGU, 3072, [P, 4, D])
        y2a = part(BIGU, 4096, [P, 4, D])
        yTa = part(BIGU, 5120, [P, 4, D])
        pa = part(BIGU, 6144, [P, 4, KEYS])
        pTa = part(BIGU, 6528, [KEYS, 4, P])
        stat = sb("stat", [P, 4, 6])
        mv = sb("mv", [P, 4, 2])
        ve = sb("ve", [P, 4])
        rstd = sb("rstd", [P, 4])
        nmax = sb("nmax", [P, 4])
        den = sb("den", [P, 4])
        rden = sb("rden", [P, 4])

        WN = part(TMP, 0, [P, 18 * 8, BLK])
        WUT = part(FW, 0, [P, CH, F])
        WGT = part(FW, CH * F, [P, CH, F])
        WDT = part(FW, 2 * CH * F, [P, FJ, D])
        WNI = part(BIGG, 8192, [P, 48, BLK])
        wamax = sb("wamax", [P, 144])
        wscale = sb("wscale", [P, 144])
        wrec = sb("wrec", [P, 144])
        amY = sb("amY", [P, NT])
        amG = sb("amG", [P, NQB * FJ])
        amU = sb("amU", [P, NQB * FJ])
        amZ = sb("amZ", [P, 2 * NQB])
        amP = sb("amP", [P, 2 * NQB])
        sc = sb("scalars", [P, 32])
        HF = 3 * QB
        ng = part(TMP, 0, [P, 2, HF], I16)
        sig = part(TMP, 2 * HF, [P, 2, HF])
        nz = part(TMP, 0, [P, 2, HF], I16)
        nu = part(TMP, HF, [P, 2, HF], I16)
        y3 = part(TMP, 0, [P, 4, D])

        WK1 = part(BIGU, 9280, [P, CH, D])
        WV1 = part(BIGU, 9792, [P, CH, D])
        WQ1 = sb("wq1", [P, CH, D])
        WO1 = sb("wo1", [P, CH, D])
        bq1 = sb("bq1", [P, CH])
        bk1 = sb("bk1", [P, CH])
        bv1 = part(BIGU, 10304, [1, D])
        bo1 = sb("bo1", [P, D])
        ls = sb("ls", [H, 1])
        els = sb("els", [H, 1])
        hscale = sb("hscale", [H, 1])
        cscale = sb("cscale", [P, CH])
        keep8 = sb("keep8", [P, NB * KEYS], U8)
        keep = part(BIGU, 10560, [P, NB * KEYS])
        K1T = sb("k1T", [P, CH, NB * KEYS])
        KBD = sb("k_blockdiag", [P, NB * CH * 8, KEYS])
        V1 = sb("v1", [KEYS, NB * H, VE])
        mrow8 = sb("mrow8", [1, NB * KEYS], U8)
        mrow = part(BIGU, 10720, [1, NB * KEYS])
        CM = sb("const_rows", [4, NB, HK], BF16)
        tab0 = sb("tab0", [1, H])
        tabT = part(BIGU, 7168, [H, 2 * MAXD + 1])
        ext = part(BIGU, 7680, [H, EXT])
        far3 = part(BIGU, 3072, [1, 3, HK], BF16)
        mask16 = part(TMP, 4656, [1, NB, HK], BF16)
        BN = part(TMP, 1024, [P, NEAR * 3, HK], BF16)
        bstage = part(TMP, 4736, [P, HK])

        e_ = part(BIGG, 8192, [P, 2, HK])
        qT = part(BIGG, 10752, [P, CH, 2 * P])
        att = part(BIGG, 11264, [P, 2, D])
        attT = part(BIGG, 11776, [P, 2, D])
        pT = part(BIGU, 8192, [KEYS, 2, H * P])
        oT = part(TMP, 0, [P, 2, NQ * P])
        rd = sb("rd", [P, 2, H])
        mx = sb("mx", [P, 2, HQ])

        WR = part(BIGU, 11136, [P, CH, G])
        WRT = part(BIGU, 11168, [G, D])
        wg = sb("wg", [E, G])
        wg2 = sb("wg2", [E, G])
        wgn = sb("wgn", [E, G])
        wss = sb("wss", [E, 3])
        WGNT = sb("wgnT", [G, E])
        GM = sb("gm", [P, CH, 32])
        W1 = part(BIGG, 0, [P, E * CH, HID])
        W2 = part(BIGU, 0, [P, E * HJ, D])
        B1 = part(FW, 0, [P, E * HID])
        B2 = part(TMP, 0, [P, E * D])
        y4 = part(TMP, 4736, [P, 4, D])
        lT = part(BIGG, 11264, [P, 2, P])
        y4T = part(BIGG, 9216, [P, 8, D])
        LG = part(BIGU, 8192, [P, NT, E])
        LX = part(BIGU, 8320, [P, NT, E])
        LM = sb("lm", [P, NT])
        OH = part(BIGU, 8448, [P, NT, E])
        OHB = sb("onehotb", [P, NT, E], BF16)
        CUM = part(BIGU, 8704, [P, NT, E])
        tot = sb("tot", [P, E])
        cnt_i = sb("cnt_i", [P, E], I32)
        tiles_e = sb("tiles_e", [P, E])
        start_e = sb("start_e", [P, E])
        start128 = sb("start128", [P, E])
        pos_i = sb("pos_i", [P, NT], I32)
        rid = sb("row_ids", [P, 2], I32)
        mv4 = sb("mv4", [P, NT, 2])
        ve4 = sb("ve4", [P, NT])
        rstd4 = sb("rstd4", [P, NT])
        eslot = sb("eslot", [P, NS])
        EXPS = sb("exp_of_slot", [P, NS], I32)
        YW = YT[:, :, :].rearrange("p a b -> p (a b)")
        rb = [part(BIGG, 8192, [P, NP + 1, ROW]), part(BIGU, 8192, [P, NP, ROW])]
        ys = part(YW, 0, [P, 2, D])
        ysT = part(YW, 512, [P, 2, D])
        hb = part(YW, 1024, [P, 2, HID])
        hT = part(YW, 2048, [P, 2, HID])
        res = part(YW, 3072, [P, 2, D])
        ob = part(YW, 3584, [P, 2, D])
        pad = part(BIGG, 4864, [P, ROW])

        NPB = TB // 2
        FAR = NPB - NEAR // 2

        def position(t):
            return t // TB * TB + (t - NEAR) % TB

        def tile_at(p):
            return p // TB * TB + (p + NEAR) % TB

        s = Signals(sem)
        block = ctx.enter_context(nc.Block())

        @block.sync
        def _(sp):
            def chunks(w):
                return w.rearrange("(c p) n -> p c n", p=P)

            def column(v):
                return v.rearrange("(c p) -> p c", p=P)

            def row(v):
                return v.rearrange("(a n) -> a n", a=1)

            sp.dma_start(CTX, a["ctx_1024"].rearrange("b k d -> k b d")).then_inc(s.ld_l0, 16)
            sp.dma_start(WK0, chunks(a["L0_xattn_Wk"])).then_inc(s.ld_l0, 16)
            sp.dma_start(WQ0, chunks(a["L0_xattn_Wq"])).then_inc(s.ld_l0, 16)
            sp.dma_start(WV0, chunks(a["L0_xattn_Wv"])).then_inc(s.ld_l0, 16)
            sp.dma_start(bk0[:, :], column(a["L0_xattn_bk"]), allow_slow_non_contiguous=True).then_inc(s.ld_l0, 16)
            sp.dma_start(bq0[:, :], column(a["L0_xattn_bq"]), allow_slow_non_contiguous=True).then_inc(s.ld_l0, 16)
            sp.dma_start(bv0, row(a["L0_xattn_bv"])).then_inc(s.ld_l0, 16)
            for n, g in enumerate(("g_xattn", "g_ffn")):
                sp.dma_start(gates[:, 2 * n:2 * n + 2], row(a[g]).to_broadcast([P, 2])).then_inc(s.ld_l0, 16)
            for b in range(NB):
                sp.dma_start(X[:, b * TB:(b + 1) * TB, 0:D],
                             a["x"][b].rearrange("(t p) d -> p t d", p=P)).then_inc((s.ld_x, s.ld_x1)[b], 16)
            for n, w in enumerate(("L0_ffn_w_gate", "L0_ffn_w_up")):
                sp.dma_start(WN[:, n * 48:(n + 1) * 48, :].rearrange("p (j q) k -> p j (q k)", j=FJ),
                             a[w].rearrange("(j p) c -> p j c", p=P)).then_inc(s.ld_ffn, 16)
            sp.dma_start(WN[:, 96:144, :].rearrange("p (j q) k -> p j (q k)", j=CH),
                         a["L0_ffn_w_down"].rearrange("(j p) c -> p j c", p=P)).then_inc(s.ld_ffn, 16)
            sp.dma_start(WK1, chunks(a["L1_xattn_Wk"])).then_inc(s.ld_l1, 16)
            sp.dma_start(WV1, chunks(a["L1_xattn_Wv"])).then_inc(s.ld_l1, 16)
            sp.dma_start(WQ1[:, :, :], chunks(a["L1_xattn_Wq"])).then_inc(s.ld_l1, 16)
            sp.dma_start(WO1[:, :, :], chunks(a["L1_xattn_Wo"])).then_inc(s.ld_l1, 16)
            sp.dma_start(bq1[:, :], column(a["L1_xattn_bq"]), allow_slow_non_contiguous=True).then_inc(s.ld_l1, 16)
            sp.dma_start(bk1[:, :], column(a["L1_xattn_bk"]), allow_slow_non_contiguous=True).then_inc(s.ld_l1, 16)
            sp.dma_start(bv1, row(a["L1_xattn_bv"])).then_inc(s.ld_l1, 16)
            sp.dma_start(bo1[:, :], row(a["L1_xattn_bo"]).to_broadcast([P, D])).then_inc(s.ld_l1, 16)
            sp.dma_start(ls[:, :], a["L1_xattn_logit_scale"].rearrange("(h a) -> h a", a=1)).then_inc(s.ld_l1, 16)
            mask = a["mask_BxS2_bf0"].rearrange("b k -> (b k)").rearrange("(a n) -> a n", a=1)
            sp.dma_start(keep8[:, :], mask.to_broadcast([P, NB * KEYS])).then_inc(s.ld_l1, 16)
            sp.dma_start(mrow8[:, :], mask).then_inc(s.ld_l1, 16)
            sp.dma_start(WR, chunks(a["L1_ffn_w_red"])).then_inc(s.ld_l1, 16)
            sp.dma_start(wg[:, :], a["L1_ffn_wg"]).then_inc(s.ld_l1, 16)
            sp.dma_start(tab0[:, :], a["L1_xattn_bias_table"][0:1, :]).then_inc(s.ld_l1, 16)
            sp.dma_start(tabT, a["L1_xattn_bias_table"].rearrange("r h -> h r"), allow_slow_non_contiguous=True).then_inc(s.ld_ext, 16)
            sp.wait_ge(s.pool_consts, 1)
            sp.dma_start(rows_d.rearrange("(t p) c -> p t c", p=P),
                         pad.unsqueeze(1).to_broadcast([P, NS, ROW])).then_inc(s.pads_written, 16)
            sp.wait_ge(s.ext_sb, 1)
            sp.dma_start(ext_d, ext).then_inc(s.ext_stored, 16)
            sp.wait_ge(s.const_sb, 1)
            sp.dma_start(CM[0:1, :, :], mask16).then_inc(s.ld_const, 16)
            for b in range(NB):
                for k in range(3):
                    sp.dma_start(CM[k + 1:k + 2, b, :], far3[:, k, :]).then_inc(s.ld_const, 16)
            sp.wait_ge(s.ext_stored, 16)
            sp.wait_ge(s.p_done, 2 + 2 * NQB)
            for n in range(NEAR):
                if n:
                    sp.wait_ge(s.near_sb, n)
                sp.dma_start(bstage.rearrange("p (h k) -> p h k", h=H),
                             bass.AP(tensor=ext_d.tensor, offset=EXT - KEYS - n * P - (P - 1),
                                     ap=[[1, P], [EXT, H], [1, KEYS]])).then_inc(s.ld_near, 16)
            sp.wait_ge(s.dn_ps, NT)
            sp.dma_start(W1.rearrange("p (e c) h -> p e c h", e=E),
                         a["L1_ffn_W1"].rearrange("e (c p) h -> p e c h", p=P)).then_inc(s.ld_w1, 16)
            sp.dma_start(W2.rearrange("p (e c) h -> p e c h", e=E),
                         a["L1_ffn_W2"].rearrange("e (c p) h -> p e c h", p=P)).then_inc(s.ld_w2, 16)
            sp.dma_start(B1, row(a["L1_ffn_b1"].rearrange("e h -> (e h)")).to_broadcast([P, E * HID])).then_inc(s.ld_b1, 16)
            sp.wait_ge(s.x3_done, NT)
            sp.dma_start(B2, row(a["L1_ffn_b2"].rearrange("e h -> (e h)")).to_broadcast([P, E * D])).then_inc(s.ld_b2, 16)
            sp.wait_ge(s.scattered, 16 * NT)
            rows_t = rows_d.rearrange("(t p) c -> p t c", p=P)
            for u in range(2):
                sp.dma_start(rb[u][:, 0, :], rows_t[:, u, :]).then_inc(s.rows_in, 16)
            for u in range(2):
                sp.dma_start(rb[u][:, 1:, :], rows_t[:, 2 + u::2, :]).then_inc(s.more_rows_in, 16)

        @block.gpsimd
        def _(pool):
            c = Chain(pool, s.pool_step)
            c.link(pool.memset(ident[:, :], 0.0))
            c.link(pool.memset(ones[:, :], 1.0))
            c.link(pool.affine_select(out=ident[:, :], in_=ident[:, :], compare_op=ALU.not_equal, fill=1.0,
                                      base=0, pattern=[[-1, P]], channel_multiplier=1))
            pool.tensor_copy(onesb[:, :], ones[:, :])
            c.link(pool.memset(flipb[:, :], 0.0))
            c.link(pool.affine_select(out=flipb[:, :], in_=flipb[:, :], compare_op=ALU.not_equal, fill=1.0,
                                      base=-(P - 1), pattern=[[1, P]], channel_multiplier=1))
            pool.memset(half[:, :], 0.5)
            pool.memset(warm[:, :], 0.0)
            pool.memset(GM[:, :, :], 0.0)
            pool.memset(mhalf[:, :], -0.5).then_inc(s.consts, 1)
            c.link(pool.affine_select(out=headof[:, :], in_=ones[:, 0:8], compare_op=ALU.is_ge, fill=0.0,
                                      base=0, pattern=[[-HD, 8]], channel_multiplier=1))
            c.link(pool.affine_select(out=headof[:, :], in_=headof[:, :], compare_op=ALU.is_ge, fill=0.0,
                                      base=HD - 1, pattern=[[HD, 8]], channel_multiplier=-1))
            c.link(pool.memset(expand, 1.0))
            c.link(pool.affine_select(out=expand, in_=expand, compare_op=ALU.is_ge, fill=0.0,
                                      base=0, pattern=[[1, D]], channel_multiplier=-HD))
            c.link(pool.affine_select(out=expand, in_=expand, compare_op=ALU.is_ge, fill=0.0,
                                      base=HD - 1, pattern=[[-1, D]], channel_multiplier=HD))
            c.link(pool.affine_select(out=before[:, :], in_=onesb[:, :], compare_op=ALU.is_gt, fill=0.0,
                                      base=0, pattern=[[1, P]], channel_multiplier=-1))
            c.link(pool.affine_select(out=earlier[:, :, :], in_=ones[:, 0:E * E].rearrange("p (a b) -> p a b", a=E),
                                      compare_op=ALU.is_gt, fill=0.0, base=0, pattern=[[1, E], [-1, E]],
                                      channel_multiplier=0))
            c.link(pool.iota(ids[:, :], pattern=[[P, NT]], base=0, channel_multiplier=1))
            c.link(pool.iota(slot_i, pattern=[[1, NS], [0, E - 1]], base=0, channel_multiplier=0))
            c.link(pool.iota(rank_i, pattern=[[-1, E]], base=E, channel_multiplier=0))
            pool.tensor_copy(slot[:, :, :], slot_i)
            pool.tensor_copy(rank[:, :], rank_i)
            c.link(pool.memset(pad, 0.0))
            pool.iota(pad[:, IDC:IDC + 1].bitcast(I32), pattern=[[0, 1]], base=NOWHERE,
                      channel_multiplier=0).then_inc(s.pool_consts, 1)
            def rstds(t, mv_ready, done, per):
                pool.wait_ge(mv_ready, t + 4)
                pool.sem_inc(s.pool_past, 1)
                c.link(pool.tensor_scalar(ve[:, :], mv[:, :, 1], EPS, None, ALU.add))
                pool.tensor_tensor(rstd[:, :], ve[:, :], mhalf[:, 0:4], ALU.pow).then_inc(done, 1)

            def rstds_of(a, b, ready, done, n):
                pool.wait_ge(ready, n)
                c.link(pool.tensor_scalar(ve4[:, a:b], mv4[:, a:b, 1], EPS, None, ALU.add))
                pool.tensor_tensor(rstd4[:, a:b], ve4[:, a:b], mhalf[:, a:b], ALU.pow).then_inc(done, 1)

            def quantised(n, part_):
                b = slice(48 * n, 48 * (n + 1))
                if part_ == 0:
                    pool.wait_ge(s.wstep_sb, n + 1)
                    if n:
                        pool.wait_ge(s.wq_sb, n)
                    pool.tensor_tensor(WNI, WN[:, b, :], wrec[:, b].unsqueeze(2).to_broadcast([P, 48, BLK]),
                                       ALU.mult).then_inc(s.wsteps_sb, 1)
                else:
                    pool.wait_ge(s.wround_sb, n + 1)
                    (pool.tensor_tensor(WN[:, b, :], WNI, wscale[:, b].unsqueeze(2).to_broadcast([P, 48, BLK]),
                                              ALU.mult)).then_inc(s.wq_sb, 1)

            for b in range(NB):
                rstds_of(b * TB, (b + 1) * TB, s.mv_a, s.rstd_a, (b + 1) * TB)
            for g in range(NT // 4):
                rstds(4 * g, s.mv_b, s.rstd_b, 2)
                if g:
                    quantised(g - 1, 1)
                if g < 3:
                    quantised(g, 0)
            pool.wait_ge(s.ld_l1, 16 * 14)
            pool.tensor_scalar(keep, keep8[:, :], -1.0, 1.0, ALU.mult, ALU.add).then_inc(s.keep_sb, 1)
            def all_max(k, ready, done):
                pool.wait_ge(ready, 1)
                pool.partition_all_reduce(sc[:, k + 1:k + 2], sc[:, k:k + 1], P,
                                          bass.bass_isa.ReduceOp.max).then_inc(done, 1)

            all_max(0, s.ax_sb, s.ar_x)
            c.link(pool.tensor_scalar(mrow, mrow8[:, :], NEG, None, ALU.mult))
            mrow3 = mrow.rearrange("p (b k) -> p b k", b=NB)
            for b in range(NB):
                pool.tensor_copy(mask16[:, b, :].rearrange("p (h k) -> p h k", h=H),
                                 mrow3[:, b, :].unsqueeze(1).to_broadcast([1, H, KEYS]))
            pool.wait_ge(s.y2T_ps, NT)
            for k in range(3):
                f3 = far3[:, k, :].rearrange("p (h k) -> p h k", h=H)
                ins = pool.tensor_copy(f3, tab0[:, :].unsqueeze(2).to_broadcast([1, H, KEYS]))
                if k < 2:
                    c.link(ins)
                    c.link(pool.tensor_tensor(tab0[:, :], tab0[:, :], f3[:, :, 0], ALU.subtract))
            ins.then_inc(s.const_sb, 1)
            pool.wait_ge(s.ld_ext, 16)
            c.link(pool.tensor_copy(ext[:, 0:MAXD - 1], tabT[:, 0:1].to_broadcast([H, MAXD - 1])))
            pool.tensor_copy(ext[:, MAXD - 1:EXT], tabT[:, 0:EXT - MAXD + 1]).then_inc(s.ext_sb, 1)
            pool.wait_ge(s.wss_sb, 1)
            pool.tensor_tensor(wss[:, 1:2], wss[:, 0:1], half[:, :], ALU.pow).then_inc(s.wnorm_sb, 1)
            all_max(2, s.am_g, s.ar_g)
            pool.wait_ge(s.k1_sb, 1)
            K1B = K1T[:, :, :].rearrange("p c (b k) -> p c b k", b=NB)
            for b in range(NB):
                for ci in range(CH):
                    n = (b * CH + ci) * 8
                    last = pool.tensor_tensor(KBD[:, n:n + 8, :],
                                              K1B[:, ci, b, :].unsqueeze(1).to_broadcast([P, 8, KEYS]),
                                              headof[:, :].unsqueeze(2).to_broadcast([P, 8, KEYS]), ALU.mult)
            last.then_inc(s.kbd_sb, 1)
            all_max(4, s.am_z, s.ar_z)
            all_max(6, s.am_u, s.ar_u)
            all_max(8, s.am_p, s.ar_p)
            with pool.Fori(0, NT // 4) as i:
                c.enter(i, 1)
                rstds(4 * i, s.mv_c, s.rstd_c, 1)
            c.leave(NT // 4)
            pool.wait_ge(s.wo_sb, 1)
            pool.wait_ge(s.y_c, NT)
            pool.tensor_tensor(X[:, :, 0:D], X[:, :, 0:D], bo1[:, :].unsqueeze(1).to_broadcast([P, NT, D]),
                               ALU.add).then_inc(s.bo_added, 1)
            for n in range(NEAR):
                pool.wait_ge(s.ld_near, 16 * (n + 1))
                for k in range(3):
                    ins = pool.tensor_copy(BN[:, 3 * n + k, :], bstage)
                    if k < 2:
                        c.link(ins)
                        c.link(pool.tensor_tensor(bstage, bstage, BN[:, 3 * n + k, :], ALU.subtract))
                ins.then_inc(s.near_sb, 1)
            rstds_of(0, TB, s.mv_d, s.rstd_d, TB)
            rstds_of(TB + NEAR, NT, s.mv_d, s.rstd_d, NT - NEAR)
            rstds_of(TB, TB + NEAR, s.mv_d, s.rstd_d, NT)
            pool.wait_ge(s.pads_written, 16)
            pool.wait_ge(s.pos_sb, 1)
            for t in range(NT):
                pool.indirect_dma_start(rows_d, bass.IndirectOffsetOnAxis(pos_i[:, t:t + 1], 0),
                                        X[:, t, :], None).then_inc(s.scattered, 16)

            def rows_out(u, t):
                pool.wait_ge(s.res_sb, 2 + t + 1)
                pool.sem_inc(s.pool_past, 1)
                pool.indirect_dma_start(out.rearrange("b s d -> (b s) d"),
                                        bass.IndirectOffsetOnAxis(rid[:, u:u + 1], 0),
                                        res[:, u, :], None, bounds_check=NB * S - 1,
                                        oob_is_err=False).then_inc(s.rows_out0 if u == 0 else s.rows_out1, 16)

            with pool.Fori(0, NS // 2) as i:
                rows_out(0, 2 * i)
                rows_out(1, 2 * i + 1)
            rows_out(0, NS - 1)
            pool.wait_ge(s.rows_out0, 16 * (NS // 2 + 1))
            pool.wait_ge(s.rows_out1, 16 * (NS // 2))

        @block.scalar
        def _(act):
            c = Chain(act, s.act_step)

            def copy(out_, in_, ready, n, done, **k):
                act.wait_ge(ready, n)
                act.activation(out_, in_, ACT.Copy, **k).then_inc(done, 1)

            act.wait_ge(s.consts, 1)
            act.wait_ge(s.ld_l0, 16 * 9)
            act.activation(tg[:, :], gates[:, :], ACT.Tanh).then_inc(s.tg_sb, 1)
            act.wait_ge(s.tg_sb, 1)
            copy(CTXT, pb[0][:, 0:2 * NB * KEYS].rearrange("p (c n) -> p c n", c=CH), s.ctxT_ps, 1, s.ctxT_sb)
            copy(WQ0T, pb[1].rearrange("p (c n) -> p c n", c=CH), s.wq0T_ps, 1, s.wq0T_sb)
            copy(A0[:, :, :], pb[3][:, 0:2 * NB * KEYS].rearrange("p (c n) -> p c n", c=CH), s.a0_ps, 1, s.a0_sb)
            copy(R0[:, :], pb[3][0:1, 320:320 + NB * KEYS], s.a0_ps, 1, s.a0_sb)
            copy(V0[:, :, :], pb[4][0:KEYS, :].rearrange("p (b n) -> p b n", b=NB), s.v0_ps, 1, s.v0_sb,
                 scale=tg[0:KEYS, 0:1])
            def yT_out(g):
                for u in range(4):
                    copy(yTa[:, u, :], pb[u][:, 0:D], s.yT_ps, 4 * g + u + 1, s.yT_sb)

            def y2T_out(g):
                for u in range(4):
                    t = 4 * g + u
                    copy(YT[:, :, t * P:(t + 1) * P], pb[u][:, 0:D].rearrange("p (c n) -> p c n", c=CH),
                         s.y2T_ps, t + 1, s.y2T_sb)
            def rounded(n):
                act.wait_ge(s.wsteps_sb, n + 1)
                c.link(act.activation(WNI, WNI, ACT.Copy, bias=MAGIC))
                act.activation(WNI, WNI, ACT.Copy, bias=-MAGIC).then_inc(s.wround_sb, 1)
            yT_out(0)
            for g in range(NT // 4):
                for u in range(4):
                    act.wait_ge(s.nmax_a, 4 * g + u + 1)
                    act.activation(pa[:, u, :], pb[4 + u][:, 0:KEYS], ACT.Exp, bias=nmax[:, u:u + 1],
                                   accum_out=den[:, u:u + 1]).then_inc(s.p0, 1)
                if g:
                    y2T_out(g - 1)
                for u in range(4):
                    copy(pTa[:, u, :], pb[u][0:KEYS, 0:P], s.pT0_ps, 4 * g + u + 1, s.pT0_sb)
                if g < NT // 4 - 1:
                    yT_out(g + 1)
                if g:
                    rounded(g - 1)
            act.wait_ge(s.ld_l1, 16 * 14)
            act.activation(els[:, :], ls[:, :], ACT.Exp).then_inc(s.els_sb, 1)
            y2T_out(NT // 4 - 1)
            for g in range(3):
                copy(FW[:, (3 + g) * 512:(4 + g) * 512], pb[g], s.wT_ps, g + 1, s.wT_sb)
            for q in range(NQB):
                copy(YT[:, :, q * QB:(q + 1) * QB], YT[:, :, q * QB:(q + 1) * QB], s.tq_y, q + 1, s.nq, bias=-MAGIC)
            act.sem_inc(s.gu_sb, FJ)
            act.wait_ge(s.pads_written, 16)
            act.wait_ge(s.wq_sb, 3)
            with act.Fori(0, NQB) as q:
                for j in range(FJ):
                    copy(GT[:, j, ds(q * QB, QB)], pb[j], s.gu_ps, FJ * q + j + 1, s.gu_sb)
            for g in range(6):
                w = g if g < 3 else g + 3
                copy(FW[:, w * 512:(w + 1) * 512], pb[(2, 3, 4)[g % 3]], s.wT_ps, 3 + g + 1, s.wT_sb)
            copy(V1[:, :, 0:HD], pb[7][0:KEYS, :].rearrange("p (n d) -> p n d", d=HD), s.v1_ps, 1, s.v1_sb)
            copy(WRT, pb[0][0:G, 0:D], s.wrT_ps, 1, s.wrT_sb)
            copy(WGNT[:, :], pb[0][0:G, D:D + E], s.wgT_ps, 1, s.wgT_sb)
            copy(GM[:, :, 0:E], pb[1][:, 0:CH * E].rearrange("p (c e) -> p c e", c=CH), s.gm_ps, 1, s.gm_sb)
            act.activation(warm[:, :], warm[:, :], ACT.Sigmoid)
            act.wait_ge(s.ld_const, 16 * 7)
            act.wait_ge(s.ext_stored, 16)
            act.wait_ge(s.scal_g, 1)
            with act.Fori(0, NQB) as q:
                c.enter(q, 2)
                for h in range(2):
                    act.wait_ge(s.z_done, 2 * q + h + 1)
                    n3 = ng[:, h, :].rearrange("p (j n) -> p j n", j=3)
                    c.link(act.activation(n3, GT[:, 3 * h:3 * h + 3, ds(q * QB, QB)], ACT.Copy,
                                          scale=sc[:, 13:14]))
                    act.activation(sig[:, h, :], ng[:, h, :], ACT.Sigmoid, scale=sc[:, 12:13]).then_inc(s.sig_done, 1)
                    for j in range(3 * h, 3 * h + 3):
                        copy(UT_[:, j, ds(q * QB, QB)], pb[j], s.gu_ps, FJ * (NQB + q) + j + 1, s.gu_sb)
            c.leave(NQB)
            act.wait_ge(s.scal_z, 1)
            with act.Fori(0, NQB) as q:
                for h in range(2):
                    act.wait_ge(s.p_done, 2 * q + h + 1)
                    act.activation(nz[:, h, :].rearrange("p (j n) -> p j n", j=3),
                                   GT[:, 3 * h:3 * h + 3, ds(q * QB, QB)], ACT.Copy, scale=sc[:, 15:16])
                    act.wait_ge(s.scal_u, 1)
                    act.activation(nu[:, h, :].rearrange("p (j n) -> p j n", j=3),
                                   UT_[:, 3 * h:3 * h + 3, ds(q * QB, QB)], ACT.Copy,
                                   scale=sc[:, 17:18]).then_inc(s.nzu_done, 1)

            def ints(q):
                copy(UT_[:, :, ds(q * HB, HB)], GT[:, :, ds(q * HB, HB)], s.tq_p, q + 1, s.no_done, bias=-MAGIC)

            def queries(t):
                act.wait_ge(s.q_ps, t + 2)
                for ci in range(CH):
                    ins = act.activation(qT[:, ci, :], pb[4][:, ci * 2 * P:(ci + 1) * 2 * P], ACT.Identity,
                                         bias=bq1[:, ci:ci + 1])
                ins.then_inc(s.q_sb, 2)

            def y3_out(q):
                for u in range(4):
                    o = position(4 * q + u) * P
                    ps = pb[u if q == NQB - 1 else 4 + u]
                    copy(YT[:, :, o:o + P], ps[:, 0:D].rearrange("p (c n) -> p c n", c=CH),
                         s.y3T_ps, 4 + 4 * q + u + 1, s.y3T_sb)
            with act.Fori(0, 2 * NQB) as q:
                ints(q)
            for q in range(NQB):
                if q == NQB - 1:
                    queries(0)
                y3_out(q)

            def weightsT(t, m):
                copy(pT[:, m // NQ, (m % NQ) * 512:(m % NQ + 1) * 512], pb[6 + m % 2][0:KEYS, :],
                     s.pT_ps, NQ * t + m + 1, s.pT_sb)

            def heads_out(t, u):
                copy(oT[:, u, :], pb[u], s.oT_ps, t + u + 1, s.oT_sb)

            def attended(t, u):
                copy(attT[:, u, :], pb[5][:, 0:D], s.attT_ps, t + u + 1, s.attT_sb)

            def pair(t, first=False, last=False):
                for k in range(2 * NQ):
                    if k >= 2:
                        weightsT(t, k - 2)
                    elif not first:
                        weightsT(t - 2, k + 6)
                    if k == 7:
                        heads_out(t, 0)
                        if not last:
                            queries(t + 2)
                    if k == 3 and not first:
                        heads_out(t - 2, 1)
                    e4 = e_[:, k // NQ, (k % NQ) * HQK:(k % NQ + 1) * HQK]
                    act.wait_ge(s.e_sub, NQ * t + k + 1)
                    act.activation(e4, e4, ACT.Exp).then_inc(s.e_exp, 1)
                    if k in (1, 5) and not first:
                        attended(t - 2, k // 4)

            for b in range(NB):
                pair(b * TB, first=b == 0)
                with act.Fori(1, FAR) as i:
                    pair(b * TB + 2 * i)
                pair(b * TB + 2 * FAR, last=b == NB - 1)
            for k in range(2):
                weightsT(NT - 2, k + 6)
            attended(NT - 2, 0)
            heads_out(NT - 2, 1)
            attended(NT - 2, 1)
            for g in range(NT // 4 + 1):
                if g < NT // 4:
                    for p in range(4 * g, 4 * g + 4):
                        if p >= 8:
                            act.wait_ge(s.lT_ps, g - 1)
                        copy(y4T[:, p % 8, :], pb[p % 4][:, 0:D], s.y4T_ps, p + 1, s.y4T_sb)
                if g:
                    if g > 2:
                        act.wait_ge(s.lg_ps, g - 2)
                    copy(lT[:, (g - 1) % 2, :], pb[4 + (g - 1) % 2][:, 0:P], s.lT_ps, g, s.lT_sb)
            act.wait_ge(s.lx_sb, 1)
            act.activation(LX, LX, ACT.Exp).then_inc(s.ex_sb, 1)

            def normalised(u, i):
                row = rb[u][:, ds(i, 1), :].rearrange("p a c -> p (a c)")
                act.activation(ys[:, u, :], row[:, 0:D], ACT.Identity, scale=row[:, RSTD:RSTD + 1],
                               bias=row[:, NMR:NMR + 1]).then_inc(s.ys_sb, 1)

            def transposed(u, i):
                copy(ysT[:, u, :], pb[u][:, 0:D], s.ysT_ps, 2 * i + u + 1, s.ysT_sb)

            def gelu(u, i):
                act.wait_ge(s.hb_sb, 2 * i + u + 1)
                act.activation(hb[:, u, :], hb[:, u, :], ACT.Gelu).then_inc(s.gelu_sb, 1)

            act.activation(warm[:, :], warm[:, :], ACT.Gelu)
            act.wait_ge(s.rows_in, 16 * 2)
            for u in range(2):
                normalised(u, 0)
            for u in range(2):
                transposed(u, 0)
            act.wait_ge(s.more_rows_in, 16 * 2)
            for u in range(2):
                normalised(u, 1)

            def step(i, now, nxt, nxt2):
                gelu(0, i)
                for u in nxt:
                    transposed(u, i + 1)
                if len(now) > 1:
                    gelu(1, i)
                for u in nxt2:
                    normalised(u, i + 2)
            with act.Fori(0, NP - 2) as i:
                step(i, (0, 1), (0, 1), (0, 1))
            step(NP - 2, (0, 1), (0, 1), (0,))
            step(NP - 1, (0, 1), (0,), ())
            step(NP, (0,), (), ())

        @block.vector
        def _(dve):
            c = Chain(dve, s.dve_step)

            def stats(tiles, ready, after=None):
                if after is not None:
                    dve.wait_ge(*after)
                    dve.sem_inc(s.dve_past, 1)
                marks = [c.mark(dve.bn_stats(stat[:, u, :], x)) for u, x in enumerate(tiles)]
                dve.wait_ge(s.dve_step, marks[3])
                dve.sem_inc(s.dve_past, 1)
                for u in range(4):
                    dve.bn_aggr(mv[:, u, :], stat[:, u, :]).then_inc(ready, 1)

            def normalise(u, y, x):
                return dve.tensor_scalar(y, x, mv[:, u, 0:1], rstd[:, u:u + 1], ALU.subtract, ALU.mult)

            def rows(t):
                return X[:, ds(t, 1), 0:D].rearrange("p a d -> p (a d)")

            def moments0(b):
                dve.wait_ge((s.ld_x, s.ld_x1)[b], 16)
                for t in range(b * TB, (b + 1) * TB):
                    if t % 4 == 0 and t:
                        dve.wait_ge(s.mv_a, t)
                    c.mark(dve.bn_stats(stat[:, t % 4, :], X[:, t, 0:D]))
                    if t % 4 == 3:
                        dve.wait_ge(s.dve_step, c.base + c.n)
                        for u in range(t - 3, t + 1):
                            dve.bn_aggr(mv4[:, u, :], stat[:, u % 4, :]).then_inc(s.mv_a, 1)

            def weight_steps(n):
                b = slice(48 * n, 48 * (n + 1))
                c.link(dve.tensor_reduce(wamax[:, b], WN[:, b, :], AX.X, ALU.max, apply_absolute_value=True))
                c.link(dve.tensor_scalar(wscale[:, b], wamax[:, b], 1.0 / 7.0, TINY, ALU.mult, ALU.max))
                dve.reciprocal(wrec[:, b], wscale[:, b]).then_inc(s.wstep_sb, 1)

            def y_in(g):
                for t in range(4 * g, 4 * g + 4):
                    if g:
                        dve.wait_ge(s.yT_ps, t - 3)
                    dve.tensor_scalar(ya[:, t % 4, :], X[:, t, 0:D], mv4[:, t, 0:1], rstd4[:, t:t + 1],
                                      ALU.subtract, ALU.mult).then_inc(s.y_a, 1)

            def y2_in(g):
                dve.wait_ge(s.rstd_b, g + 1)
                for u in range(4):
                    if g:
                        dve.wait_ge(s.y2T_ps, 4 * g + u - 3)
                    normalise(u, y2a[:, u, :], X[:, 4 * g + u, 0:D]).then_inc(s.y_b, 1)
                for u in range(4):
                    dve.wait_ge(s.y_b, 4 * g + u + 1)
                    c.mark(dve.tensor_reduce(amY[:, 4 * g + u:4 * g + u + 1], y2a[:, u, :], AX.X, ALU.max,
                                             apply_absolute_value=True))
            moments0(0)
            dve.wait_ge(s.ld_l0, 16 * 9)
            dve.wait_ge(s.k0_ps, 1)
            for ci in range(CH):
                ins = dve.tensor_scalar(K0T[:, ci, :], pb[2][:, ci * NB * KEYS:(ci + 1) * NB * KEYS],
                                        bk0[:, ci:ci + 1], D ** -0.5, ALU.add, ALU.mult)
            ins.then_inc(s.k0_sb, 1)
            dve.wait_ge(s.pool_consts, 1)
            dve.tensor_copy(XI[:, :, IDC], ids[:, :])
            dve.wait_ge(s.rstd_a, 1)
            y_in(0)
            moments0(1)
            dve.wait_ge(s.ld_ffn, 16 * 3)
            for g in range(NT // 4):
                for u in range(4):
                    dve.wait_ge(s.s0_ps, 4 * g + u + 1)
                    dve.tensor_reduce(nmax[:, u:u + 1], pb[4 + u][:, 0:KEYS], AX.X, ALU.max,
                                      negate=True).then_inc(s.nmax_a, 1)
                if g:
                    y2_in(g - 1)
                if g == TB // 4 - 1:
                    dve.wait_ge(s.rstd_a, 2)
                if g < NT // 4 - 1:
                    y_in(g + 1)
                    weight_steps(g)
                dve.wait_ge(s.p0, 4 * g + 4)
                c.link(dve.reciprocal(rden[:, :], den[:, :]))
                for u in range(4):
                    x = X[:, 4 * g + u, 0:D]
                    dve.wait_ge(s.o0_ps, 4 * g + u + 1)
                    dve.scalar_tensor_tensor(x, pb[4 + u][:, 0:D], rden[:, u:u + 1], x,
                                             ALU.mult, ALU.add).then_inc(s.x1_done, 1)
                stats([X[:, 4 * g + u, 0:D] for u in range(4)], s.mv_b, (s.x1_done, 4 * g + 4))
            y2_in(NT // 4 - 1)

            def scalar(k, in_, op0, s1, op1=None, s2=None):
                c.link(dve.tensor_scalar(sc[:, k:k + 1], in_, s1, s2, op0, op1 if op1 is not None else ALU.bypass))

            def step_of(k, amax, unit):
                if unit is None:
                    scalar(k, amax, ALU.mult, 1.0 / QMAX, ALU.max, TINY)
                    c.link(dve.reciprocal(sc[:, k + 1:k + 2], sc[:, k:k + 1]))
                else:
                    scalar(k, amax, ALU.mult, unit)
                    scalar(k, sc[:, k:k + 1], ALU.mult, 1.0 / QMAX, ALU.max, TINY)
                    c.link(dve.reciprocal(sc[:, k + 1:k + 2], sc[:, k:k + 1]))
                    scalar(k + 1, sc[:, k + 1:k + 2], ALU.mult, unit)

            dve.wait_ge(s.dve_step, c.base + c.n)
            dve.tensor_reduce(sc[:, 0:1], amY[:, :], AX.X, ALU.max).then_inc(s.ax_sb, 1)
            dve.wait_ge(s.ar_x, 1)
            step_of(10, sc[:, 1:2], None)
            dve.wait_ge(s.y2T_sb, NT)
            for q in range(NQB):
                dve.tensor_scalar(YT[:, :, q * QB:(q + 1) * QB], YT[:, :, q * QB:(q + 1) * QB], sc[:, 11:12], MAGIC,
                                  ALU.mult, ALU.add).then_inc(s.tq_y, 1)
            dve.wait_ge(s.els_sb, 1)
            dve.tensor_scalar(hscale[:, :], els[:, :], 4.0, HD ** -0.5, ALU.min, ALU.mult).then_inc(s.hsc_sb, 1)
            c.link(dve.tensor_tensor(wg2[:, :], wg[:, :], wg[:, :], ALU.mult))
            dve.tensor_reduce(wss[:, 0:1], wg2[:, :], AX.X, ALU.add).then_inc(s.wss_sb, 1)
            dve.memset(V1[:, :, HD:HD + 1], 1.0)
            dve.memset(V1[:, :, HD + 1:VE], 0.0)
            c.link(dve.tensor_scalar(WO1[:, :, :], WO1[:, :, :], tg[:, 1:2], None, ALU.mult))
            dve.tensor_scalar(bo1[:, :], bo1[:, :], tg[:, 1:2], None, ALU.mult).then_inc(s.wo_sb, 1)
            with dve.Fori(0, NQB) as q:
                c.enter(q, FJ)
                for j in range(FJ):
                    dve.wait_ge(s.gu_sb, FJ + FJ * q + j + 1)
                    c.mark(dve.tensor_reduce(amG[:, ds(FJ * q + j, 1)], GT[:, j, ds(q * QB, QB)], AX.X, ALU.max,
                                             apply_absolute_value=True))
            c.leave(NQB)
            dve.wait_ge(s.dve_step, c.base)
            dve.tensor_reduce(sc[:, 2:3], amG[:, :], AX.X, ALU.max).then_inc(s.am_g, 1)
            dve.wait_ge(s.csc_ps, 1)
            c.link(dve.tensor_copy(cscale[:, :], pb[5][:, 0:CH]))
            dve.wait_ge(s.k1_ps, 1)
            dve.wait_ge(s.keep_sb, 1)
            for ci in range(CH):
                c.link(dve.tensor_scalar(K1T[:, ci, :], pb[6][:, ci * NB * KEYS:(ci + 1) * NB * KEYS],
                                         bk1[:, ci:ci + 1], cscale[:, ci:ci + 1], ALU.add, ALU.mult))
            dve.tensor_tensor(K1T[:, :, :], K1T[:, :, :], keep.unsqueeze(1).to_broadcast([P, CH, NB * KEYS]),
                              ALU.mult).then_inc(s.k1_sb, 1)
            dve.wait_ge(s.wnorm_sb, 1)
            c.link(dve.tensor_scalar(wss[:, 1:2], wss[:, 1:2], 1e-4, None, ALU.max))
            c.link(dve.reciprocal(wss[:, 2:3], wss[:, 1:2]))
            dve.tensor_scalar(wgn[:, :], wg[:, :], wss[:, 2:3], None, ALU.mult).then_inc(s.wgn_sb, 1)
            dve.wait_ge(s.ar_g, 1)
            step_of(12, sc[:, 3:4], sc[:, 10:11])
            dve.sem_inc(s.z_done, 2)
            dve.sem_inc(s.scal_g, 1)
            def half(h):
                return slice(3 * h, 3 * h + 3)

            def rounded(q, h):
                dve.wait_ge(s.sig_done, 2 * q + h + 1)
                return c.mark(dve.tensor_scalar(sig[:, h, :], sig[:, h, :], (U16 - 1) / U16, MAGIC / U16,
                                                ALU.min, ALU.add))

            def gated(q, h, mark):
                dve.wait_ge(s.dve_step, mark)
                dve.scalar_tensor_tensor(GT[:, half(h), ds(q * QB, QB)], sig[:, h, :].rearrange("p (j n) -> p j n", j=3),
                                         MAGIC / U16, ng[:, h, :].rearrange("p (j n) -> p j n", j=3),
                                         ALU.subtract, ALU.mult).then_inc(s.z_done, 1)

            def largest_gated(q, h):
                dve.wait_ge(s.z_done, 2 + 2 * q + h + 1)
                c.mark(dve.tensor_reduce(amZ[:, ds(2 * q + h, 1)], GT[:, half(h), ds(q * QB, QB)], AX.XY, ALU.max,
                                         apply_absolute_value=True))

            def largest_up(q, h):
                for j in range(3 * h, 3 * h + 3):
                    dve.wait_ge(s.gu_sb, FJ + FJ * (NQB + q) + j + 1)
                    c.mark(dve.tensor_reduce(amU[:, ds(FJ * q + j, 1)], UT_[:, j, ds(q * QB, QB)], AX.X, ALU.max,
                                             apply_absolute_value=True))
            with dve.Fori(0, NQB) as q:
                c.enter(q, FJ + 4)
                mark0 = rounded(q, 0)
                largest_up(q, 0)
                gated(q, 0, mark0)
                mark1 = rounded(q, 1)
                largest_gated(q, 0)
                gated(q, 1, mark1)
                largest_up(q, 1)
                largest_gated(q, 1)
            c.leave(NQB)
            dve.wait_ge(s.dve_step, c.base)
            dve.tensor_reduce(sc[:, 4:5], amZ[:, :], AX.X, ALU.max).then_inc(s.am_z, 1)
            dve.tensor_reduce(sc[:, 6:7], amU[:, :], AX.X, ALU.max).then_inc(s.am_u, 1)
            dve.wait_ge(s.ar_z, 1)
            dve.sem_inc(s.p_done, 2)
            step_of(14, sc[:, 5:6], sc[:, 12:13])
            dve.sem_inc(s.scal_z, 1)
            dve.wait_ge(s.ar_u, 1)
            step_of(16, sc[:, 7:8], sc[:, 10:11])
            dve.sem_inc(s.scal_u, 1)
            scalar(18, sc[:, 14:15], ALU.mult, sc[:, 16:17])
            with dve.Fori(0, NQB) as q:
                c.enter(q, 2)
                for h in range(2):
                    dve.wait_ge(s.nzu_done, 2 * q + h + 1)
                    dve.tensor_tensor(GT[:, half(h), ds(q * QB, QB)], nz[:, h, :].rearrange("p (j n) -> p j n", j=3),
                                      nu[:, h, :].rearrange("p (j n) -> p j n", j=3), ALU.mult).then_inc(s.p_done, 1)
                for h in range(2):
                    dve.wait_ge(s.p_done, 2 + 2 * q + h + 1)
                    c.mark(dve.tensor_reduce(amP[:, ds(2 * q + h, 1)], GT[:, half(h), ds(q * QB, QB)], AX.XY, ALU.max,
                                             apply_absolute_value=True))
            c.leave(NQB)
            dve.wait_ge(s.dve_step, c.base)
            dve.tensor_reduce(sc[:, 8:9], amP[:, :], AX.X, ALU.max).then_inc(s.am_p, 1)
            dve.wait_ge(s.ar_p, 1)
            step_of(19, sc[:, 9:10], sc[:, 18:19])
            with dve.Fori(0, 2 * NQB) as q:
                b = GT[:, :, ds(q * HB, HB)]
                dve.tensor_scalar(b, b, sc[:, 20:21], MAGIC, ALU.mult, ALU.add).then_inc(s.tq_p, 1)
            scalar(21, sc[:, 19:20], ALU.mult, tg[:, 2:3])
            with dve.Fori(0, NT // 4) as i:
                c.enter(i, 4)
                t = 4 * i
                for u in range(4):
                    dve.wait_ge(s.dn_ps, t + u + 1)
                    dve.scalar_tensor_tensor(rows(t + u), pb[u][:, 0:D], sc[:, 21:22], rows(t + u),
                                             ALU.mult, ALU.add).then_inc(s.x2_done, 1)
                stats([rows(t + u) for u in range(4)], s.mv_c, (s.x2_done, t + 4))
                dve.wait_ge(s.rstd_c, i + 1)
                for u in range(4):
                    dve.wait_ge(s.y3T_ps, t + u + 1)
                    normalise(u, y3[:, u, :], rows(t + u)).then_inc(s.y_c, 1)
            c.leave(NT // 4)

            def head_out(t, u):
                dve.wait_ge(s.o_ps, t + u + 1)
                o = pb[u][:, 0:H * VE].rearrange("p (h d) -> p h d", d=VE)
                c.link(dve.reciprocal(rd[:, u, :], o[:, :, HD]))
                dve.tensor_tensor(att[:, u, :].rearrange("p (h d) -> p h d", d=HD), o[:, :, 0:HD],
                                  rd[:, u, :].unsqueeze(2).to_broadcast([P, H, HD]), ALU.mult).then_inc(s.att_sb, 1)

            def residual(t, tile, u):
                dve.wait_ge(s.wo_ps, t + u + 1)
                dve.tensor_tensor(rows(tile + u), pb[5][:, 0:D], rows(tile + u), ALU.add).then_inc(s.x3_done, 1)

            def moments(t, tile):
                dve.wait_ge(s.x3_done, t + 2)
                dve.sem_inc(s.dve_past, 1)
                for u in range(2):
                    mk = c.mark(dve.bn_stats(stat[:, u, :], rows(tile + u)))
                dve.wait_ge(s.dve_step, mk)
                dve.sem_inc(s.dve_past, 1)
                for u in range(2):
                    mk = c.mark(dve.bn_aggr(mv[:, u, :], stat[:, u, :]))
                dve.wait_ge(s.dve_step, mk)
                dve.tensor_copy(mv4[:, ds(tile, 2), :], mv[:, 0:2, :]).then_inc(s.mv_d, 2)

            def pair(t, before):
                for k in range(2 * NQ):
                    u, hq = k // NQ, k % NQ
                    if before is not None:
                        if k in (0, 4):
                            head_out(t - 2, k // 4)
                        if k == 3:
                            dve.wait_ge(s.bo_added, 1)
                        if k in (3, 7):
                            residual(t - 2, before, k // 4)
                    s4 = pb[2 + k % 2][:, 0:HQK].rearrange("p (h k) -> p h k", h=HQ)
                    m4 = mx[:, k % 2, :]
                    dve.wait_ge(s.s_ps, NQ * t + k + 1)
                    c.link(dve.tensor_reduce(m4, s4, AX.X, ALU.max))
                    dve.tensor_tensor(e_[:, u, hq * HQK:(hq + 1) * HQK].rearrange("p (h k) -> p h k", h=HQ), s4,
                                      m4.unsqueeze(2).to_broadcast([P, HQ, KEYS]), ALU.subtract).then_inc(s.e_sub, 1)
                if before is not None:
                    moments(t - 2, before)

            per = 2 * NQ + 6
            for b in range(NB):
                pair(b * TB, (b - 1) * TB if b else None)
                with dve.Fori(1, FAR) as i:
                    c.enter(i - 1, per)
                    pair(b * TB + 2 * i, b * TB + NEAR + 2 * i - 2)
                c.leave(FAR - 1)
                pair(b * TB + 2 * FAR, b * TB + TB - 2)
            head_out(NT - 2, 0)
            residual(NT - 2, (NB - 1) * TB, 0)
            head_out(NT - 2, 1)

            def router_in(a, b):
                for p in range(a, b):
                    t = tile_at(p)
                    dve.wait_ge(s.rstd_d, 1 if p < TB else 2 if p < NT - NEAR else 3)
                    if p >= 4:
                        dve.wait_ge(s.y4T_ps, p - 3)
                    dve.tensor_scalar(y4[:, p % 4, :], X[:, t, 0:D], mv4[:, t, 0:1], rstd4[:, t:t + 1],
                                      ALU.subtract, ALU.mult).then_inc(s.y_d, 1)
            dve.wait_ge(s.near_sb, NEAR)
            router_in(0, 4)
            residual(NT - 2, (NB - 1) * TB, 1)
            moments(NT - 2, (NB - 1) * TB)
            router_in(4, NT)
            dve.tensor_copy(X[:, :, RSTD], rstd4[:, :])
            dve.scalar_tensor_tensor(X[:, :, NMR], mv4[:, :, 0], -1.0, rstd4[:, :], ALU.mult, ALU.mult)
            dve.wait_ge(s.lg_ps, NT // 4)
            lg = pb[6][:, 0:NT * 32].rearrange("p (b t e) -> p b t e", b=NB, t=TB)
            LGB = LG.rearrange("p (b t) e -> p b t e", b=NB)
            dve.tensor_copy(LGB[:, :, NEAR:TB, :], lg[:, :, 0:TB - NEAR, 0:E])
            c.link(dve.tensor_copy(LGB[:, :, 0:NEAR, :], lg[:, :, TB - NEAR:TB, 0:E]))
            c.link(dve.tensor_reduce(LM[:, :], LG, AX.X, ALU.max))
            LMB = LM[:, :].unsqueeze(2).to_broadcast([P, NT, E])
            dve.tensor_tensor(LX, LG, LMB, ALU.subtract).then_inc(s.lx_sb, 1)
            c.link(dve.tensor_tensor(OH, LG, LMB, ALU.is_ge))
            c.link(dve.tensor_tensor(OH, OH, rank[:, :].unsqueeze(1).to_broadcast([P, NT, E]), ALU.mult))
            c.link(dve.tensor_reduce(LM[:, :], OH, AX.X, ALU.max))
            c.link(dve.tensor_tensor(OH, OH, LMB, ALU.is_equal))
            dve.tensor_copy(OHB[:, :, :], OH).then_inc(s.oh_sb, 1)
            dve.wait_ge(s.ex_sb, 1)
            c.link(dve.tensor_reduce(LM[:, :], LX, AX.X, ALU.add))
            c.link(dve.reciprocal(LM[:, :], LM[:, :]))
            dve.tensor_scalar(X[:, :, COEF], LM[:, :], tg[:, 3:4], None, ALU.mult)
            dve.wait_ge(s.cnt_ps, 1)
            c.link(dve.tensor_reduce(tot[:, :], pb[1][:, 0:NT * E].rearrange("p (t e) -> p e t", e=E), AX.X, ALU.add))
            c.link(dve.tensor_scalar(cnt_i[:, :], tot[:, :], float(P - 1), None, ALU.add))
            c.link(dve.tensor_scalar(cnt_i[:, :], cnt_i[:, :], 7, None, ALU.arith_shift_right))
            c.link(dve.tensor_copy(tiles_e[:, :], cnt_i[:, :]))
            c.link(dve.tensor_tensor(earlier[:, :, :], earlier[:, :, :], tiles_e[:, :].unsqueeze(1).to_broadcast([P, E, E]),
                                     ALU.mult))
            c.link(dve.tensor_reduce(start_e[:, :], earlier[:, :, :], AX.X, ALU.add))
            c.link(dve.tensor_scalar(start128[:, :], start_e[:, :], float(P), None, ALU.mult))
            c.link(dve.tensor_tensor(CUM, pb[0][:, 0:NT * E].rearrange("p (t e) -> p t e", e=E),
                                     start128[:, :].unsqueeze(1).to_broadcast([P, NT, E]), ALU.add))
            c.link(dve.tensor_tensor(CUM, CUM, OH, ALU.mult))
            c.link(dve.tensor_reduce(LM[:, :], CUM, AX.X, ALU.add))
            dve.tensor_copy(pos_i[:, :], LM[:, :]).then_inc(s.pos_sb, 1)
            c.link(dve.tensor_tensor(slot[:, :, :], slot[:, :, :],
                                     start_e[:, 1:E].unsqueeze(1).to_broadcast([P, NS, E - 1]), ALU.is_ge))
            c.link(dve.tensor_reduce(eslot[:, :], slot[:, :, :], AX.X, ALU.add))
            dve.tensor_copy(EXPS[:, :], eslot[:, :]).then_inc(s.slots_sb, 1)
            dve.wait_ge(s.slots_sb, 1)
            dve.wait_ge(s.ld_b1, 16)
            dve.wait_ge(s.ld_b2, 16)

            def bias1(u, i):
                e = dve.value_load(EXPS[0:1, ds(2 * i + u, 1)], min_val=0, max_val=E - 1)
                dve.wait_ge(s.h_ps, 2 * i + u + 1)
                dve.tensor_tensor(hb[:, u, :], pb[2 + u], B1[:, ds(e * HID, HID)], ALU.add).then_inc(s.hb_sb, 1)

            def hidden(u, i):
                dve.wait_ge(s.hT_ps, 2 * i + u + 1)
                dve.tensor_copy(hT[:, u, :], pb[4 + u]).then_inc(s.hT_sb, 1)

            def result(u, i, first=False):
                row = rb[u][:, ds(i, 1), :].rearrange("p a c -> p (a c)")
                e = dve.value_load(EXPS[0:1, ds(2 * i + u, 1)], min_val=0, max_val=E - 1)
                if not first:
                    dve.wait_ge(s.rows_out0 if u == 0 else s.rows_out1, 16 * i)
                dve.tensor_copy(rid[:, u:u + 1], row[:, IDC:IDC + 1].bitcast(I32))
                dve.wait_ge(s.eo_ps, 2 * i + u + 1)
                c.link(dve.tensor_tensor(ob[:, u, :], pb[6 + u][:, 0:D], B2[:, ds(e * D, D)], ALU.add))
                dve.scalar_tensor_tensor(res[:, u, :], ob[:, u, :], row[:, COEF:COEF + 1], row[:, 0:D],
                                         ALU.mult, ALU.add).then_inc(s.res_sb, 1)

            def step(i, now, prev, first=False):
                for u in now:
                    bias1(u, i)
                for u in prev:
                    result(u, i - 1, first)
                for u in now:
                    hidden(u, i)
            dve.sem_inc(s.res_sb, 2)
            dve.wait_ge(s.rows_in, 16 * 2)
            dve.wait_ge(s.more_rows_in, 16 * 2)
            step(0, (0, 1), ())
            c.enter(0, 2)
            step(1, (0, 1), (0, 1), True)
            c.leave(1)
            with dve.Fori(2, NP) as i:
                c.enter(i - 2, 2)
                step(i, (0, 1), (0, 1))
            c.leave(NP - 2)
            c.enter(0, 3)
            step(NP, (0,), (0, 1))
            step(NP + 1, (), (0,))
            c.leave(1)

        @block.tensor
        def _(pe):
            def mm(out_, lhsT, rhs, first, last):
                return pe.matmul(out_, lhsT=lhsT, rhs=rhs, start=first, stop=last)

            pe.wait_ge(s.consts, 1)
            pe.wait_ge(s.ld_l0, 16 * 9)
            for ci in range(CH):
                for b in range(NB):
                    o = (ci * NB + b) * KEYS
                    ins = pe.transpose(pb[0][:, o:o + KEYS], CTX[:, b, ci * P:(ci + 1) * P], ident[0:KEYS, 0:KEYS])
            ins.then_inc(s.ctxT_ps, 1)
            for dj in range(CH):
                for ci in range(CH):
                    ins = pe.transpose(pb[1][:, dj * D + ci * P:dj * D + (ci + 1) * P],
                                       WQ0[:, ci, dj * P:(dj + 1) * P], ident[:, :])
            ins.then_inc(s.wq0T_ps, 1)

            def keysT(ps, w, done):
                for dj in range(CH):
                    for ci in range(CH):
                        ins = mm(ps[:, dj * NB * KEYS:(dj + 1) * NB * KEYS], w[:, ci, dj * P:(dj + 1) * P],
                                 CTXT[:, ci, :], ci == 0, ci == CH - 1)
                ins.then_inc(done, 1)

            def values(ps, w, bias, done):
                for b in range(NB):
                    for ci in range(CH):
                        mm(ps[0:KEYS, b * D:(b + 1) * D], CTXT[:, ci, b * KEYS:(b + 1) * KEYS], w[:, ci, :], ci == 0, False)
                    ins = mm(ps[0:KEYS, b * D:(b + 1) * D], ones[0:1, 0:KEYS], bias, False, True)
                ins.then_inc(done, 1)

            pe.wait_ge(s.ctxT_sb, 1)
            keysT(pb[2], WK0, s.k0_ps)
            values(pb[4], WV0, bv0, s.v0_ps)
            pe.wait_ge(s.wq0T_sb, 1)
            pe.wait_ge(s.k0_sb, 1)
            for ci in range(CH):
                for dj in range(CH):
                    mm(pb[3][:, ci * NB * KEYS:(ci + 1) * NB * KEYS], WQ0T[:, dj, ci * P:(ci + 1) * P], K0T[:, dj, :],
                       dj == 0, dj == CH - 1)
            for dj in range(CH):
                ins = mm(pb[3][0:1, 320:320 + NB * KEYS], bq0[:, dj:dj + 1], K0T[:, dj, :], dj == 0, dj == CH - 1)
            ins.then_inc(s.a0_ps, 1)
            pe.wait_ge(s.a0_sb, 2)
            pe.wait_ge(s.v0_sb, 1)

            def transposed(ps, y, done):
                for ci in range(CH):
                    ins = pe.transpose(ps[:, ci * P:(ci + 1) * P], y[:, ci * P:(ci + 1) * P], ident[:, :])
                ins.then_inc(done, 1)

            def y_in(g):
                for t in range(4 * g, 4 * g + 4):
                    pe.wait_ge(s.y_a, t + 1)
                    transposed(pb[t % 4], ya[:, t % 4, :], s.yT_ps)

            def y2_in(g):
                for t in range(4 * g, 4 * g + 4):
                    pe.wait_ge(s.y_b, t + 1)
                    transposed(pb[t % 4], y2a[:, t % 4, :], s.y2T_ps)
            y_in(0)
            for g in range(NT // 4):
                b = 4 * g // TB
                sl = slice(b * KEYS, (b + 1) * KEYS)
                for u in range(4):
                    pe.wait_ge(s.yT_sb, 4 * g + u + 1)
                    if g:
                        pe.wait_ge(s.x1_done, 4 * g - 3 + u)
                    for ci in range(CH):
                        mm(pb[4 + u][:, 0:KEYS], yTa[:, u, ci * P:(ci + 1) * P], A0[:, ci, sl], ci == 0, False)
                    mm(pb[4 + u][:, 0:KEYS], ones[0:1, :], R0[:, sl], False, True).then_inc(s.s0_ps, 1)
                if g:
                    y2_in(g - 1)
                for u in range(4):
                    if g:
                        pe.wait_ge(s.y2T_sb, 4 * g - 3 + u)
                    pe.wait_ge(s.p0, 4 * g + u + 1)
                    pe.transpose(pb[u][0:KEYS, 0:P], pa[:, u, :], ident[:, :]).then_inc(s.pT0_ps, 1)
                for u in range(4):
                    pe.wait_ge(s.pT0_sb, 4 * g + u + 1)
                    mm(pb[4 + u][:, 0:D], pTa[:, u, :], V0[:, b, :], True, True).then_inc(s.o0_ps, 1)
                if g < NT // 4 - 1:
                    y_in(g + 1)
            y2_in(NT // 4 - 1)
            pe.wait_ge(s.y2T_sb, NT)
            WF = TMP[:, 0:4608]
            src = [1536 + j * D + ci * P for ci in range(CH) for j in range(FJ)]
            src += [j * D + ci * P for ci in range(CH) for j in range(FJ)]
            src += [3072 + o * F + j * P for j in range(FJ) for o in range(CH)]

            def weightsT(w, ps):
                for k in range(4):
                    ins = pe.transpose(ps[:, k * P:(k + 1) * P], WF[:, src[4 * w + k]:src[4 * w + k] + P], ident[:, :])
                ins.then_inc(s.wT_ps, 1)
            pe.wait_ge(s.wq_sb, 1)
            for g in range(3):
                weightsT(3 + g, pb[g])
            pe.wait_ge(s.wT_sb, 3)

            def layer1_operands():
                pe.wait_ge(s.gu_sb, FJ + FJ * NQB)
                pe.wait_ge(s.wq_sb, 3)
                for g in range(6):
                    if g >= 3:
                        pe.wait_ge(s.wT_sb, 3 + g - 2)
                    weightsT(g if g < 3 else g + 3, pb[(2, 3, 4)[g % 3]])
                pe.wait_ge(s.ld_l1, 16 * 14)
                pe.wait_ge(s.pool_consts, 1)
                pe.wait_ge(s.hsc_sb, 1)
                for ci in range(CH):
                    ins = mm(pb[5][:, ci:ci + 1], expand[:, ci * P:(ci + 1) * P], hscale[:, :], True, True)
                ins.then_inc(s.csc_ps, 1)
                keysT(pb[6], WK1, s.k1_ps)
                values(pb[7], WV1, bv1, s.v1_ps)
                for ci in range(CH):
                    ins = pe.transpose(pb[0][0:G, ci * P:(ci + 1) * P], WR[:, ci, :], ident[:, :])
                ins.then_inc(s.wrT_ps, 1)
                pe.wait_ge(s.wgn_sb, 1)
                pe.wait_ge(s.wrT_sb, 1)
                pe.transpose(pb[0][0:G, D:D + E], wgn[:, :], ident[0:E, 0:E]).then_inc(s.wgT_ps, 1)
                pe.wait_ge(s.wgT_sb, 1)
                for ci in range(CH):
                    ins = mm(pb[1][:, ci * E:(ci + 1) * E], WRT[:, ci * P:(ci + 1) * P], WGNT[:, :], True, True)
                ins.then_inc(s.gm_ps, 1)
                pe.wait_ge(s.gm_sb, 1)
                pe.wait_ge(s.k1_sb, 1)
                pe.wait_ge(s.wT_sb, 9)

            for n, w in enumerate((WGT, WUT)):
                if n:
                    layer1_operands()
                with pe.Fori(0, NQB) as q:
                    if n == 0:
                        pe.wait_ge(s.nq, q + 1)
                    for j in range(FJ):
                        pe.wait_ge(s.gu_sb, FJ * (n * NQB + q) + j + 1)
                        for ci in range(CH):
                            ins = mm(pb[j], w[:, ci, j * P:(j + 1) * P], YT[:, ci, ds(q * QB, QB)], ci == 0, ci == CH - 1)
                        ins.then_inc(s.gu_ps, 1)

            def down(q):
                for u in range(4):
                    t = 4 * q + u
                    pe.wait_ge(s.no_done, t // 2 + 1)
                    if q:
                        pe.wait_ge(s.x2_done, t - 3)
                    for j in range(FJ):
                        ins = mm(pb[u][:, 0:D], UT_[:, j, t * P:(t + 1) * P], WDT[:, j, :], j == 0, j == FJ - 1)
                    ins.then_inc(s.dn_ps, 1)

            def queries(t):
                for dj in range(CH):
                    for ci in range(CH):
                        ins = mm(pb[4][:, dj * 2 * P:(dj + 1) * 2 * P], WQ1[:, ci, dj * P:(dj + 1) * P],
                                 YT[:, ci, ds(t * P, 2 * P)], ci == 0, ci == CH - 1)
                ins.then_inc(s.q_ps, 2)

            def y3_in(q):
                for u in range(4):
                    pe.wait_ge(s.y_c, 4 * q + u + 1)
                    if q:
                        pe.wait_ge(s.y3T_sb, 4 * q + u - 3)
                    transposed(pb[u if q == NQB - 1 else 4 + u], y3[:, u, :], s.y3T_ps)
            pe.wait_ge(s.gu_sb, FJ + 2 * FJ * NQB)
            pe.sem_inc(s.y3T_ps, 4)
            for q in range(NQB):
                down(q)
                if q:
                    y3_in(q - 1)
            pe.wait_ge(s.y3T_sb, 4 * NQB - 7)
            queries(0)
            y3_in(NQB - 1)

            def scores(b, k, near):
                u, hq = k // NQ, k % NQ
                ps = pb[2 + k % 2][:, 0:HQK]
                cols = slice(hq * HQK, (hq + 1) * HQK)
                ci, n = hq // 2, (b * CH + hq // 2) * 8 + (hq % 2) * HQ
                mm(ps, qT[:, ci, u * P:(u + 1) * P], KBD[:, n:n + HQ, :].rearrange("p h k -> p (h k)"), True, False)
                if near:
                    for m in range(3):
                        mm(ps, flipb[:, :], BN[:, 3 * u + m, cols], False, False)
                ins = mm(ps, onesb[0:1 if near else 4, :], CM[0:1 if near else 4, b, cols], False, True)
                ins.then_inc(s.s_ps, 1)

            def weightsT(t, k):
                u, hq = k // NQ, k % NQ
                pe.wait_ge(s.e_exp, NQ * t + k + 1)
                for h in range(HQ):
                    ins = pe.transpose(pb[6 + k % 2][0:KEYS, h * P:(h + 1) * P],
                                       e_[:, u, hq * HQK + h * KEYS:hq * HQK + (h + 1) * KEYS], ident[:, :])
                ins.then_inc(s.pT_ps, 1)

            def heads(b, t, k):
                u, hq = k // NQ, k % NQ
                pe.wait_ge(s.pT_sb, NQ * t + k + 1)
                for g in range(HQ):
                    h = hq * HQ + g
                    ins = mm(pb[u][g * VE:(g + 1) * VE, hq * P:(hq + 1) * P], V1[:, b * H + h, :],
                             pT[:, u, h * P:(h + 1) * P], True, True)
                if hq == NQ - 1:
                    ins.then_inc(s.oT_ps, 1)

            def tokens_back(t, u):
                pe.wait_ge(s.oT_sb, t + u + 1)
                for hq in range(NQ):
                    ins = pe.transpose(pb[u][:, hq * P:(hq + 1) * P], oT[:, u, hq * P:(hq + 1) * P], ident[:, :])
                ins.then_inc(s.o_ps, 1)

            def project_in(t, u):
                pe.wait_ge(s.att_sb, t + u + 1)
                transposed(pb[5], att[:, u, :], s.attT_ps)

            def project(t, u):
                pe.wait_ge(s.attT_sb, t + u + 1)
                for ci in range(CH):
                    ins = mm(pb[5][:, 0:D], attT[:, u, ci * P:(ci + 1) * P], WO1[:, ci, :], ci == 0, ci == CH - 1)
                ins.then_inc(s.wo_ps, 1)

            def end_of_pair(b, t, k):
                if k < 3:
                    heads(b, t, k + 5)
                if k == 3:
                    tokens_back(t, 1)
                if k in (1, 5):
                    project_in(t, k // 4)
                if k in (2, 6):
                    project(t, k // 4)

            def pair(b, t, near, before, last=False):
                pe.wait_ge(s.q_sb, t + 2)
                for k in range(2 * NQ):
                    if k >= 2:
                        weightsT(t, k - 2)
                    elif before is not None:
                        weightsT(t - 2, k + 6)
                    scores(b, k, near)
                    if k == 7 and not last:
                        queries(t + 2)
                    if k >= 3:
                        heads(b, t, k - 3)
                    if before is not None:
                        end_of_pair(before, t - 2, k)
                    if k == 7:
                        tokens_back(t, 0)

            pe.wait_ge(s.kbd_sb, 1)
            pe.wait_ge(s.wo_sb, 1)
            pe.wait_ge(s.ld_const, 16 * 7)
            pe.wait_ge(s.y3T_sb, NT)
            for b in range(NB):
                pair(b, b * TB, False, b - 1 if b else None)
                with pe.Fori(1, FAR) as i:
                    pair(b, b * TB + 2 * i, False, b)
                pe.wait_ge(s.near_sb, NEAR)
                pair(b, b * TB + 2 * FAR, True, b, b == NB - 1)
            for k in range(7):
                if k < 2:
                    weightsT(NT - 2, k + 6)
                end_of_pair(NB - 1, NT - 2, k)
            def y4_in(g):
                for p in range(4 * g, 4 * g + 4):
                    if p >= 4:
                        pe.wait_ge(s.y4T_sb, p - 3)
                    pe.wait_ge(s.y_d, p + 1)
                    transposed(pb[p % 4], y4[:, p % 4, :], s.y4T_ps)

            def logits(g):
                if g == 1:
                    pe.wait_ge(s.x3_done, NT)
                if g >= 2:
                    pe.wait_ge(s.lT_sb, g - 1)
                for ci in range(CH):
                    for u in range(4):
                        pe.wait_ge(s.y4T_sb, 4 * g + u + 1)
                        ins = mm(pb[4 + g % 2][32 * u:32 * (u + 1), 0:P], GM[:, ci, :],
                                 y4T[:, (4 * g + u) % 8, ci * P:(ci + 1) * P], ci == 0, ci == CH - 1)
                ins.then_inc(s.lT_ps, 1)

            def logits_back(g):
                pe.wait_ge(s.lT_sb, g + 1)
                pe.transpose(pb[6][:, g * P:(g + 1) * P], lT[:, g % 2, :], ident[:, :]).then_inc(s.lg_ps, 1)
            y4_in(0)
            for g in range(NT // 4):
                if g < NT // 4 - 1:
                    y4_in(g + 1)
                logits(g)
                if g:
                    logits_back(g - 1)
            logits_back(NT // 4 - 1)
            pe.wait_ge(s.oh_sb, 1)
            oh = OHB[:, :, :].rearrange("p t e -> p (t e)")
            mm(pb[1][:, 0:NT * E], onesb[:, :], oh, True, True)
            mm(pb[0][:, 0:NT * E], before[:, :], oh, True, False)
            for t in range(NT - 1):
                n = NT - 1 - t
                ins = mm(pb[0][:, (t + 1) * E:NT * E].rearrange("p (t e) -> p t e", e=E), onesb[:, :],
                         OHB[:, t:t + 1, :].to_broadcast([P, n, E]), False, t == NT - 2)
            ins.then_inc(s.cnt_ps, 1)
            pe.wait_ge(s.pos_sb, 1)
            pe.wait_ge(s.slots_sb, 1)
            pe.wait_ge(s.ld_w1, 16)
            pe.wait_ge(s.ld_w2, 16)

            W1f = W1.rearrange("p n h -> p (n h)")
            W2f = W2.rearrange("p n h -> p (n h)")

            def inputs(u, i):
                pe.wait_ge(s.ys_sb, 2 * i + u + 1)
                transposed(pb[u], ys[:, u, :], s.ysT_ps)

            def layer1(u, i):
                e = pe.value_load(EXPS[0:1, ds(2 * i + u, 1)], min_val=0, max_val=E - 1)
                pe.wait_ge(s.ysT_sb, 2 * i + u + 1)
                for ci in range(CH):
                    ins = mm(pb[2 + u], ysT[:, u, ci * P:(ci + 1) * P], W1f[:, ds(e * (CH * HID) + ci * HID, HID)],
                             ci == 0, ci == CH - 1)
                ins.then_inc(s.h_ps, 1)

            def hiddenT(u, i):
                pe.wait_ge(s.gelu_sb, 2 * i + u + 1)
                for j in range(HJ):
                    ins = pe.transpose(pb[4 + u][:, j * P:(j + 1) * P], hb[:, u, j * P:(j + 1) * P], ident[:, :])
                ins.then_inc(s.hT_ps, 1)

            def layer2(u, i):
                e = pe.value_load(EXPS[0:1, ds(2 * i + u, 1)], min_val=0, max_val=E - 1)
                pe.wait_ge(s.res_sb, 2 * i + u + 1)
                pe.wait_ge(s.hT_sb, 2 * i + u + 1)
                for j in range(HJ):
                    ins = mm(pb[6 + u][:, 0:D], hT[:, u, j * P:(j + 1) * P], W2f[:, ds(e * (HJ * D) + j * D, D)],
                             j == 0, j == HJ - 1)
                ins.then_inc(s.eo_ps, 1)

            def step(i, now, nxt, prev):
                for u in now:
                    layer1(u, i)
                for u in nxt:
                    inputs(u, i + 1)
                for u in prev:
                    layer2(u, i - 1)
                for u in now:
                    hiddenT(u, i)
            for u in range(2):
                inputs(u, 0)
            step(0, (0, 1), (0, 1), ())
            with pe.Fori(1, NP - 1) as i:
                step(i, (0, 1), (0, 1), (0, 1))
            step(NP - 1, (0, 1), (0,), (0, 1))
            step(NP, (0,), (), (0, 1))
            step(NP + 1, (), (), (0,))


_INS = ["x", "ctx_1024", "mask_BxS2_bf0", "g_xattn", "g_ffn",
        "L0_xattn_Wq", "L0_xattn_bq", "L0_xattn_Wk", "L0_xattn_bk", "L0_xattn_Wv", "L0_xattn_bv",
        "L0_ffn_w_gate", "L0_ffn_w_up", "L0_ffn_w_down",
        "L1_xattn_Wq", "L1_xattn_bq", "L1_xattn_Wk", "L1_xattn_bk", "L1_xattn_Wv", "L1_xattn_bv",
        "L1_xattn_Wo", "L1_xattn_bo", "L1_xattn_logit_scale", "L1_xattn_bias_table",
        "L1_ffn_w_red", "L1_ffn_wg", "L1_ffn_W1", "L1_ffn_b1", "L1_ffn_W2", "L1_ffn_b2"]


def kernel(**inputs):
    import concourse.bacc as bacc
    from concourse.bass_utils import run_bass_kernel_spmd

    nc = bacc.Bacc("TRN2", target_bir_lowering=False, num_devices=1)
    arrays, args = {}, {}
    for name in _INS:
        v = np.ascontiguousarray(inputs[name])
        arrays[f"in_{name}"] = v
        args[name] = nc.dram_tensor(f"in_{name}", v.shape, mybir.dt.from_np(v.dtype), kind="ExternalInput").ap()
    out = nc.dram_tensor("out_0", (NB, S, D), F32, kind="ExternalOutput").ap()
    flamingo_kernel(nc, args, out)
    r = run_bass_kernel_spmd(nc, [arrays], core_ids=[0])
    return r.results[0]["out_0"]
```
